# Optimizing a Trainium2 kernel written in Bass

```python
import numpy as np
import jax
import jax.numpy as jnp

def _softmax(x, axis=-1):
    return jax.nn.softmax(x, axis=axis)

def _gelu(x):
    return jax.nn.gelu(x, approximate=True)

def _silu(x):
    return jax.nn.silu(x)

def _sigmoid(x):
    return jax.nn.sigmoid(x)

def _layernorm(x, axis=-1, eps=1e-05):
    m = jnp.mean(x, axis=axis, keepdims=True)
    v = jnp.var(x, axis=axis, keepdims=True)
    return (x - m) / jnp.sqrt(v + eps)

def _scatter_add(tgt, idx, src, axis=0):
    return tgt.at[idx].add(src)

def _segment_sum(src, seg, n):
    return jax.ops.segment_sum(src, seg, n)
kernel_name = 'mk_perceiver_d2_seqx_r4_2f24f8'

def setup_inputs(seed: int=0):
    np.random.seed(seed)
    _w = jnp.asarray

    def _rec_inputs():
        import jax
        import jax.numpy as jnp
        _rk = jax.random.key(seed)
        x = 7.22e-05 + 1 * jax.random.normal(jax.random.fold_in(_rk, 1), (8, 64, 256), jnp.float32)
        _lenS = 64 - jax.random.randint(jax.random.fold_in(_rk, 7), (8,), 0, max(1, 64 // 4) + 1, jnp.int32)
        _lenS2 = 1601 - jax.random.randint(jax.random.fold_in(_rk, 8), (8,), 0, max(1, 1601 // 4) + 1, jnp.int32)
        _ctx_1024P = jax.random.normal(jax.random.fold_in(_rk, 11), (8, 16, 256), jnp.float32)
        _ctx_1024c = jax.random.dirichlet(jax.random.fold_in(_rk, 511), 0.3 * jnp.ones((16,), jnp.float32), (8, 1601))
        _ctx_1024t = jnp.einsum('bsk,bkd->bsd', _ctx_1024c, _ctx_1024P)
        _ctx_1024t = _ctx_1024t * jax.lax.rsqrt(jnp.mean(jnp.square(_ctx_1024t)) + 1e-12) * 0.953939
        ctx_1024 = 4.13588e-05 + 0.999923 * (_ctx_1024t + 0.3 * jax.random.normal(jax.random.fold_in(_rk, 611), (8, 1601, 256), jnp.float32))
        _validS = jnp.arange(64)[None, :] < _lenS[:, None]
        _validS2 = jnp.arange(1601)[None, :] < _lenS2[:, None]
        _causal = jnp.tril(jnp.ones((64, 64), dtype=bool))
        mask_Bx1x1xS2_ff0 = jnp.where(jnp.ones((8, 1, 1, 1601), dtype=bool), 0.0, -1000000000.0).astype(jnp.float32)
        return (x, ctx_1024, mask_Bx1x1xS2_ff0)
    x, ctx_1024, mask_Bx1x1xS2_ff0 = _rec_inputs()

    def _L0_xattn_setup():
        import jax, jax.numpy as jnp
        import numpy as np
        B, S, D, H = (4, 512, 256, 16)
        DEPTH = D // H

        def _split_heads(x):
            b, s, _ = x.shape
            return x.reshape(b, s, H, DEPTH).transpose(0, 2, 1, 3)
        key = jax.random.key(seed)
        ks = jax.random.split(key, 12)
        s = 1.0 / np.sqrt(D)
        return {'q': jax.random.normal(ks[0], (B, S, D), jnp.float32), 'k': jax.random.normal(ks[1], (B, S, D), jnp.float32), 'v': jax.random.normal(ks[2], (B, S, D), jnp.float32), 'mask': jnp.zeros((B, 1, 1, S), jnp.float32), 'wq': jax.random.normal(ks[3], (D, D), jnp.float32) * s, 'bq': jnp.zeros((D,), jnp.float32), 'wk': jax.random.normal(ks[4], (D, D), jnp.float32) * s, 'bk': jnp.zeros((D,), jnp.float32), 'wv': jax.random.normal(ks[5], (D, D), jnp.float32) * s, 'bv': jnp.zeros((D,), jnp.float32), 'wo': jax.random.normal(ks[6], (D, D), jnp.float32) * s, 'bo': jnp.zeros((D,), jnp.float32)}
    _L0_xattn_all = _L0_xattn_setup()
    _L0_xattn_in = {k: v for k, v in _L0_xattn_all.items() if k in ('wq', 'bq', 'wk', 'bk', 'wv', 'bv', 'wo', 'bo')}
    del _L0_xattn_all

    def _L0_attn_setup():
        import jax, jax.numpy as jnp
        import numpy as np
        EMB = 256
        HEADS = 16
        EPS = 1e-05

        def layer_norm(x):
            mu = jnp.mean(x, axis=-1, keepdims=True)
            var = jnp.var(x, axis=-1, keepdims=True)
            return (x - mu) / jnp.sqrt(var + EPS)

        def pattention(x, K, V):
            scale = EMB ** (-0.5)
            a = jax.nn.softmax(scale * jnp.einsum('btc,nc->btn', x, K), axis=-1)
            return jnp.einsum('btn,nc->btc', a, V)

        def causal_sdpa(q, k, v):
            T = q.shape[2]
            d = q.shape[-1]
            scores = jnp.einsum('bhqd,bhkd->bhqk', q, k) / jnp.sqrt(jnp.asarray(d, q.dtype))
            mask = jnp.tril(jnp.ones((T, T), dtype=bool))
            scores = jnp.where(mask, scores, jnp.asarray(-jnp.inf, q.dtype))
            attn = jax.nn.softmax(scores, axis=-1)
            return jnp.einsum('bhqk,bhkd->bhqd', attn, v)
        key = jax.random.key(seed)
        ks = jax.random.split(key, 11)
        B, T, C = (2, 512, EMB)
        N = 512 // 2
        inp = {'x': jax.random.normal(ks[0], (B, T, C), dtype=jnp.float32)}
        names = ['qK', 'qV', 'kK', 'kV', 'vK', 'vV', 'pK', 'pV']
        for i, nm in enumerate(names):
            inp[nm] = jax.random.normal(ks[1 + i], (N, C), dtype=jnp.float32)
        inp['fK'] = jax.random.normal(ks[9], (4 * N, C), dtype=jnp.float32)
        inp['fV'] = jax.random.normal(ks[10], (4 * N, C), dtype=jnp.float32)
        return inp
    _L0_attn_all = _L0_attn_setup()
    _L0_attn_in = {k: v for k, v in _L0_attn_all.items() if k in ('qK', 'qV', 'kK', 'kV', 'vK', 'vV', 'pK', 'pV', 'fK', 'fV')}
    del _L0_attn_all

    def _L0_ffn_setup():
        import jax, jax.numpy as jnp
        import numpy as np
        S_LEN, BATCH, HIDDEN = (512, 2, 256)
        N_HEADS, N_KV = (16, 8)
        N_EXP, TOP_K, CAP_F = (8, 2, 1.25)
        FFN = 1024
        HEAD_DIM = HIDDEN // N_HEADS
        Q_PER_KV = N_HEADS // N_KV
        EPS = 1e-05
        NEG = -1000000000.0

        def _ln(x, w, b):
            mu = jnp.mean(x, -1, keepdims=True)
            var = jnp.var(x, -1, keepdims=True)
            return (x - mu) * jax.lax.rsqrt(var + EPS) * w + b

        def _forward(hidden_states, ln1_weight, ln1_bias, ln2_weight, ln2_bias, qkv_weight, proj_weight, router_weight, moe_w1, moe_w2):
            S, B, H = hidden_states.shape
            ln1 = _ln(hidden_states, ln1_weight, ln1_bias)
            qkv = (ln1 @ qkv_weight.T).reshape(S, B, N_KV, (Q_PER_KV + 2) * HEAD_DIM)
            q_dim = Q_PER_KV * HEAD_DIM
            q = qkv[..., :q_dim].reshape(S, B, N_HEADS, HEAD_DIM)
            k = jnp.repeat(qkv[..., q_dim:q_dim + HEAD_DIM], Q_PER_KV, axis=2)
            v = jnp.repeat(qkv[..., q_dim + HEAD_DIM:], Q_PER_KV, axis=2)
            scores = jnp.einsum('sbhd,tbhd->bhst', q, k) / jnp.sqrt(jnp.float32(HEAD_DIM))
            causal = jnp.tril(jnp.ones((S, S), bool))
            attn = jax.nn.softmax(jnp.where(causal[None, None], scores, NEG), axis=-1)
            attn_out = jnp.einsum('bhst,tbhd->sbhd', attn, v).reshape(S, B, H)
            hidden_after_attn = hidden_states + attn_out @ proj_weight.T
            x = _ln(hidden_after_attn, ln2_weight, ln2_bias).reshape(-1, H)
            N = S * B
            probs = jax.nn.softmax(x.astype(jnp.float32) @ router_weight, axis=-1)
            top_p, top_i = jax.lax.top_k(probs, TOP_K)
            top_p = top_p / jnp.sum(top_p, -1, keepdims=True)
            flat_exp = top_i.reshape(-1)
            order = jnp.argsort(flat_exp)
            sorted_exp = flat_exp[order]
            counts = jnp.bincount(sorted_exp, length=N_EXP)
            offsets = jnp.concatenate([jnp.zeros((1,), counts.dtype), jnp.cumsum(counts)])
            within = jnp.arange(N * TOP_K) - offsets[sorted_exp]
            cap = int(np.ceil(N * TOP_K / N_EXP * CAP_F))
            keep = within < cap
            slot = jnp.where(keep, sorted_exp * cap + within, N_EXP * cap)
            tok_id = order // TOP_K
            padded_tokens = jnp.zeros((N_EXP * cap + 1, H), x.dtype).at[slot].set(x[tok_id])[:-1]
            padded_probs = jnp.zeros((N_EXP * cap + 1,), jnp.float32).at[slot].set(top_p.reshape(-1)[order])[:-1]
            padded_ids = jnp.zeros((N_EXP * cap + 1,), jnp.int32).at[slot].set(tok_id.astype(jnp.int32))[:-1]
            exp_in = padded_tokens.reshape(N_EXP, cap, H)
            act = jax.nn.gelu(jnp.einsum('ech,ehf->ecf', exp_in, moe_w1), approximate=False)
            exp_out = jnp.einsum('ecf,efh->ech', act, moe_w2).reshape(N_EXP * cap, H)
            weighted = exp_out * padded_probs[:, None].astype(exp_out.dtype)
            moe = jnp.zeros((N, H), exp_out.dtype).at[padded_ids].add(weighted)
            return hidden_after_attn + moe.reshape(S, B, H)
        ks = jax.random.split(jax.random.key(seed), 6)
        qkv_out = N_KV * (Q_PER_KV + 2) * HEAD_DIM
        sc = 0.02
        return {'hidden_states': jax.random.normal(ks[0], (S_LEN, BATCH, HIDDEN), jnp.float32), 'ln1_weight': jnp.ones((HIDDEN,), jnp.float32), 'ln1_bias': jnp.zeros((HIDDEN,), jnp.float32), 'ln2_weight': jnp.ones((HIDDEN,), jnp.float32), 'ln2_bias': jnp.zeros((HIDDEN,), jnp.float32), 'qkv_weight': jax.random.normal(ks[1], (qkv_out, HIDDEN), jnp.float32) * sc, 'proj_weight': jax.random.normal(ks[2], (HIDDEN, HIDDEN), jnp.float32) * sc, 'router_weight': jax.random.normal(ks[3], (HIDDEN, N_EXP), jnp.float32) * sc, 'moe_w1': jax.random.normal(ks[4], (N_EXP, HIDDEN, FFN), jnp.float32) * sc, 'moe_w2': jax.random.normal(ks[5], (N_EXP, FFN, HIDDEN), jnp.float32) * sc}
    _L0_ffn_all = _L0_ffn_setup()
    _L0_ffn_in = {k: v for k, v in _L0_ffn_all.items() if k in ('ln1_weight', 'ln1_bias', 'ln2_weight', 'ln2_bias', 'qkv_weight', 'proj_weight', 'router_weight', 'moe_w1', 'moe_w2')}
    del _L0_ffn_all

    def _L1_xattn_setup():
        import jax, jax.numpy as jnp
        import numpy as np
        D_MODEL = 256
        NUM_HEADS = 16
        HEAD_DIM = D_MODEL // NUM_HEADS

        def _split_heads(x):
            B, S, _ = x.shape
            return x.reshape(B, S, NUM_HEADS, HEAD_DIM).transpose(0, 2, 1, 3)
        key = jax.random.key(seed)
        ks = jax.random.split(key, 8)
        B, S = (2, 512)
        scale = 1.0 / np.sqrt(D_MODEL)
        return {'query': jax.random.normal(ks[0], (B, S, D_MODEL), jnp.float32), 'key': jax.random.normal(ks[1], (B, S, D_MODEL), jnp.float32), 'value': jax.random.normal(ks[2], (B, S, D_MODEL), jnp.float32), 'Wq': jax.random.normal(ks[3], (D_MODEL, D_MODEL), jnp.float32) * scale, 'Wk': jax.random.normal(ks[4], (D_MODEL, D_MODEL), jnp.float32) * scale, 'Wv': jax.random.normal(ks[5], (D_MODEL, D_MODEL), jnp.float32) * scale, 'Wo': jax.random.normal(ks[6], (D_MODEL, D_MODEL), jnp.float32) * scale, 'bo': jnp.zeros((D_MODEL,), jnp.float32)}
    _L1_xattn_all = _L1_xattn_setup()
    _L1_xattn_in = {k: v for k, v in _L1_xattn_all.items() if k in ('Wq', 'Wk', 'Wv', 'Wo', 'bo')}
    del _L1_xattn_all

    def _L1_attn_setup():
        import jax, jax.numpy as jnp
        import numpy as np
        HIDDEN, KEY_DIM, VALUE_DIM = (256, 256, 256)
        BATCH, SEQ = (8, 512)
        key = jax.random.key(seed)
        ks = jax.random.split(key, 9)
        s = lambda fan_in: 1.0 / np.sqrt(fan_in)
        return {'y_all': jax.random.normal(ks[0], (BATCH, SEQ, HIDDEN), dtype=jnp.float32), 'Wq': jax.random.uniform(ks[1], (HIDDEN, KEY_DIM), jnp.float32, -s(HIDDEN), s(HIDDEN)), 'bq': jax.random.uniform(ks[2], (KEY_DIM,), jnp.float32, -s(HIDDEN), s(HIDDEN)), 'Wk': jax.random.uniform(ks[3], (HIDDEN, KEY_DIM), jnp.float32, -s(HIDDEN), s(HIDDEN)), 'bk': jax.random.uniform(ks[4], (KEY_DIM,), jnp.float32, -s(HIDDEN), s(HIDDEN)), 'Wv': jax.random.uniform(ks[5], (HIDDEN, VALUE_DIM), jnp.float32, -s(HIDDEN), s(HIDDEN)), 'bv': jax.random.uniform(ks[6], (VALUE_DIM,), jnp.float32, -s(HIDDEN), s(HIDDEN)), 'Wo': jax.random.uniform(ks[7], (VALUE_DIM, HIDDEN), jnp.float32, -s(VALUE_DIM), s(VALUE_DIM)), 'bo': jax.random.uniform(ks[8], (HIDDEN,), jnp.float32, -s(VALUE_DIM), s(VALUE_DIM))}
    _L1_attn_all = _L1_attn_setup()
    _L1_attn_in = {k: v for k, v in _L1_attn_all.items() if k in ('Wq', 'bq', 'Wk', 'bk', 'Wv', 'bv', 'Wo', 'bo')}
    del _L1_attn_all

    def _L1_ffn_setup():
        import jax, jax.numpy as jnp
        import numpy as np
        TOP_K = 2
        key = jax.random.key(seed)
        ks = jax.random.split(key, 6)
        B, L, D, E, F = (2, 512, 256, 8, 1024)
        x = jax.random.normal(ks[0], (B, L, D), dtype=jnp.float32)
        Wg = jax.random.normal(ks[1], (D, E), dtype=jnp.float32) * D ** (-0.5)
        W1 = jax.random.normal(ks[2], (E, D, F), dtype=jnp.float32) * D ** (-0.5)
        b1 = jnp.zeros((E, F), dtype=jnp.float32)
        W2 = jax.random.normal(ks[3], (E, F, D), dtype=jnp.float32) * F ** (-0.5)
        b2 = jnp.zeros((E, D), dtype=jnp.float32)
        return {'x': x, 'Wg': Wg, 'W1': W1, 'b1': b1, 'W2': W2, 'b2': b2}
    _L1_ffn_all = _L1_ffn_setup()
    _L1_ffn_in = {k: v for k, v in _L1_ffn_all.items() if k in ('Wg', 'W1', 'b1', 'W2', 'b2')}
    del _L1_ffn_all
    return {'x': x, 'ctx_1024': ctx_1024, 'mask_Bx1x1xS2_ff0': mask_Bx1x1xS2_ff0, 'L0_xattn_wq': _L0_xattn_in['wq'], 'L0_xattn_bq': _L0_xattn_in['bq'], 'L0_xattn_wk': _L0_xattn_in['wk'], 'L0_xattn_bk': _L0_xattn_in['bk'], 'L0_xattn_wv': _L0_xattn_in['wv'], 'L0_xattn_bv': _L0_xattn_in['bv'], 'L0_xattn_wo': _L0_xattn_in['wo'], 'L0_xattn_bo': _L0_xattn_in['bo'], 'L0_attn_qK': _L0_attn_in['qK'], 'L0_attn_qV': _L0_attn_in['qV'], 'L0_attn_kK': _L0_attn_in['kK'], 'L0_attn_kV': _L0_attn_in['kV'], 'L0_attn_vK': _L0_attn_in['vK'], 'L0_attn_vV': _L0_attn_in['vV'], 'L0_attn_pK': _L0_attn_in['pK'], 'L0_attn_pV': _L0_attn_in['pV'], 'L0_attn_fK': _L0_attn_in['fK'], 'L0_attn_fV': _L0_attn_in['fV'], 'L0_ffn_ln1_weight': _L0_ffn_in['ln1_weight'], 'L0_ffn_ln1_bias': _L0_ffn_in['ln1_bias'], 'L0_ffn_ln2_weight': _L0_ffn_in['ln2_weight'], 'L0_ffn_ln2_bias': _L0_ffn_in['ln2_bias'], 'L0_ffn_qkv_weight': _L0_ffn_in['qkv_weight'], 'L0_ffn_proj_weight': _L0_ffn_in['proj_weight'], 'L0_ffn_router_weight': _L0_ffn_in['router_weight'], 'L0_ffn_moe_w1': _L0_ffn_in['moe_w1'], 'L0_ffn_moe_w2': _L0_ffn_in['moe_w2'], 'L1_xattn_Wq': _L1_xattn_in['Wq'], 'L1_xattn_Wk': _L1_xattn_in['Wk'], 'L1_xattn_Wv': _L1_xattn_in['Wv'], 'L1_xattn_Wo': _L1_xattn_in['Wo'], 'L1_xattn_bo': _L1_xattn_in['bo'], 'L1_attn_Wq': _L1_attn_in['Wq'], 'L1_attn_bq': _L1_attn_in['bq'], 'L1_attn_Wk': _L1_attn_in['Wk'], 'L1_attn_bk': _L1_attn_in['bk'], 'L1_attn_Wv': _L1_attn_in['Wv'], 'L1_attn_bv': _L1_attn_in['bv'], 'L1_attn_Wo': _L1_attn_in['Wo'], 'L1_attn_bo': _L1_attn_in['bo'], 'L1_ffn_Wg': _L1_ffn_in['Wg'], 'L1_ffn_W1': _L1_ffn_in['W1'], 'L1_ffn_b1': _L1_ffn_in['b1'], 'L1_ffn_W2': _L1_ffn_in['W2'], 'L1_ffn_b2': _L1_ffn_in['b2']}

def reference(x, ctx_1024, mask_Bx1x1xS2_ff0, L0_xattn_wq, L0_xattn_bq, L0_xattn_wk, L0_xattn_bk, L0_xattn_wv, L0_xattn_bv, L0_xattn_wo, L0_xattn_bo, L0_attn_qK, L0_attn_qV, L0_attn_kK, L0_attn_kV, L0_attn_vK, L0_attn_vV, L0_attn_pK, L0_attn_pV, L0_attn_fK, L0_attn_fV, L0_ffn_ln1_weight, L0_ffn_ln1_bias, L0_ffn_ln2_weight, L0_ffn_ln2_bias, L0_ffn_qkv_weight, L0_ffn_proj_weight, L0_ffn_router_weight, L0_ffn_moe_w1, L0_ffn_moe_w2, L1_xattn_Wq, L1_xattn_Wk, L1_xattn_Wv, L1_xattn_Wo, L1_xattn_bo, L1_attn_Wq, L1_attn_bq, L1_attn_Wk, L1_attn_bk, L1_attn_Wv, L1_attn_bv, L1_attn_Wo, L1_attn_bo, L1_ffn_Wg, L1_ffn_W1, L1_ffn_b1, L1_ffn_W2, L1_ffn_b2):
    import jax
    import jax.numpy as jnp

    def _L0_xattn_ref(q, k, v, mask, wq, bq, wk, bk, wv, bv, wo, bo):
        import jax, jax.numpy as jnp
        import numpy as np
        B, S, D, H = (4, 512, 256, 16)
        DEPTH = D // H

        def _split_heads(x):
            b, s, _ = x.shape
            return x.reshape(b, s, H, DEPTH).transpose(0, 2, 1, 3)
        qh = _split_heads(q @ wq + bq)
        kh = _split_heads(k @ wk + bk)
        vh = _split_heads(v @ wv + bv)
        scale = 1.0 / jnp.sqrt(jnp.asarray(DEPTH, jnp.float32))
        logits = jnp.einsum('bhqd,bhkd->bhqk', qh, kh) * scale
        logits = logits + mask * -1000000000.0
        attn = jax.nn.softmax(logits, axis=-1)
        out = jnp.einsum('bhqk,bhkd->bhqd', attn, vh)
        out = out.transpose(0, 2, 1, 3).reshape(q.shape[0], -1, D)
        return out @ wo + bo

    def _L0_attn_ref(x, qK, qV, kK, kV, vK, vV, pK, pV, fK, fV):
        import jax, jax.numpy as jnp
        import numpy as np
        EMB = 256
        HEADS = 16
        EPS = 1e-05

        def layer_norm(x):
            mu = jnp.mean(x, axis=-1, keepdims=True)
            var = jnp.var(x, axis=-1, keepdims=True)
            return (x - mu) / jnp.sqrt(var + EPS)

        def pattention(x, K, V):
            scale = EMB ** (-0.5)
            a = jax.nn.softmax(scale * jnp.einsum('btc,nc->btn', x, K), axis=-1)
            return jnp.einsum('btn,nc->btc', a, V)

        def causal_sdpa(q, k, v):
            T = q.shape[2]
            d = q.shape[-1]
            scores = jnp.einsum('bhqd,bhkd->bhqk', q, k) / jnp.sqrt(jnp.asarray(d, q.dtype))
            mask = jnp.tril(jnp.ones((T, T), dtype=bool))
            scores = jnp.where(mask, scores, jnp.asarray(-jnp.inf, q.dtype))
            attn = jax.nn.softmax(scores, axis=-1)
            return jnp.einsum('bhqk,bhkd->bhqd', attn, v)
        B, T, C = x.shape
        H = HEADS
        D = C // H
        x_in = x
        h = layer_norm(x)
        k = pattention(h, kK, kV)
        q = pattention(h, qK, qV)
        v = pattention(h, vK, vV)
        to_heads = lambda t: t.reshape(B, T, H, D).transpose(0, 2, 1, 3)
        o = causal_sdpa(to_heads(q), to_heads(k), to_heads(v))
        o = o.transpose(0, 2, 1, 3).reshape(B, T, C)
        o = pattention(o, pK, pV)
        x = o + x_in
        x_inter = x
        x = pattention(layer_norm(x), fK, fV)
        return x + x_inter

    def _L0_ffn_ref(hidden_states, ln1_weight, ln1_bias, ln2_weight, ln2_bias, qkv_weight, proj_weight, router_weight, moe_w1, moe_w2):
        import jax, jax.numpy as jnp
        import numpy as np
        S_LEN, BATCH, HIDDEN = (512, 2, 256)
        N_HEADS, N_KV = (16, 8)
        N_EXP, TOP_K, CAP_F = (8, 2, 1.25)
        FFN = 1024
        HEAD_DIM = HIDDEN // N_HEADS
        Q_PER_KV = N_HEADS // N_KV
        EPS = 1e-05
        NEG = -1000000000.0

        def _ln(x, w, b):
            mu = jnp.mean(x, -1, keepdims=True)
            var = jnp.var(x, -1, keepdims=True)
            return (x - mu) * jax.lax.rsqrt(var + EPS) * w + b

        def _forward(hidden_states, ln1_weight, ln1_bias, ln2_weight, ln2_bias, qkv_weight, proj_weight, router_weight, moe_w1, moe_w2):
            S, B, H = hidden_states.shape
            ln1 = _ln(hidden_states, ln1_weight, ln1_bias)
            qkv = (ln1 @ qkv_weight.T).reshape(S, B, N_KV, (Q_PER_KV + 2) * HEAD_DIM)
            q_dim = Q_PER_KV * HEAD_DIM
            q = qkv[..., :q_dim].reshape(S, B, N_HEADS, HEAD_DIM)
            k = jnp.repeat(qkv[..., q_dim:q_dim + HEAD_DIM], Q_PER_KV, axis=2)
            v = jnp.repeat(qkv[..., q_dim + HEAD_DIM:], Q_PER_KV, axis=2)
            scores = jnp.einsum('sbhd,tbhd->bhst', q, k) / jnp.sqrt(jnp.float32(HEAD_DIM))
            causal = jnp.tril(jnp.ones((S, S), bool))
            attn = jax.nn.softmax(jnp.where(causal[None, None], scores, NEG), axis=-1)
            attn_out = jnp.einsum('bhst,tbhd->sbhd', attn, v).reshape(S, B, H)
            hidden_after_attn = hidden_states + attn_out @ proj_weight.T
            x = _ln(hidden_after_attn, ln2_weight, ln2_bias).reshape(-1, H)
            N = S * B
            probs = jax.nn.softmax(x.astype(jnp.float32) @ router_weight, axis=-1)
            top_p, top_i = jax.lax.top_k(probs, TOP_K)
            top_p = top_p / jnp.sum(top_p, -1, keepdims=True)
            flat_exp = top_i.reshape(-1)
            order = jnp.argsort(flat_exp)
            sorted_exp = flat_exp[order]
            counts = jnp.bincount(sorted_exp, length=N_EXP)
            offsets = jnp.concatenate([jnp.zeros((1,), counts.dtype), jnp.cumsum(counts)])
            within = jnp.arange(N * TOP_K) - offsets[sorted_exp]
            cap = int(np.ceil(N * TOP_K / N_EXP * CAP_F))
            keep = within < cap
            slot = jnp.where(keep, sorted_exp * cap + within, N_EXP * cap)
            tok_id = order // TOP_K
            padded_tokens = jnp.zeros((N_EXP * cap + 1, H), x.dtype).at[slot].set(x[tok_id])[:-1]
            padded_probs = jnp.zeros((N_EXP * cap + 1,), jnp.float32).at[slot].set(top_p.reshape(-1)[order])[:-1]
            padded_ids = jnp.zeros((N_EXP * cap + 1,), jnp.int32).at[slot].set(tok_id.astype(jnp.int32))[:-1]
            exp_in = padded_tokens.reshape(N_EXP, cap, H)
            act = jax.nn.gelu(jnp.einsum('ech,ehf->ecf', exp_in, moe_w1), approximate=False)
            exp_out = jnp.einsum('ecf,efh->ech', act, moe_w2).reshape(N_EXP * cap, H)
            weighted = exp_out * padded_probs[:, None].astype(exp_out.dtype)
            moe = jnp.zeros((N, H), exp_out.dtype).at[padded_ids].add(weighted)
            return hidden_after_attn + moe.reshape(S, B, H)
        return _forward(hidden_states, ln1_weight, ln1_bias, ln2_weight, ln2_bias, qkv_weight, proj_weight, router_weight, moe_w1, moe_w2)

    def _L1_xattn_ref(query, key, value, Wq, Wk, Wv, Wo, bo):
        import jax, jax.numpy as jnp
        import numpy as np
        D_MODEL = 256
        NUM_HEADS = 16
        HEAD_DIM = D_MODEL // NUM_HEADS

        def _split_heads(x):
            B, S, _ = x.shape
            return x.reshape(B, S, NUM_HEADS, HEAD_DIM).transpose(0, 2, 1, 3)
        B, S, _ = query.shape
        q = _split_heads(query @ Wq.T)
        k = _split_heads(key @ Wk.T)
        v = _split_heads(value @ Wv.T)
        scores = jnp.einsum('bhqd,bhkd->bhqk', q, k) / jnp.sqrt(jnp.float32(HEAD_DIM))
        attn = jax.nn.softmax(scores, axis=-1)
        out = jnp.einsum('bhqk,bhkd->bhqd', attn, v)
        out = out.transpose(0, 2, 1, 3).reshape(B, S, D_MODEL)
        return out @ Wo.T + bo

    def _L1_attn_ref(y_all, Wq, bq, Wk, bk, Wv, bv, Wo, bo):
        import jax, jax.numpy as jnp
        import numpy as np
        HIDDEN, KEY_DIM, VALUE_DIM = (256, 256, 256)
        BATCH, SEQ = (8, 512)
        B, T, H = y_all.shape
        dk = Wq.shape[1]
        q = (y_all @ Wq + bq) / jnp.sqrt(jnp.asarray(dk, y_all.dtype))
        k = y_all @ Wk + bk
        v = y_all @ Wv + bv
        scores = jnp.einsum('bid,bjd->bij', q, k)
        causal = jnp.tril(jnp.ones((T, T), dtype=bool))
        scores = jnp.where(causal, scores, -jnp.inf)
        weights = jax.nn.softmax(scores, axis=-1)
        ctx = jnp.einsum('bij,bjd->bid', weights, v)
        return ctx @ Wo + bo

    def _L1_ffn_ref(x, Wg, W1, b1, W2, b2):
        import jax, jax.numpy as jnp
        import numpy as np
        TOP_K = 2
        b, l, d = x.shape
        E = Wg.shape[1]
        xt = x.reshape(b * l, d)
        N = xt.shape[0]
        S = jax.nn.sigmoid(xt @ Wg)
        G, I = jax.lax.top_k(S, TOP_K)
        h = jax.nn.gelu(jnp.einsum('nd,edf->enf', xt, W1) + b1[:, None, :])
        y = jnp.einsum('enf,efd->end', h, W2) + b2[:, None, :]
        combine = jnp.zeros((N, E), dtype=x.dtype).at[jnp.arange(N)[:, None], I].add(G)
        out = jnp.einsum('ne,end->nd', combine, y)
        return out.reshape(b, l, d)
    x = x + _L0_xattn_ref(_layernorm(x, axis=-1), ctx_1024, ctx_1024, mask_Bx1x1xS2_ff0, L0_xattn_wq, L0_xattn_bq, L0_xattn_wk, L0_xattn_bk, L0_xattn_wv, L0_xattn_bv, L0_xattn_wo, L0_xattn_bo)
    x = x + _L0_attn_ref(_layernorm(x, axis=-1), L0_attn_qK, L0_attn_qV, L0_attn_kK, L0_attn_kV, L0_attn_vK, L0_attn_vV, L0_attn_pK, L0_attn_pV, L0_attn_fK, L0_attn_fV)
    x = x + _L0_ffn_ref(_layernorm(x, axis=-1), L0_ffn_ln1_weight, L0_ffn_ln1_bias, L0_ffn_ln2_weight, L0_ffn_ln2_bias, L0_ffn_qkv_weight, L0_ffn_proj_weight, L0_ffn_router_weight, L0_ffn_moe_w1, L0_ffn_moe_w2)
    x = x + _L1_xattn_ref(_layernorm(x, axis=-1), ctx_1024, ctx_1024, L1_xattn_Wq, L1_xattn_Wk, L1_xattn_Wv, L1_xattn_Wo, L1_xattn_bo)
    x = x + _L1_attn_ref(_layernorm(x, axis=-1), L1_attn_Wq, L1_attn_bq, L1_attn_Wk, L1_attn_bk, L1_attn_Wv, L1_attn_bv, L1_attn_Wo, L1_attn_bo)
    x = x + _L1_ffn_ref(_layernorm(x, axis=-1), L1_ffn_Wg, L1_ffn_W1, L1_ffn_b1, L1_ffn_W2, L1_ffn_b2)
    return x

_drawn_inputs = setup_inputs


def setup_inputs(seed=0):
    import zlib

    import numpy as np

    out = dict(_drawn_inputs(seed))
    spreads = {'L0_xattn_bq': (0.0, 0.1),
     'L0_xattn_bk': (0.0, 2.0),
     'L0_xattn_bv': (0.0, 0.1),
     'L0_xattn_bo': (0.0, 0.1),
     'L0_ffn_ln1_weight': (1.0, 0.6),
     'L0_ffn_ln1_bias': (0.0, 1.345),
     'L0_ffn_ln2_weight': (1.0, 0.584),
     'L0_ffn_ln2_bias': (0.0, 0.419),
     'L1_xattn_bo': (0.0, 0.1),
     'L1_ffn_b1': (0.0, 0.35),
     'L1_ffn_b2': (0.0, 0.1)}
    factors = {'L0_attn_qK': 8.0,
     'L0_attn_qV': 8.0,
     'L0_attn_kK': 8.0,
     'L0_attn_kV': 8.0,
     'L0_attn_vK': 6.788,
     'L0_attn_vV': 8.0,
     'L0_attn_pK': 6.138,
     'L1_attn_Wq': 4.446,
     'L1_attn_bq': 24.117,
     'L1_attn_Wk': 3.31,
     'L1_attn_bk': 64.0,
     'L1_attn_bv': 3.258,
     'L1_attn_bo': 2.672}
    for name, (base, spread) in spreads.items():
        noise = np.random.default_rng([zlib.crc32(name.encode()), seed]).standard_normal(out[name].shape)
        drawn = base * np.exp(spread * noise) if base else spread * noise
        out[name] = jnp.asarray(drawn.astype(out[name].dtype))
    for name, factor in factors.items():
        out[name] = (out[name] * factor).astype(out[name].dtype)
    return out
```

```python
from contextlib import ExitStack

import concourse.bass as bass
from concourse import mybir

F32 = mybir.dt.float32
ALU = mybir.AluOpType
ACT = mybir.ActivationFunctionType
AX = mybir.AxisListType

P = 128
B, T, D = 8, 64, 256
ROWS = B * T
RT = ROWS // P
DC = D // P
H, HD = 16, 16
PAIRS = H // 2
HPC = P // HD
S = 1601
KT_N = (S + P - 1) // P
S_LAST = S - (KT_N - 1) * P
HALF_A = 1024
BANK = 512
NE, FF = 8, 1024
FC = FF // P
CAP = 160
EPS = 1e-5
NEG = -1e30
K_UNITS = 8
V_UNITS = (KT_N + 1) // 2
UNITS = K_UNITS + V_UNITS
KEY_BLOCKS = [(0, 512), (512, 512), (1024, 512), (1536, S - 1536)]

COLS = {"bq0": 0, "bk0": 2, "bv0": 4, "bq5": 6, "bk5": 8, "bv5": 10, "b1": 12}
N_COLS = 12 + NE * FC
ROWV = ["bo0", "ln1w", "ln1b", "ln2w", "ln2b", "bo3", "bo5"]


def perceiver(nc, x, ctxT, mask, cols, rowv, xw0, patt_k, patt_v, fk, fv, wqkv, wproj, wrt, m0w1, m0w2,
              xw1, aw, wg, m1w1, m1w2, b2, out):
    ctx = ExitStack()
    with ctx:
        def sb(name, shape, dt=F32):
            return ctx.enter_context(nc.sbuf_tensor(name, shape, dt))

        named = {}

        def sem(name):
            if name not in named:
                named[name] = ctx.enter_context(nc.semaphore(name))
            return named[name]

        PS = ctx.enter_context(nc.psum_tensor("PS", [P, 8, BANK], F32))
        psf = PS[:, :, :].rearrange("p a b -> p (a b)")

        X = sb("X", [P, RT, D])
        XN = sb("XN", [P, RT, D])
        XT = sb("XT", [P, DC, ROWS])
        QT = sb("QT", [P, DC, ROWS])
        OT = sb("OT", [P, DC, ROWS])
        QB = sb("QB", [P, 2, DC, HPC, T])
        rows_b = sb("rows_b", [P, len(ROWV), D])
        colv = sb("colv", [P, N_COLS])
        ident = sb("ident", [P, P])
        ones = sb("ones", [P, P])
        before = sb("before", [P, P])
        headmask = sb("headmask", [P, HPC])
        parity = sb("parity", [P, 2])
        causal = sb("causal", [P, T])
        causal2 = sb("causal2", [P, P])
        lower8 = sb("lower8", [P, NE, NE])
        eps_c = sb("eps_c", [P, 1])
        stats = sb("stats", [P, RT, 6])
        mv = sb("mv", [P, RT, 2])
        rstd = sb("rstd", [P, RT])
        mx = sb("mx", [P, PAIRS, 2])
        nmax = sb("nmax", [P, PAIRS])
        rsum = sb("rsum", [P, PAIRS])
        rinv = sb("rinv", [P, 4])
        rexp = sb("rexp", [P, 4, 32])
        rbc = sb("rbc", [P, P])
        osc = sb("osc", [P, P])
        otmp = sb("otmp", [P, T])
        W4 = sb("W4", [P, 4, DC, D])
        PK = sb("PK", [P, 4, DC, D])
        PV = sb("PV", [P, 4, DC, D])

        ARENA = 34800
        arena = sb("arena", [P, ARENA])

        class Region:
            def __init__(self):
                self.at = 0

            def take(self, n):
                a = self.at
                self.at += (n + 7) // 8 * 8
                assert self.at <= ARENA, self.at
                return arena[:, a:a + n]

        r = Region()
        CT = r.take(2 * DC * S).rearrange("p (b c s) -> p b c s", b=2, c=DC)
        KT = r.take(2 * DC * S).rearrange("p (b c s) -> p b c s", b=2, c=DC)
        VS = r.take(2 * KT_N * D).rearrange("p (b k d) -> p b k d", b=2, k=KT_N)
        SC = r.take(2 * S).rearrange("p (b s) -> p b s", b=2)
        MK = r.take(2 * S).rearrange("p (b s) -> p b s", b=2)
        PT = r.take(KT_N * 4 * P).rearrange("p (k j q) -> p k j q", k=KT_N, j=4)
        r = Region()
        HN = r.take(RT * D).rearrange("p (t d) -> p t d", t=RT)
        X1 = r.take(RT * D).rearrange("p (t d) -> p t d", t=RT)
        PA = r.take(RT * FF).rearrange("p (t n) -> p t n", t=RT)
        PAT = r.take(FC * ROWS).rearrange("p (c r) -> p c r", c=FC)
        KT2 = r.take(DC * ROWS).rearrange("p (c r) -> p c r", c=DC)
        V2 = r.take(RT * D).rearrange("p (t d) -> p t d", t=RT)
        SP = r.take(2 * PAIRS * P).rearrange("p (u g k) -> p u g k", u=2, g=2 * PAIRS)
        SPT = r.take(2 * PAIRS * P).rearrange("p (u g q) -> p u g q", u=2, g=PAIRS)
        gmax = r.take(16)
        gsum = r.take(16)
        FKs = r.take(DC * FF).rearrange("p (c n) -> p c n", c=DC)
        FVs = r.take(FC * D).rearrange("p (n d) -> p n d", n=FC)
        pmax = r.take(20)
        psm = r.take(20)
        otm = r.take(4 * T).rearrange("p (a q) -> p a q", a=4)
        WQKV = r.take(DC * 2 * D).rearrange("p (c n) -> p c n", c=DC)
        WPJ = r.take(DC * D).rearrange("p (c n) -> p c n", c=DC)
        r2 = Region()
        r2.at = 2 * RT * D
        QKV = r2.take(B * D).rearrange("p (b n) -> p b n", b=B)
        PRD = r2.take(2 * B * 64).rearrange("p (r n) -> p r n", r=2)
        PRV = r2.take(2 * 64 * B).rearrange("p (r n) -> p r n", r=2)
        SE = r2.take(B * 2 * 4 * B).rearrange("p (b r h k) -> p b r h k", b=B, r=2, h=4)
        AO = r2.take(B * P).rearrange("p (b n) -> p b n", b=B)
        gm2 = r2.take(64)
        gs2 = r2.take(64)
        assert r.at <= 22600
        r3 = Region()
        r3.at = 22600
        W1 = r3.take(2 * DC * FF).rearrange("p (b c f) -> p b c f", b=2, c=DC)
        W2 = r3.take(2 * FC * D).rearrange("p (b f d) -> p b f d", b=2, f=FC)
        PROB, SEL, GW, GX = (r3.take(RT * NE).rearrange("p (t e) -> p t e", t=RT) for _ in range(4))
        GA, GB = (r3.take(RT * NE * NE).rearrange("p (t e j) -> p t e j", t=RT, e=NE) for _ in range(2))
        gmx, gsm = (r3.take(RT) for _ in range(2))
        wcur = r3.take(2 * 8).rearrange("p (b t) -> p b t", b=2)
        b1cur = r3.take(2 * FC).rearrange("p (b f) -> p b f", b=2)
        WRT = r3.take(DC * NE).rearrange("p (c e) -> p c e", c=DC)
        WGT = r3.take(DC * NE).rearrange("p (c e) -> p c e", c=DC)
        B2 = r3.take(D)
        wT = r3.take(ROWS)
        r3 = Region()
        r3.at = 2 * RT * D
        HT = r3.take(FC * ROWS).rearrange("p (f r) -> p f r", f=FC)
        ACC = r3.take(RT * D).rearrange("p (t d) -> p t d", t=RT)
        r5 = Region()
        r5.at = 2 * RT * D
        KT5 = r5.take(DC * ROWS).rearrange("p (c r) -> p c r", c=DC)
        V5 = r5.take(RT * D).rearrange("p (t d) -> p t d", t=RT)
        S5 = r5.take(RT * P).rearrange("p (t k) -> p t k", t=RT)
        S5T = r5.take(RT * P).rearrange("p (t q) -> p t q", t=RT)
        m5 = r5.take(RT)
        s5 = r5.take(RT)

        dve_n = [0]
        pool_n = [0]

        def lk(ins):
            dve_n[0] += 1
            ins.then_inc(sem("dve_step"), 1)
            nc.vector.wait_ge(sem("dve_step"), dve_n[0])

        def plk(ins):
            pool_n[0] += 1
            ins.then_inc(sem("pool_step"), 1)
            nc.gpsimd.wait_ge(sem("pool_step"), pool_n[0])

        def bc(ap, shape):
            return ap.broadcast_to(shape)

        def row(name):
            i = ROWV.index(name)
            return rows_b[:, i, :]

        def col(name, i=0, n=1):
            return colv[:, COLS[name] + i:COLS[name] + i + n]

        def ln_dve(v, k, src, dst, w=None, b=None, last=None):
            for t in range(RT):
                ins = v.bn_stats(stats[:, t, :], src[:, t, :])
            lk(ins)
            for t in range(RT):
                ins = v.bn_aggr(mv[:, t, :], stats[:, t, :])
            ins.then_inc(sem("ln_var"), 1)
            v.wait_ge(sem("ln_std"), k + 1)
            lk(v.reciprocal(rstd[:, :], rstd[:, :]))
            for t in range(RT):
                ins = v.tensor_scalar(dst[:, t, :], src[:, t, :], mv[:, t, 0:1], rstd[:, t:t + 1],
                                      ALU.subtract, ALU.mult)
            if w is not None:
                lk(ins)
                lk(v.tensor_tensor(dst[:, :, :], dst[:, :, :], bc(row(w).unsqueeze(1), [P, RT, D]), ALU.mult))
                ins = v.tensor_tensor(dst[:, :, :], dst[:, :, :], bc(row(b).unsqueeze(1), [P, RT, D]), ALU.add)
            dve_n[0] += 1
            ins.then_inc(sem("dve_step"), 1)
            v.wait_ge(sem("dve_step"), dve_n[0])
            v.engine_nop().then_inc(sem("ln_out"), 1)

        def ln_act(a, k):
            a.wait_ge(sem("ln_var"), k + 1)
            a.activation(rstd[:, :], mv[:, :, 1], ACT.Sqrt, bias=eps_c[:, 0:1]).then_inc(sem("ln_std"), 1)

        def tr_pe(pe, k, src, ready, value, bank=6):
            pe.wait_ge(ready, value)
            if k:
                pe.wait_ge(sem("tr_out_v"), k)
                pe.wait_ge(sem("tr_out_a"), k)
            for c in range(DC):
                for t in range(RT):
                    ins = pe.transpose(PS[:, bank + c, t * P:(t + 1) * P], src[:, t, c * P:(c + 1) * P], ident[:, :])
                ins.then_inc(sem("tr_ps"), 1)

        def tr_dve(v, k, dst, bank=6):
            v.wait_ge(sem("tr_ps"), 2 * k + 1)
            v.tensor_copy(dst[:, 0, :], PS[:, bank, :]).then_inc(sem("tr_out_v"), 1)

        def tr_act(a, k, dst, bank=6):
            a.wait_ge(sem("tr_ps"), 2 * k + 2)
            a.activation(dst[:, 1, :], PS[:, bank + 1, :], ACT.Copy).then_inc(sem("tr_out_a"), 1)

        def tr_done(eng, k):
            eng.wait_ge(sem("tr_out_v"), k + 1)
            eng.wait_ge(sem("tr_out_a"), k + 1)

        def rows_mm(pe, srcT, w, done, banks=(0, 1), n=D):
            for t in range(RT):
                for c in range(DC):
                    ins = pe.matmul(PS[:, banks[t // 2], (t % 2) * n:(t % 2 + 1) * n],
                                    srcT[:, c, t * P:(t + 1) * P], w[:, c, 0:n], start=(c == 0), stop=(c == DC - 1))
                ins.then_inc(done, 1)

        def cols_mm(pe, srcT, w, done, banks=(0, 1)):
            for m in range(DC):
                for c in range(DC):
                    ins = pe.matmul(PS[:, banks[m], :], w[:, c, m * P:(m + 1) * P], srcT[:, c, :],
                                    start=(c == 0), stop=(c == DC - 1))
                ins.then_inc(done, 1)

        def pst(banks, t):
            return PS[:, banks[t // 2], (t % 2) * D:(t % 2 + 1) * D]

        def hold(eng, s, v):
            eng.wait_ge(s, v)
            if not isinstance(v, int):
                eng.sem_inc(sem(f"held_{'pool' if eng is nc.gpsimd else 'dve'}"), 1)

        class Cross:
            def __init__(self, L, ln_k, tr_k):
                self.L, self.ln_k, self.tr_k = L, ln_k, tr_k
                x = f"x{L}_"
                self.q_ps, self.q_out = sem(x + "q_ps"), sem(x + "q_out")
                self.qb = sem(x + "qb")
                self.ctx0, self.ctx1 = sem(x + "ctx0"), sem(x + "ctx1")
                self.mask0, self.mask1 = sem(x + "mask0"), sem(x + "mask1")
                self.mk = sem(x + "mk")
                self.unit_ps = sem(x + "unit_ps")
                self.k_out, self.v_out = sem(x + "k_out"), sem(x + "v_out")
                self.score_ps = sem(x + "score_ps")
                self.score_out = sem(x + "score_out")
                self.nmax = sem(x + "nmax")
                self.exp = sem(x + "exp")
                self.turn_ps, self.turn_out = sem(x + "turn_ps"), sem(x + "turn_out")
                self.rexp = sem(x + "rexp")
                self.pv_ps, self.pv_out = sem(x + "pv_ps"), sem(x + "pv_out")
                self.gather_step = sem(x + "gather_step")
                self.o_ps = sem(x + "o_ps")
                self.done = sem(x + "done")

            def load(self, sp, b, p, after=None):
                if after is not None:
                    sp.wait_ge(self.unit_ps, after[0])
                sp.dma_start(CT[:, p, :, :], ctxT[b].rearrange("(c p) s -> p c s", p=P)).then_inc(
                    self.ctx0 if p == 0 else self.ctx1, 16)
                if self.L == 0:
                    if after is not None:
                        sp.wait_ge(self.score_out, after[1])
                    sp.dma_start(MK[:, p, :], bc(mask[b:b + 1, :], [P, S]) if isinstance(b, int)
                                 else bc(mask[bass.ds(b, 1), :], [P, S])).then_inc(
                        self.mask0 if p == 0 else self.mask1, 16)

            def sp_main(self, sp):
                with sp.Fori(0, 3) as i:
                    for p in range(2):
                        self.load(sp, 2 * i + 2 + p, p, after=(UNITS * (2 * i + p + 1), 16 * (2 * i + p + 1)))
                for p in range(2):
                    sp.wait_ge(self.ctx0 if p == 0 else self.ctx1, 64)

            def pool_batch(self, g, b, p, j, free):
                if free:
                    hold(g, self.score_ps, 16 * (b - 1))
                for c in range(DC):
                    g.tensor_tensor(QB[:, p, c, :, :],
                                    bc(QT[:, c, b * T:(b + 1) * T].unsqueeze(1) if isinstance(b, int)
                                       else QT[:, c, bass.ds(b * T, T)].unsqueeze(1), [P, HPC, T]),
                                    bc(headmask[:, :].unsqueeze(2), [P, HPC, T]), ALU.mult).then_inc(self.qb, 1)
                if self.L == 0:
                    hold(g, self.mask0 if p == 0 else self.mask1, 16 * (j + 1))
                    g.tensor_scalar(MK[:, p, :], MK[:, p, :], -1e9, None, ALU.mult).then_inc(self.mk, 1)

            def pool_main(self, g):
                g.wait_ge(self.q_out, 2)
                for p in range(2):
                    self.pool_batch(g, p, p, 0, False)
                with g.Fori(0, 3) as i:
                    for p in range(2):
                        self.pool_batch(g, 2 * i + 2 + p, p, i + 1, True)

            def unit(self, pe, b, p, u):
                if u == 0:
                    if not isinstance(b, int) or b > 0:
                        pe.wait_ge(self.v_out, V_UNITS * b)
                elif u <= K_UNITS:
                    pe.wait_ge(self.k_out, K_UNITS * b + u)
                else:
                    pe.wait_ge(self.v_out, V_UNITS * b + u - K_UNITS)
                if u < K_UNITS:
                    m, (k0, n) = u // 4, KEY_BLOCKS[u % 4]
                    for c in range(DC):
                        ins = pe.matmul(PS[:, 6, 0:n], W4[:, 1, c, m * P:(m + 1) * P], CT[:, p, c, k0:k0 + n],
                                        start=(c == 0), stop=(c == DC - 1))
                else:
                    for s in range(2):
                        kt = 2 * (u - K_UNITS) + s
                        if kt < KT_N:
                            n = P if kt < KT_N - 1 else S_LAST
                            for c in range(DC):
                                ins = pe.matmul(PS[0:n, 6, s * D:(s + 1) * D], CT[:, p, c, kt * P:kt * P + n],
                                                W4[:, 2, c, :], start=(c == 0), stop=(c == DC - 1))
                ins.then_inc(self.unit_ps, 1)

            def scores(self, pe, b, p, g):
                c, j = g // 4, g % 4
                if g == 0:
                    pe.wait_ge(self.qb, 2 * (b + 1))
                    pe.wait_ge(self.k_out, K_UNITS * (b + 1))
                lhs = QB[:, p, c, 2 * j:2 * j + 2, :].rearrange("p h q -> p (h q)")
                for half in range(2):
                    if g:
                        pe.wait_ge(self.score_out, 16 * b + 2 * g - 1 + half)
                    for k0, n in KEY_BLOCKS[2 * half:2 * half + 2]:
                        ins = pe.matmul(psf[:, k0:k0 + n], lhs, KT[:, p, c, k0:k0 + n], start=True, stop=True)
                    ins.then_inc(self.score_ps, 1)

            def turn(self, pe, b, p, g):
                pe.wait_ge(self.exp, 8 * b + g + 1)
                for k in range(4):
                    if g or k >= 2:
                        pe.wait_ge(self.turn_out, 32 * b + 4 * g + k - 1)
                    for kt in range(4 * k, min(4 * k + 4, KT_N)):
                        n = P if kt < KT_N - 1 else S_LAST
                        ins = pe.transpose(PS[0:n, 4 + k % 2, (kt % 4) * P:(kt % 4 + 1) * P],
                                           SC[:, g % 2, kt * P:kt * P + n], ident[:, :])
                    ins.then_inc(self.turn_ps, 1)

            def pv(self, pe, b, p, q):
                pe.wait_ge(self.rexp, 2 * b + q + 1)
                if q:
                    pe.wait_ge(self.pv_out, 2 * b + 1)
                pe.matmul(PS[:, 7, P:2 * P], rexp[:, :, :].rearrange("p a b -> p (a b)"), ident[:, :],
                          start=True, stop=True)
                pe.wait_ge(self.turn_out, 32 * b + 16 * (q + 1))
                if q == 0:
                    pe.wait_ge(self.v_out, V_UNITS * (b + 1))
                for kt in range(KT_N):
                    n = P if kt < KT_N - 1 else S_LAST
                    for j in range(4):
                        g = 4 * q + j
                        ins = pe.matmul(PS[32 * j:32 * j + 32, 7, 0:P], VS[0:n, p, kt, 32 * g:32 * g + 32],
                                        PT[0:n, kt, j, :], start=(kt == 0), stop=(kt == KT_N - 1))
                ins.then_inc(self.pv_ps, 1)

            def pe_batch(self, pe, b, p, project):
                if project:
                    nb, np_ = b + 1, 1 - p
                    arrived = 8 * nb + 8 if np_ else 8 * nb + 16
                unit = 0
                for g in range(PAIRS):
                    self.scores(pe, b, p, g)
                    if g:
                        self.turn(pe, b, p, g - 1)
                    if project:
                        if g == 0:
                            pe.wait_ge(self.ctx1 if np_ else self.ctx0, arrived)
                        self.unit(pe, nb, np_, unit)
                        unit += 1
                    if g == 4:
                        self.pv(pe, b, p, 0)
                if project:
                    for _ in range(4):
                        self.unit(pe, nb, np_, unit)
                        unit += 1
                self.turn(pe, b, p, PAIRS - 1)
                if project:
                    while unit < UNITS:
                        self.unit(pe, nb, np_, unit)
                        unit += 1
                self.pv(pe, b, p, 1)

            def pe_main(self, pe):
                tr_pe(pe, self.tr_k, XN, sem("ln_out"), self.ln_k + 1)
                tr_done(pe, self.tr_k)
                pe.wait_ge(sem(f"w_x{self.L}"), 64)
                cols_mm(pe, XT, W4[:, 0], self.q_ps)
                pe.wait_ge(self.ctx0, 16)
                for u in range(UNITS):
                    self.unit(pe, 0, 0, u)
                with pe.Fori(0, 3) as i:
                    for p in range(2):
                        self.pe_batch(pe, 2 * i + p, p, True)
                self.pe_batch(pe, 6, 0, True)
                self.pe_batch(pe, 7, 1, False)
                pe.wait_ge(self.done, 1)
                rows_mm(pe, OT, W4[:, 3], self.o_ps)

            def k_evac(self, v, b, p, u):
                v.wait_ge(self.unit_ps, UNITS * b + u + 1)
                m, (k0, n) = u // 4, KEY_BLOCKS[u % 4]
                if self.L == 0:
                    ins = v.tensor_scalar(KT[:, p, m, k0:k0 + n], PS[:, 6, 0:n], col("bk0", m), None, ALU.add)
                else:
                    ins = v.tensor_copy(KT[:, p, m, k0:k0 + n], PS[:, 6, 0:n])
                ins.then_inc(self.k_out, 1)

            def row_max(self, v, b, p, g):
                if g == 0 and self.L == 0:
                    v.wait_ge(self.mk, b + 1)
                if g >= 2:
                    v.wait_ge(self.turn_ps, 32 * b + 4 * (g - 1))
                for half, (k0, k1) in enumerate(((0, HALF_A), (HALF_A, S))):
                    hold(v, self.score_ps, 16 * b + 2 * g + 1 + half)
                    if self.L == 0:
                        ins = v.tensor_tensor_reduce(SC[:, g % 2, k0:k1], psf[:, k0:k1], MK[:, p, k0:k1], 1.0, -3e38,
                                                     ALU.add, ALU.max, mx[:, g, half:half + 1])
                    else:
                        ins = v.tensor_scalar(SC[:, g % 2, k0:k1], psf[:, k0:k1], 1.0, -3e38, ALU.mult, ALU.max,
                                              accum_out=mx[:, g, half:half + 1])
                    ins.then_inc(self.score_out, 1)
                v.wait_ge(self.score_out, 16 * b + 2 * g + 2)
                v.tensor_scalar(nmax[:, g:g + 1], mx[:, g, 0:1], mx[:, g, 1:2], -1.0, ALU.max, ALU.mult)\
                    .then_inc(self.nmax, 1)

            def recip(self, v, b, q):
                v.wait_ge(self.exp, 8 * b + 4 * q + 4)
                v.reciprocal(rinv[:, :], rsum[:, 4 * q:4 * q + 4]).then_inc(self.gather_step, 1)
                v.wait_ge(self.gather_step, 5 * (2 * b + q) + 1)
                v.tensor_copy(rexp[:, :, :], bc(rinv[:, :].unsqueeze(2), [P, 4, 32])).then_inc(self.rexp, 1)

            def gather(self, v, b, q):
                n0 = 5 * (2 * b + q) + 1
                v.wait_ge(self.pv_ps, 2 * b + q + 1)
                v.tensor_copy(rbc[:, :], PS[:, 7, P:2 * P]).then_inc(self.gather_step, 1)
                v.wait_ge(self.gather_step, n0 + 1)
                v.tensor_tensor(osc[:, :], PS[:, 7, 0:P], rbc[:, :], ALU.mult).then_inc(self.pv_out, 1)
                v.wait_ge(self.pv_out, 2 * b + q + 1)
                if self.L == 0:
                    v.tensor_scalar(otmp[:, :], osc[:, 0:T], parity[:, 0:1], col("bv0", q), ALU.mult, ALU.add)\
                        .then_inc(self.gather_step, 1)
                else:
                    v.tensor_scalar(otmp[:, :], osc[:, 0:T], parity[:, 0:1], None, ALU.mult).then_inc(self.gather_step, 1)
                v.wait_ge(self.gather_step, n0 + 2)
                v.tensor_scalar(osc[:, T:P], osc[:, T:P], parity[:, 1:2], None, ALU.mult).then_inc(self.gather_step, 1)
                v.wait_ge(self.gather_step, n0 + 3)
                dst = OT[:, q, b * T:(b + 1) * T] if isinstance(b, int) else OT[:, q, bass.ds(b * T, T)]
                v.tensor_tensor(dst, osc[:, T:P], otmp[:, :], ALU.add).then_inc(self.gather_step, 1)

            def dve_batch(self, v, b, p, project):
                for g in range(PAIRS):
                    self.row_max(v, b, p, g)
                    if project and g < K_UNITS:
                        self.k_evac(v, b + 1, 1 - p, g)
                    if g == 4:
                        self.recip(v, b, 0)
                        self.gather(v, b, 0)
                self.recip(v, b, 1)
                self.gather(v, b, 1)

            def dve_main(self, v):
                ln_dve(v, self.ln_k, X, XN)
                tr_dve(v, self.tr_k, XT)
                for m in range(DC):
                    v.wait_ge(self.q_ps, m + 1)
                    if self.L == 0:
                        ins = v.tensor_scalar(QT[:, m, :], PS[:, m, :], col("bq0", m), HD ** -0.5, ALU.add, ALU.mult)
                    else:
                        ins = v.tensor_scalar(QT[:, m, :], PS[:, m, :], HD ** -0.5, None, ALU.mult)
                    ins.then_inc(self.q_out, 1)
                for u in range(K_UNITS):
                    self.k_evac(v, 0, 0, u)
                with v.Fori(0, 3) as i:
                    for p in range(2):
                        self.dve_batch(v, 2 * i + p, p, True)
                self.dve_batch(v, 6, 0, True)
                self.dve_batch(v, 7, 1, False)
                v.wait_ge(self.gather_step, 80)
                v.engine_nop().then_inc(self.done, 1)
                lk(v.tensor_tensor(X[:, :, :], X[:, :, :], bc(row("bo0" if self.L == 0 else "bo3").unsqueeze(1),
                                                              [P, RT, D]), ALU.add))
                for t in range(RT):
                    v.wait_ge(self.o_ps, (t // 2 + 1) * 2)
                    ins = v.tensor_tensor(X[:, t, :], X[:, t, :], pst((0, 1), t), ALU.add)
                lk(ins)

            def v_evac(self, a, b, p, u):
                a.wait_ge(self.unit_ps, UNITS * b + u + 1)
                kt = 2 * (u - K_UNITS)
                if kt < KT_N - 1:
                    ins = a.activation(VS[:, p, kt:kt + 2, :].rearrange("p k d -> p (k d)"), PS[:, 6, :], ACT.Copy)
                else:
                    ins = a.activation(VS[0:S_LAST, p, kt, :], PS[0:S_LAST, 6, 0:D], ACT.Copy)
                ins.then_inc(self.v_out, 1)

            def turn_evac(self, a, b, g):
                for k in range(4):
                    a.wait_ge(self.turn_ps, 32 * b + 4 * g + k + 1)
                    if k < 3:
                        ins = a.activation(PT[:, 4 * k:4 * k + 4, g % 4, :],
                                           PS[:, 4 + k % 2, :].rearrange("p (k q) -> p k q", k=4), ACT.Copy)
                    else:
                        ins = a.activation(PT[0:S_LAST, KT_N - 1, g % 4, :], PS[0:S_LAST, 4 + k % 2, 0:P], ACT.Copy)
                    ins.then_inc(self.turn_out, 1)

            def exp_row(self, a, b, g):
                a.wait_ge(self.nmax, 8 * b + g + 1)
                a.activation(SC[:, g % 2, :], SC[:, g % 2, :], ACT.Exp, bias=nmax[:, g:g + 1],
                             accum_out=rsum[:, g:g + 1]).then_inc(self.exp, 1)

            def act_batch(self, a, b, p, project):
                for g in range(PAIRS):
                    if g:
                        self.turn_evac(a, b, g - 1)
                    self.exp_row(a, b, g)
                if project:
                    for u in range(K_UNITS, 12):
                        self.v_evac(a, b + 1, 1 - p, u)
                self.turn_evac(a, b, PAIRS - 1)
                if project:
                    for u in range(12, UNITS):
                        self.v_evac(a, b + 1, 1 - p, u)

            def act_main(self, a):
                ln_act(a, self.ln_k)
                tr_act(a, self.tr_k, XT)
                for u in range(K_UNITS, UNITS):
                    self.v_evac(a, 0, 0, u)
                with a.Fori(0, 3) as i:
                    for p in range(2):
                        self.act_batch(a, 2 * i + p, p, True)
                self.act_batch(a, 6, 0, True)
                self.act_batch(a, 7, 1, False)


        cross0 = Cross(0, 0, 0)
        cross1 = Cross(1, 7, 5)

        PATT = dict(
            q=dict(i=0, src=XT, k=PK[:, 0], v=PV[:, 0], nch=2, a=PA[:, :, 0:D], at=PAT[:, 0:2], C=0),
            k=dict(i=1, src=XT, k=PK[:, 1], v=PV[:, 1], nch=2, a=PA[:, :, D:2 * D], at=PAT[:, 2:4], C=2),
            v=dict(i=2, src=XT, k=PK[:, 2], v=PV[:, 2], nch=2, a=PA[:, :, 2 * D:3 * D], at=PAT[:, 4:6], C=4),
            p=dict(i=3, src=OT, k=PK[:, 3], v=PV[:, 3], nch=2, a=PA[:, :, 3 * D:4 * D], at=PAT[:, 6:8], C=6),
            f=dict(i=4, src=XT, k=FKs, v=FVs, nch=FC, a=PA, at=PAT, C=8))
        PSCALE = D ** -0.5

        def patt_scores(pe, p):
            for t in range(RT):
                n = RT * p["i"] + t
                if n >= 2:
                    pe.wait_ge(sem("p_exp"), n - 1)
                for blk in range(0, p["nch"] * P, BANK):
                    w = min(BANK, p["nch"] * P - blk)
                    for c in range(DC):
                        ins = pe.matmul(PS[:, 2 * (n % 2) + blk // BANK, 0:w], p["src"][:, c, t * P:(t + 1) * P],
                                        p["k"][:, c, blk:blk + w], start=(c == 0), stop=(c == DC - 1))
                ins.then_inc(sem("p_score"), 1)

        def patt_ps(p, n):
            return psf[:, 2 * BANK * (n % 2):2 * BANK * (n % 2) + p["nch"] * P]

        def patt_softmax_dve(v, p):
            def norm(n):
                v.wait_ge(sem("p_exp"), n + 1)
                lk(v.reciprocal(psm[:, n:n + 1], psm[:, n:n + 1]))
                a = p["a"][:, n % RT, :]
                v.tensor_scalar(a, a, psm[:, n:n + 1], None, ALU.mult).then_inc(sem("p_norm"), 1)

            for t in range(RT):
                n = RT * p["i"] + t
                v.wait_ge(sem("p_score"), n + 1)
                lk(v.tensor_reduce(pmax[:, n:n + 1], patt_ps(p, n), AX.X, ALU.max))
                v.tensor_scalar(pmax[:, n:n + 1], pmax[:, n:n + 1], -PSCALE, None, ALU.mult).then_inc(sem("p_nmax"), 1)
                if t:
                    norm(n - 1)
            norm(RT * p["i"] + RT - 1)

        def patt_exp(a, p):
            for t in range(RT):
                n = RT * p["i"] + t
                a.wait_ge(sem("p_nmax"), n + 1)
                a.activation(p["a"][:, t, :], patt_ps(p, n), ACT.Exp, bias=pmax[:, n:n + 1], scale=PSCALE,
                             accum_out=psm[:, n:n + 1]).then_inc(sem("p_exp"), 1)

        def patt_turn(pe, p):
            pe.wait_ge(sem("p_norm"), RT * (p["i"] + 1))
            for ch in range(p["nch"]):
                C = p["C"] + ch
                if C >= 2:
                    pe.wait_ge(sem("p_at_v" if C % 2 == 0 else "p_at_a"), C // 2)
                for t in range(RT):
                    ins = pe.transpose(PS[:, 4 + C % 2, t * P:(t + 1) * P], p["a"][:, t, ch * P:(ch + 1) * P],
                                       ident[:, :])
                ins.then_inc(sem("p_turn"), 1)

        def patt_turn_v(v, p):
            for ch in range(0, p["nch"], 2):
                v.wait_ge(sem("p_turn"), p["C"] + ch + 1)
                v.tensor_copy(p["at"][:, ch, :], PS[:, 4, :]).then_inc(sem("p_at_v"), 1)

        def patt_turn_a(a, p):
            for ch in range(1, p["nch"], 2):
                a.wait_ge(sem("p_turn"), p["C"] + ch + 1)
                a.activation(p["at"][:, ch, :], PS[:, 5, :], ACT.Copy).then_inc(sem("p_at_a"), 1)

        def patt_out(pe, p, cols):
            chunks = (p["C"] + p["nch"]) // 2
            pe.wait_ge(sem("p_at_v"), chunks)
            pe.wait_ge(sem("p_at_a"), chunks)
            for half in range(2):
                if 1 <= p["i"] <= 2:
                    pe.wait_ge(sem("p_out_v" if half == 0 else "p_out_a"), p["i"])
                if cols:
                    for ch in range(p["nch"]):
                        ins = pe.matmul(PS[:, 6 + half, :], p["v"][:, ch, half * P:(half + 1) * P], p["at"][:, ch, :],
                                        start=(ch == 0), stop=(ch == p["nch"] - 1))
                else:
                    for t in range(2 * half, 2 * half + 2):
                        for ch in range(p["nch"]):
                            ins = pe.matmul(pst((6, 7), t), p["at"][:, ch, t * P:(t + 1) * P], p["v"][:, ch, :],
                                            start=(ch == 0), stop=(ch == p["nch"] - 1))
                ins.then_inc(sem("p_out"), 1)

        def latent_dve(v):
            ln_dve(v, 1, X, XN)
            ln_dve(v, 2, XN, HN)
            tr_dve(v, 1, XT)
            patt_softmax_dve(v, PATT["q"])
            patt_softmax_dve(v, PATT["k"])
            patt_turn_v(v, PATT["q"])
            patt_softmax_dve(v, PATT["v"])
            patt_turn_v(v, PATT["k"])
            v.wait_ge(sem("p_out"), 1)
            v.tensor_scalar(QT[:, 0, :], PS[:, 6, :], HD ** -0.5, None, ALU.mult).then_inc(sem("p_out_v"), 1)
            patt_turn_v(v, PATT["v"])
            v.wait_ge(sem("p_out"), 3)
            v.tensor_copy(KT2[:, 0, :], PS[:, 6, :]).then_inc(sem("p_out_v"), 1)
            v.wait_ge(sem("p_out"), 5)
            v.tensor_copy(V2[:, 0:2, :].rearrange("p t d -> p (t d)"), PS[:, 6, :]).then_inc(sem("p_out_v"), 1)

            def soft(t):
                u = t % 2
                if t >= 2:
                    v.wait_ge(sem("s_turn"), 2 * (t - 1))
                v.wait_ge(sem("s_score"), t + 1)
                ins = v.tensor_tensor(SP[:, u], psf[:, 2 * BANK * u:2 * BANK * (u + 1)].rearrange("p (g k) -> p g k", k=T),
                                      bc(causal[:, :].unsqueeze(1), [P, 2 * PAIRS, T]), ALU.add)
                lk(ins)
                lk(v.tensor_reduce(gmax[:, :], SP[:, u], AX.X, ALU.max))
                v.tensor_tensor(SP[:, u], SP[:, u], bc(gmax[:, :].unsqueeze(2), [P, 2 * PAIRS, T]), ALU.subtract)\
                    .then_inc(sem("s_sub"), 1)

            def norm(t):
                u = t % 2
                v.wait_ge(sem("s_exp"), t + 1)
                lk(v.tensor_reduce(gsum[:, :], SP[:, u], AX.X, ALU.add))
                lk(v.reciprocal(gsum[:, :], gsum[:, :]))
                v.tensor_tensor(SP[:, u], SP[:, u], bc(gsum[:, :].unsqueeze(2), [P, 2 * PAIRS, T]), ALU.mult)\
                    .then_inc(sem("s_norm"), 1)

            def gather(t):
                v.wait_ge(sem("s_turn"), 2 * t + 1)
                v.tensor_copy(SPT[:, t % 2, 0:4].rearrange("p g q -> p (g q)"), PS[:, 4, :]).then_inc(sem("s_out_v"), 1)
                v.wait_ge(sem("s_pv"), t + 1)
                o = PS[:, 6:8, 0:D].rearrange("p b (c s q) -> p b c s q", c=DC, s=2)
                lk(v.tensor_scalar(otm[:, :, :].rearrange("p (b c) q -> p b c q", b=2), o[:, :, :, 0], parity[:, 0:1],
                                   None, ALU.mult))
                for bb in range(2):
                    b = 2 * t + bb
                    ins = v.scalar_tensor_tensor(OT[:, :, b * T:(b + 1) * T], o[:, bb, :, 1], parity[:, 1:2],
                                                 otm[:, 2 * bb:2 * bb + 2, :], ALU.mult, ALU.add)
                ins.then_inc(sem("s_o"), 1)

            for t in range(RT):
                soft(t)
                if t:
                    gather(t - 1)
                norm(t)
            gather(RT - 1)
            patt_softmax_dve(v, PATT["p"])
            patt_turn_v(v, PATT["p"])
            v.wait_ge(sem("p_out"), 8)
            for t in range(RT):
                ins = v.tensor_tensor(X1[:, t, :], pst((6, 7), t), XN[:, t, :], ALU.add)
            lk(ins)
            ln_dve(v, 3, X1, HN)
            tr_dve(v, 2, XT)
            patt_softmax_dve(v, PATT["f"])
            patt_turn_v(v, PATT["f"])
            lk(v.tensor_tensor(X[:, :, :], X[:, :, :], X1[:, :, :], ALU.add))
            for t in range(RT):
                v.wait_ge(sem("p_out"), 9 + t // 2)
                ins = v.tensor_tensor(X[:, t, :], X[:, t, :], pst((6, 7), t), ALU.add)
            lk(ins)

        def latent_act(a):
            ln_act(a, 1)
            ln_act(a, 2)
            tr_act(a, 1, XT)
            patt_exp(a, PATT["q"])
            patt_exp(a, PATT["k"])
            patt_turn_a(a, PATT["q"])
            patt_exp(a, PATT["v"])
            patt_turn_a(a, PATT["k"])
            a.wait_ge(sem("p_out"), 2)
            a.activation(QT[:, 1, :], PS[:, 7, :], ACT.Copy, scale=HD ** -0.5).then_inc(sem("p_out_a"), 1)
            patt_turn_a(a, PATT["v"])
            a.wait_ge(sem("p_out"), 4)
            a.activation(KT2[:, 1, :], PS[:, 7, :], ACT.Copy).then_inc(sem("p_out_a"), 1)
            a.wait_ge(sem("p_out"), 6)
            a.activation(V2[:, 2:4, :].rearrange("p t d -> p (t d)"), PS[:, 7, :], ACT.Copy).then_inc(sem("p_out_a"), 1)

            def turned(t):
                a.wait_ge(sem("s_turn"), 2 * t + 2)
                a.activation(SPT[:, t % 2, 4:8].rearrange("p g q -> p (g q)"), PS[:, 5, :], ACT.Copy)\
                    .then_inc(sem("s_out_a"), 1)

            for t in range(RT):
                a.wait_ge(sem("s_sub"), t + 1)
                a.activation(SP[:, t % 2], SP[:, t % 2], ACT.Exp).then_inc(sem("s_exp"), 1)
                if t:
                    turned(t - 1)
            turned(RT - 1)
            patt_exp(a, PATT["p"])
            patt_turn_a(a, PATT["p"])
            ln_act(a, 3)
            tr_act(a, 2, XT)
            patt_exp(a, PATT["f"])
            patt_turn_a(a, PATT["f"])

        def latent_pool(g):
            g.wait_ge(sem("p_out_v"), 1)
            g.wait_ge(sem("p_out_a"), 1)
            for b in range(B):
                if b >= 2:
                    g.wait_ge(sem("s_score"), b // 2)
                for c in range(DC):
                    g.tensor_tensor(QB[:, b % 2, c, :, :], bc(QT[:, c, b * T:(b + 1) * T].unsqueeze(1), [P, HPC, T]),
                                    bc(headmask[:, :].unsqueeze(2), [P, HPC, T]), ALU.mult).then_inc(sem("s_qb"), 1)

        def latent_pe(pe):
            tr_pe(pe, 1, HN, sem("ln_out"), 3)
            tr_done(pe, 1)
            pe.wait_ge(sem("w_patt"), 128)
            q, k, w, p, f = (PATT[n] for n in "qkvpf")
            patt_scores(pe, q)
            patt_scores(pe, k)
            patt_turn(pe, q)
            patt_scores(pe, w)
            patt_turn(pe, k)
            patt_out(pe, q, True)
            patt_turn(pe, w)
            patt_out(pe, k, True)
            patt_out(pe, w, False)

            def scores(t):
                if t == 0:
                    pe.wait_ge(sem("p_out_v"), 2)
                    pe.wait_ge(sem("p_out_a"), 2)
                    pe.wait_ge(sem("p_exp"), 12)
                if t >= 2:
                    pe.wait_ge(sem("s_sub"), t - 1)
                pe.wait_ge(sem("s_qb"), 4 * (t + 1))
                for g in range(PAIRS):
                    c, j = g // 4, g % 4
                    for bb in range(2):
                        b = 2 * t + bb
                        a0 = 2 * BANK * (t % 2) + g * P + bb * T
                        ins = pe.matmul(psf[:, a0:a0 + T], QB[:, bb, c, 2 * j:2 * j + 2, :].rearrange("p h q -> p (h q)"),
                                        KT2[:, c, b * T:(b + 1) * T], start=True, stop=True)
                ins.then_inc(sem("s_score"), 1)

            def turn(t):
                pe.wait_ge(sem("s_norm"), t + 1)
                for half in range(2):
                    if t:
                        pe.wait_ge(sem("s_out_v" if half == 0 else "s_out_a"), t)
                    for g in range(4 * half, 4 * half + 4):
                        ins = pe.transpose(PS[:, 4 + half, (g % 4) * P:(g % 4 + 1) * P],
                                           SP[:, t % 2, 2 * g:2 * g + 2, :].rearrange("p b k -> p (b k)"), ident[:, :])
                    ins.then_inc(sem("s_turn"), 1)

            def pv(t):
                if t == 0:
                    pe.wait_ge(sem("p_out_v"), 3)
                    pe.wait_ge(sem("p_out_a"), 3)
                pe.wait_ge(sem("s_out_v"), t + 1)
                pe.wait_ge(sem("s_out_a"), t + 1)
                if t:
                    pe.wait_ge(sem("s_o"), t)
                for bb in range(2):
                    for c in range(DC):
                        for j in range(4):
                            g = 4 * c + j
                            ins = pe.matmul(PS[32 * j:32 * j + 32, 6 + bb, c * P:(c + 1) * P],
                                            V2[T * bb:T * bb + T, t, 32 * g:32 * g + 32],
                                            SPT[T * bb:T * bb + T, t % 2, g, :], start=True, stop=True)
                ins.then_inc(sem("s_pv"), 1)

            scores(0)
            for t in range(RT):
                if t + 1 < RT:
                    scores(t + 1)
                turn(t)
                pv(t)
            pe.wait_ge(sem("s_o"), RT)
            patt_scores(pe, p)
            patt_turn(pe, p)
            patt_out(pe, p, False)
            tr_pe(pe, 2, HN, sem("ln_out"), 4)
            tr_done(pe, 2)
            pe.wait_ge(sem("w_ff"), 32)
            patt_scores(pe, f)
            patt_turn(pe, f)
            patt_out(pe, f, False)

        def top2(v):
            for t in range(RT):
                pj = bc(PROB[:, t, :].unsqueeze(1), [P, NE, NE])
                pe_ = bc(PROB[:, t, :].unsqueeze(2), [P, NE, NE])
                v.tensor_tensor(GA[:, t], pj, pe_, ALU.is_gt)
                ins = v.tensor_tensor(GB[:, t], pj, pe_, ALU.is_equal)
            lk(ins)
            lk(v.tensor_tensor(GB[:, :, :, :].rearrange("p t e j -> p t (e j)"),
                               GB[:, :, :, :].rearrange("p t e j -> p t (e j)"),
                               bc(lower8[:, :, :].rearrange("p e j -> p (e j)").unsqueeze(1), [P, RT, NE * NE]), ALU.mult))
            lk(v.tensor_tensor(GA[:, :, :, :].rearrange("p t e j -> p (t e j)"),
                               GA[:, :, :, :].rearrange("p t e j -> p (t e j)"),
                               GB[:, :, :, :].rearrange("p t e j -> p (t e j)"), ALU.add))
            lk(v.tensor_reduce(SEL[:, :, :], GA[:, :, :, :], AX.X, ALU.add))
            lk(v.tensor_scalar(SEL[:, :, :], SEL[:, :, :], 1.5, None, ALU.is_lt))

        def gate_pe(pe, L, tr_k, w):
            for t in range(RT):
                for c in range(DC):
                    ins = pe.matmul(PS[:, 0, t * NE:(t + 1) * NE], XT[:, c, t * P:(t + 1) * P], w[:, c, :],
                                    start=(c == 0), stop=(c == DC - 1))
            ins.then_inc(sem(f"g{L}_logit"), 1)

        class Experts:
            def __init__(self, L, w1, w2, act, bias):
                self.L, self.w1, self.w2, self.act, self.bias = L, w1, w2, act, bias
                e = f"e{L}_"
                self.s_w0, self.s_w1 = sem(e + "w0"), sem(e + "w1")
                self.s_h_ps, self.s_h_act = sem(e + "h_ps"), sem(e + "h_act")
                self.s_y_ps, self.s_y_out = sem(e + "y_ps"), sem(e + "y_out")
                self.s_b1 = sem(e + "b1")

            def load(self, sp, e, p):
                s = self.s_w1 if p else self.s_w0
                sp.dma_start(W1[:, p], self.w1[e].rearrange("(c p) f -> p c f", p=P)).then_inc(s, 16)
                sp.dma_start(W2[:, p], self.w2[e].rearrange("(f p) d -> p f d", p=P)).then_inc(s, 16)

            def sp_main(self, sp):
                with sp.Fori(0, 3) as i:
                    for p in range(2):
                        sp.wait_ge(self.s_y_ps, RT * (2 * i + p + 1))
                        self.load(sp, 2 * i + 2 + p, p)
                for s in (self.s_w0, self.s_w1):
                    sp.wait_ge(s, 128)

            def pe_main(self, pe):
                with pe.Fori(0, NE // 2) as i:
                    for p in range(2):
                        e = 2 * i + p
                        pe.wait_ge(self.s_w1 if p else self.s_w0, 32 * i + 32)
                        for f in range(FC):
                            if f >= 4:
                                pe.wait_ge(self.s_h_act, FC * e + f - 3)
                            for c in range(DC):
                                ins = pe.matmul(PS[:, f % 4, :], W1[:, p, c, f * P:(f + 1) * P], XT[:, c, :],
                                                start=(c == 0), stop=(c == DC - 1))
                            ins.then_inc(self.s_h_ps, 1)
                        pe.wait_ge(self.s_y_out, RT * e + RT)
                        for f in range(FC):
                            pe.wait_ge(self.s_h_act, FC * e + f + 1)
                            for t in range(RT):
                                ins = pe.matmul(PS[:, 4 + t, 0:D], HT[:, f, t * P:(t + 1) * P], W2[:, p, f, :],
                                                start=(f == 0), stop=(f == FC - 1))
                                if f == FC - 1:
                                    ins.then_inc(self.s_y_ps, 1)

            def act_main(self, a):
                with a.Fori(0, NE // 2) as i:
                    for p in range(2):
                        e = 2 * i + p
                        if self.bias:
                            a.wait_ge(self.s_b1, e + 1)
                        for f in range(FC):
                            a.wait_ge(self.s_h_ps, FC * e + f + 1)
                            a.activation(HT[:, f, :], PS[:, f % 4, :], self.act,
                                         bias=b1cur[:, p, f:f + 1] if self.bias else 0.0).then_inc(self.s_h_act, 1)

            def dve_main(self, v):
                v.engine_nop().then_inc(self.s_y_out, RT)
                with v.Fori(0, NE // 2) as i:
                    for p in range(2):
                        e = 2 * i + p
                        if self.bias:
                            v.tensor_copy(b1cur[:, p, :], colv[:, bass.ds(COLS["b1"] + FC * e, FC)]).then_inc(self.s_b1, 1)
                        v.tensor_copy(wcur[:, p, 0:RT], GW[:, :, bass.ds(e, 1)].rearrange("p t o -> p (t o)"))\
                            .then_inc(sem("wcur"), 1)
                        v.wait_ge(sem("wcur"), NE * self.L + e + 1)
                        for t in range(RT):
                            v.wait_ge(self.s_y_ps, RT * e + t + 1)
                            v.scalar_tensor_tensor(ACC[:, t, :], PS[:, 4 + t, 0:D], wcur[:, p, t:t + 1], ACC[:, t, :],
                                                   ALU.mult, ALU.add).then_inc(self.s_y_out, 1)
                v.wait_ge(self.s_y_out, RT * (NE + 1))
                lk(v.tensor_tensor(X[:, :, :], X[:, :, :], ACC[:, :, :], ALU.add))

        experts0 = Experts(0, m0w1, m0w2, ACT.Gelu, False)
        experts1 = Experts(1, m1w1, m1w2, ACT.Gelu_apprx_tanh, True)

        def across_pe(pe):
            tr_pe(pe, 3, HN, sem("ln_out"), 6)
            tr_done(pe, 3)
            pe.wait_ge(sem("w_moe"), 48)
            for b in range(B):
                for hh in range(2):
                    for c in range(DC):
                        ins = pe.matmul(PS[T * hh:T * hh + T, b // 2, (b % 2) * D:(b % 2 + 1) * D],
                                        XT[:, c, b * T:(b + 1) * T], WQKV[:, c, hh * D:(hh + 1) * D],
                                        start=(c == 0), stop=(c == DC - 1))
                if b % 2:
                    ins.then_inc(sem("c_qkv"), 1)
            pe.wait_ge(sem("c_ao"), 1)
            for half in range(2):
                for b in range(4 * half, 4 * half + 4):
                    ins = pe.transpose(PS[:, 4 + half, (b % 4) * P:(b % 4 + 1) * P], AO[:, b, :], ident[:, :])
                ins.then_inc(sem("c_turn"), 1)
            pe.wait_ge(sem("c_ot"), 2)
            rows_mm(pe, OT, WPJ, sem("c_proj"))
            tr_pe(pe, 4, XN, sem("ln_out"), 7)
            tr_done(pe, 4)
            gate_pe(pe, 0, 4, WRT)
            pe.wait_ge(sem("g0_sel"), 1)
            for t in range(RT):
                for s in range(t + 1):
                    ins = pe.matmul(PS[:, 1, t * NE:(t + 1) * NE], (before if s == t else ones)[:, :], SEL[:, s, :],
                                    start=(s == 0), stop=(s == t))
            ins.then_inc(sem("g0_rank"), 1)
            pe.wait_ge(sem("g0_w"), 1)
            experts0.pe_main(pe)

        def across_act(a):
            ln_act(a, 4)
            ln_act(a, 5)
            tr_act(a, 3, XT)
            for i in (1, 3):
                a.wait_ge(sem("c_qkv"), i + 1)
                a.activation(QKV[:, 2 * i:2 * i + 2, :].rearrange("p b n -> p (b n)"), PS[:, i, :], ACT.Copy)\
                    .then_inc(sem("c_in_a"), 1)
            a.wait_ge(sem("c_sub"), 1)
            a.activation(SE[:, :, :, :, :].rearrange("p b r h k -> p (b r h k)"),
                         SE[:, :, :, :, :].rearrange("p b r h k -> p (b r h k)"), ACT.Exp, scale=HD ** -0.5)\
                .then_inc(sem("c_exp"), 1)
            a.wait_ge(sem("c_turn"), 2)
            a.activation(OT[:, :, 4 * T:8 * T].rearrange("p h (b t) -> p b h t", b=4),
                         PS[:, 5, :].rearrange("p (b h t) -> p b h t", b=4, h=2), ACT.Copy).then_inc(sem("c_ot"), 1)
            ln_act(a, 6)
            tr_act(a, 4, XT)
            a.wait_ge(sem("g0_sub"), 1)
            a.activation(PROB[:, :, :], PROB[:, :, :], ACT.Exp).then_inc(sem("g0_exp"), 1)
            experts0.act_main(a)

        def across_dve(v):
            ln_dve(v, 4, X, XN)
            ln_dve(v, 5, XN, HN, "ln1w", "ln1b")
            tr_dve(v, 3, XT)
            lk(v.memset(SE[:, :, :, :, :].rearrange("p b r h k -> p (b r h k)"), NEG))
            for i in (0, 2):
                v.wait_ge(sem("c_qkv"), i + 1)
                ins = v.tensor_copy(QKV[:, 2 * i:2 * i + 2, :].rearrange("p b n -> p (b n)"), PS[:, i, :])
            lk(ins)
            v.wait_ge(sem("c_in_a"), 2)
            for b in range(B):
                n = b + 1
                for r in range(2):
                    ins = v.tensor_tensor(PRD[:, r, 0:n * 64].rearrange("p (k h d) -> p k h d", k=n, h=4),
                                          bc(QKV[:, b, 0:P].rearrange("p (h r d) -> p h r d", h=4, r=2)[:, :, r, :]
                                             .unsqueeze(1), [P, n, 4, HD]),
                                          QKV[:, 0:n, P:P + 64].rearrange("p k (h d) -> p k h d", h=4), ALU.mult)
                lk(ins)
                for r in range(2):
                    ins = v.tensor_reduce(SE[:, b, r, :, 0:n].rearrange("p h k -> p k h"),
                                          PRD[:, r, 0:n * 64].rearrange("p (k h d) -> p k h d", k=n, h=4), AX.X, ALU.add)
                lk(ins)
            se = SE[:, :, :, :, :].rearrange("p b r h k -> p (b r h) k")
            lk(v.tensor_reduce(gm2[:, :], se, AX.X, ALU.max))
            v.tensor_tensor(se, se, bc(gm2[:, :].unsqueeze(2), [P, 64, B]), ALU.subtract).then_inc(sem("c_sub"), 1)
            v.wait_ge(sem("c_exp"), 1)
            lk(v.tensor_reduce(gs2[:, :], se, AX.X, ALU.add))
            lk(v.reciprocal(gs2[:, :], gs2[:, :]))
            lk(v.tensor_tensor(se, se, bc(gs2[:, :].unsqueeze(2), [P, 64, B]), ALU.mult))
            for b in range(B):
                n = b + 1
                for r in range(2):
                    ins = v.tensor_tensor(PRV[:, r, 0:n * 64].rearrange("p (h d k) -> p h d k", h=4, d=HD),
                                          bc(SE[:, b, r, :, 0:n].unsqueeze(2), [P, 4, HD, n]),
                                          QKV[:, 0:n, P + 64:D].rearrange("p k (h d) -> p h d k", h=4), ALU.mult)
                lk(ins)
                for r in range(2):
                    ins = v.tensor_reduce(AO[:, b, :].rearrange("p (h r d) -> p h r d", h=4, r=2)[:, :, r, :],
                                          PRV[:, r, 0:n * 64].rearrange("p (h d k) -> p h d k", h=4, d=HD), AX.X, ALU.add)
                lk(ins)
            v.engine_nop().then_inc(sem("c_ao"), 1)
            v.wait_ge(sem("c_turn"), 1)
            v.tensor_copy(OT[:, :, 0:4 * T].rearrange("p h (b t) -> p b h t", b=4),
                          PS[:, 4, :].rearrange("p (b h t) -> p b h t", b=4, h=2)).then_inc(sem("c_ot"), 1)
            for t in range(RT):
                v.wait_ge(sem("c_proj"), (t // 2 + 1) * 2)
                ins = v.tensor_tensor(ACC[:, t, :], pst((0, 1), t), XN[:, t, :], ALU.add)
            lk(ins)
            ln_dve(v, 6, ACC, XN, "ln2w", "ln2b")
            tr_dve(v, 4, XT)
            v.wait_ge(sem("g0_logit"), 1)
            lg = PS[:, 0, 0:RT * NE].rearrange("p (t e) -> p t e", t=RT)
            lk(v.tensor_reduce(gmx[:, :], lg, AX.X, ALU.max))
            v.tensor_tensor(PROB[:, :, :], lg, bc(gmx[:, :].unsqueeze(2), [P, RT, NE]), ALU.subtract)\
                .then_inc(sem("g0_sub"), 1)
            v.wait_ge(sem("g0_exp"), 1)
            lk(v.tensor_reduce(gsm[:, :], PROB[:, :, :], AX.X, ALU.add))
            lk(v.reciprocal(gsm[:, :], gsm[:, :]))
            lk(v.tensor_tensor(PROB[:, :, :], PROB[:, :, :], bc(gsm[:, :].unsqueeze(2), [P, RT, NE]), ALU.mult))
            top2(v)
            v.engine_nop().then_inc(sem("g0_sel"), 1)
            lk(v.tensor_tensor(GW[:, :, :], PROB[:, :, :], SEL[:, :, :], ALU.mult))
            lk(v.tensor_reduce(gsm[:, :], GW[:, :, :], AX.X, ALU.add))
            lk(v.reciprocal(gsm[:, :], gsm[:, :]))
            lk(v.tensor_tensor(GW[:, :, :], GW[:, :, :], bc(gsm[:, :].unsqueeze(2), [P, RT, NE]), ALU.mult))
            v.wait_ge(sem("g0_rank"), 1)
            lk(v.tensor_scalar(GX[:, :, :], PS[:, 1, 0:RT * NE].rearrange("p (t e) -> p t e", t=RT), CAP - 0.5, None,
                               ALU.is_lt))
            lk(v.tensor_tensor(GW[:, :, :], GW[:, :, :], GX[:, :, :], ALU.mult))
            v.engine_nop().then_inc(sem("g0_w"), 1)
            experts0.dve_main(v)

        WA = PK

        def single_pe(pe):
            tr_pe(pe, 6, XN, sem("ln_out"), 9)
            tr_done(pe, 6)
            pe.wait_ge(sem("w_a"), 64)
            cols_mm(pe, XT, WA[:, 0], sem("d_q"), banks=(0, 1))
            cols_mm(pe, XT, WA[:, 1], sem("d_q"), banks=(2, 3))
            rows_mm(pe, XT, WA[:, 2], sem("d_q"), banks=(4, 5))
            pe.wait_ge(sem("d_in"), 4)
            for t in range(RT):
                for c in range(DC):
                    ins = pe.matmul(PS[:, 0, t * P:(t + 1) * P], QT[:, c, t * P:(t + 1) * P],
                                    KT5[:, c, t * P:(t + 1) * P], start=(c == 0), stop=(c == DC - 1))
            ins.then_inc(sem("d_score"), 1)
            pe.wait_ge(sem("d_norm"), 1)
            for t in range(RT):
                ins = pe.transpose(PS[:, 1, t * P:(t + 1) * P], S5[:, t, :], ident[:, :])
            ins.then_inc(sem("d_turn"), 1)
            pe.wait_ge(sem("d_p"), 1)
            pe.wait_ge(sem("d_v"), 2)
            for m in range(DC):
                for t in range(RT):
                    ins = pe.matmul(PS[:, 2 + m, t * P:(t + 1) * P], V5[:, t, m * P:(m + 1) * P], S5T[:, t, :],
                                    start=True, stop=True)
                ins.then_inc(sem("d_pv"), 1)
            pe.wait_ge(sem("d_o"), 2)
            rows_mm(pe, OT, WA[:, 3], sem("d_out"), banks=(4, 5))

        def single_dve(v):
            ln_dve(v, 8, X, XN)
            tr_dve(v, 6, XT)
            for m in range(DC):
                v.wait_ge(sem("d_q"), m + 1)
                v.tensor_scalar(QT[:, m, :], PS[:, m, :], col("bq5", m), D ** -0.5, ALU.add, ALU.mult)\
                    .then_inc(sem("d_in"), 1)
            for m in range(DC):
                v.wait_ge(sem("d_q"), 3 + m)
                v.tensor_scalar(KT5[:, m, :], PS[:, 2 + m, :], col("bk5", m), None, ALU.add).then_inc(sem("d_in"), 1)
            v.wait_ge(sem("d_score"), 1)
            lk(v.tensor_tensor(S5[:, :, :], PS[:, 0, :].rearrange("p (t k) -> p t k", t=RT),
                               bc(causal2[:, :].unsqueeze(1), [P, RT, P]), ALU.add))
            lk(v.tensor_reduce(m5[:, :], S5[:, :, :], AX.X, ALU.max))
            v.tensor_tensor(S5[:, :, :], S5[:, :, :], bc(m5[:, :].unsqueeze(2), [P, RT, P]), ALU.subtract)\
                .then_inc(sem("d_sub"), 1)
            v.wait_ge(sem("d_exp"), 1)
            lk(v.tensor_reduce(s5[:, :], S5[:, :, :], AX.X, ALU.add))
            lk(v.reciprocal(s5[:, :], s5[:, :]))
            v.tensor_tensor(S5[:, :, :], S5[:, :, :], bc(s5[:, :].unsqueeze(2), [P, RT, P]), ALU.mult)\
                .then_inc(sem("d_norm"), 1)
            v.wait_ge(sem("d_turn"), 1)
            v.tensor_copy(S5T[:, :, :].rearrange("p t q -> p (t q)"), PS[:, 1, :]).then_inc(sem("d_p"), 1)
            for m in range(DC):
                v.wait_ge(sem("d_pv"), m + 1)
                v.tensor_scalar(OT[:, m, :], PS[:, 2 + m, :], col("bv5", m), None, ALU.add).then_inc(sem("d_o"), 1)
            lk(v.tensor_tensor(X[:, :, :], X[:, :, :], bc(row("bo5").unsqueeze(1), [P, RT, D]), ALU.add))
            for t in range(RT):
                v.wait_ge(sem("d_out"), (t // 2 + 1) * 2)
                ins = v.tensor_tensor(X[:, t, :], X[:, t, :], pst((4, 5), t), ALU.add)
            lk(ins)

        def single_act(a):
            ln_act(a, 8)
            tr_act(a, 6, XT)
            for i in range(2):
                a.wait_ge(sem("d_q"), 4 + 2 * (i + 1))
                a.activation(V5[:, 2 * i:2 * i + 2, :].rearrange("p t d -> p (t d)"), PS[:, 4 + i, :], ACT.Copy)\
                    .then_inc(sem("d_v"), 1)
            a.wait_ge(sem("d_sub"), 1)
            a.activation(S5[:, :, :], S5[:, :, :], ACT.Exp).then_inc(sem("d_exp"), 1)

        def moe_pe(pe):
            tr_pe(pe, 7, XN, sem("ln_out"), 10)
            tr_done(pe, 7)
            pe.wait_ge(sem("w_gate1"), 32)
            gate_pe(pe, 1, 7, WGT)
            pe.wait_ge(sem("g1_w"), 1)
            for t in range(RT):
                ins = pe.transpose(PS[0:NE, 1, t * P:(t + 1) * P], GW[:, t, :], ident[:, :])
            ins.then_inc(sem("g1_turn"), 1)
            pe.wait_ge(sem("g1_wT"), 1)
            for t in range(RT):
                ins = pe.matmul(pst((2, 3), t), wT[0:NE, t * P:(t + 1) * P], B2[0:NE, :], start=True, stop=True)
            ins.then_inc(sem("g1_b2"), 1)
            pe.wait_ge(sem("g1_acc"), 1)
            experts1.pe_main(pe)

        def moe_dve(v):
            ln_dve(v, 9, X, XN)
            tr_dve(v, 7, XT)
            v.wait_ge(sem("g1_exp"), 1)
            lk(v.tensor_scalar(PROB[:, :, :], PROB[:, :, :], 1.0, None, ALU.add))
            lk(v.reciprocal(PROB[:, :, :], PROB[:, :, :]))
            top2(v)
            lk(v.tensor_tensor(GW[:, :, :], PROB[:, :, :], SEL[:, :, :], ALU.mult))
            v.engine_nop().then_inc(sem("g1_w"), 1)
            v.wait_ge(sem("g1_turn"), 1)
            v.tensor_copy(wT[0:NE, :], PS[0:NE, 1, :]).then_inc(sem("g1_wT"), 1)
            v.wait_ge(sem("g1_b2"), 1)
            for i in range(2):
                ins = v.tensor_copy(ACC[:, 2 * i:2 * i + 2, :].rearrange("p t d -> p (t d)"), PS[:, 2 + i, :])
            lk(ins)
            v.engine_nop().then_inc(sem("g1_acc"), 1)
            experts1.dve_main(v)

        def moe_act(a):
            ln_act(a, 9)
            tr_act(a, 7, XT)
            a.wait_ge(sem("g1_logit"), 1)
            a.activation(PROB[:, :, :], PS[:, 0, 0:RT * NE].rearrange("p (t e) -> p t e", t=RT), ACT.Exp, scale=-1.0)\
                .then_inc(sem("g1_exp"), 1)
            experts1.act_main(a)

        block = ctx.enter_context(nc.Block())

        def w_load(eng, dst, src, s):
            eng.dma_start(dst, src.rearrange("(c p) n -> p c n", p=P)).then_inc(s, 16)

        @block.sync
        def _(sp):
            sp.dma_start(X[:, :, :], x.rearrange("(t p) d -> p t d", p=P)).then_inc(sem("x_in"), 16)
            for i in range(4):
                w_load(sp, W4[:, i], xw0[i], sem("w_x0"))
            sp.dma_start(colv[:, :], cols).then_inc(sem("vec_in"), 16)
            for b in range(2):
                cross0.load(sp, b, b)
            sp.dma_start(rows_b[:, :, :], bc(rowv.unsqueeze(0), [P, len(ROWV), D])).then_inc(sem("vec_in"), 16)
            for i in range(4):
                w_load(sp, PK[:, i], patt_k[i], sem("w_patt"))
                w_load(sp, PV[:, i], patt_v[i], sem("w_patt"))
            cross0.sp_main(sp)
            sp.wait_ge(cross0.o_ps, RT)
            w_load(sp, FKs, fk, sem("w_ff"))
            w_load(sp, FVs, fv, sem("w_ff"))
            w_load(sp, WQKV, wqkv, sem("w_moe"))
            w_load(sp, WPJ, wproj, sem("w_moe"))
            w_load(sp, WRT, wrt, sem("w_moe"))
            for e in range(2):
                experts0.load(sp, e, e)
            for i in range(4):
                w_load(sp, W4[:, i], xw1[i], sem("w_x1"))
            sp.wait_ge(sem("p_score"), RT * 4)
            for i in range(4):
                w_load(sp, WA[:, i], aw[i], sem("w_a"))
            experts0.sp_main(sp)
            sp.wait_ge(sem("experts0_done"), 1)
            for b in range(2):
                cross1.load(sp, b, b)
            cross1.sp_main(sp)
            sp.wait_ge(cross1.o_ps, RT)
            w_load(sp, WGT, wg, sem("w_gate1"))
            sp.dma_start(B2[0:NE, :], b2).then_inc(sem("w_gate1"), 16)
            for e in range(2):
                experts1.load(sp, e, e)
            experts1.sp_main(sp)
            sp.wait_ge(sem("x_final"), 1)
            sp.dma_start(out.rearrange("(t p) d -> p t d", p=P), X[:, :, :]).then_inc(sem("stored"), 16)
            sp.wait_ge(sem("stored"), 16)

        @block.gpsimd
        def _(g):
            plk(g.memset(ident[:, :], 0.0))
            plk(g.memset(ones[:, :], 1.0))
            plk(g.memset(before[:, :], 1.0))
            plk(g.memset(headmask[:, :], 1.0))
            plk(g.memset(causal[:, :], 0.0))
            plk(g.memset(causal2[:, :], 0.0))
            plk(g.memset(lower8[:, :, :], 1.0))
            plk(g.memset(eps_c[:, :], EPS))
            plk(g.affine_select(out=ident[:, :], in_=ident[:, :], compare_op=ALU.not_equal, fill=1.0, base=0,
                            pattern=[[-1, P]], channel_multiplier=1))
            plk(g.affine_select(out=before[:, :], in_=before[:, :], compare_op=ALU.is_gt, fill=0.0, base=0,
                            pattern=[[1, P]], channel_multiplier=-1))
            plk(g.affine_select(out=headmask[:, :], in_=headmask[:, :], compare_op=ALU.is_ge, fill=0.0, base=0,
                                pattern=[[-HD, HPC]], channel_multiplier=1))
            plk(g.affine_select(out=headmask[:, :], in_=headmask[:, :], compare_op=ALU.is_ge, fill=0.0, base=HD - 1,
                            pattern=[[HD, HPC]], channel_multiplier=-1))
            for i in range(2):
                plk(g.affine_select(out=causal[T * i:T * i + T, :], in_=causal[T * i:T * i + T, :], compare_op=ALU.is_ge,
                                fill=NEG, base=0, pattern=[[-1, T]], channel_multiplier=1))
            plk(g.affine_select(out=lower8[:, :, :], in_=lower8[:, :, :], compare_op=ALU.is_gt, fill=0.0, base=0,
                            pattern=[[1, NE], [-1, NE]], channel_multiplier=0))
            plk(g.affine_select(out=causal2[:, :], in_=causal2[:, :], compare_op=ALU.is_ge, fill=NEG, base=0,
                                pattern=[[-1, P]], channel_multiplier=1))
            plk(g.memset(causal2[T:P, 0:T], NEG))
            g.engine_nop().then_inc(sem("consts"), 1)
            cross0.pool_main(g)
            latent_pool(g)
            cross1.pool_main(g)

        @block.tensor
        def _(pe):
            pe.wait_ge(sem("consts"), 1)
            cross0.pe_main(pe)
            latent_pe(pe)
            across_pe(pe)
            cross1.pe_main(pe)
            single_pe(pe)
            moe_pe(pe)

        @block.vector
        def _(v):
            v.wait_ge(sem("consts"), 1)
            lk(v.tensor_reduce(parity[:, :], headmask[:, :].rearrange("p (a b) -> p b a", b=2), AX.X, ALU.add))
            v.wait_ge(sem("vec_in"), 32)
            v.wait_ge(sem("x_in"), 16)
            cross0.dve_main(v)
            latent_dve(v)
            across_dve(v)
            v.engine_nop().then_inc(sem("experts0_done"), 1)
            cross1.dve_main(v)
            single_dve(v)
            moe_dve(v)
            v.engine_nop().then_inc(sem("x_final"), 1)

        @block.scalar
        def _(a):
            a.wait_ge(sem("consts"), 1)
            cross0.act_main(a)
            latent_act(a)
            across_act(a)
            cross1.act_main(a)
            single_act(a)
            moe_act(a)


NAMES = ["x", "ctxT", "mask", "cols", "rowv", "xw0", "patt_k", "patt_v", "fk", "fv", "wqkv", "wproj", "wrt", "m0w1",
         "m0w2", "xw1", "aw", "wg", "m1w1", "m1w2", "b2"]


def layout(inputs):
    import numpy as np
    """What kernel() gives the program: every input in its own type, only laid out."""
    np_ = {k: np.asarray(v) for k, v in inputs.items()}
    t = lambda n: np_[n].T
    colm = lambda v: v.reshape(-1, 128).T
    cols = np.concatenate([colm(np_[n]) for n in ("L0_xattn_bq", "L0_xattn_bk", "L0_xattn_bv", "L1_attn_bq", "L1_attn_bk", "L1_attn_bv", "L1_ffn_b1")], axis=1)
    rowv = np.stack([np_[n] for n in ("L0_xattn_bo", "L0_ffn_ln1_weight", "L0_ffn_ln1_bias", "L0_ffn_ln2_weight", "L0_ffn_ln2_bias", "L1_xattn_bo", "L1_attn_bo")])
    w = np_["L0_ffn_qkv_weight"].reshape(2, 4, 64, 256)
    wqkv = np.concatenate([w[:, :, 0:32].reshape(2, 128, 256), w[:, :, 32:48].reshape(2, 64, 256), w[:, :, 48:64].reshape(2, 64, 256)], axis=1).reshape(512, 256).T
    return [np.ascontiguousarray(a) for a in (
        np_["x"].reshape(512, 256), np_["ctx_1024"].transpose(0, 2, 1), np_["mask_Bx1x1xS2_ff0"].reshape(8, 1601), cols, rowv,
        np.stack([np_["L0_xattn_" + n] for n in ("wq", "wk", "wv", "wo")]),
        np.stack([t("L0_attn_" + n) for n in ("qK", "kK", "vK", "pK")]), np.stack([np_["L0_attn_" + n] for n in ("qV", "kV", "vV", "pV")]),
        t("L0_attn_fK"), np_["L0_attn_fV"], wqkv, t("L0_ffn_proj_weight"), np_["L0_ffn_router_weight"],
        np_["L0_ffn_moe_w1"], np_["L0_ffn_moe_w2"],
        np.stack([t("L1_xattn_" + n) for n in ("Wq", "Wk", "Wv", "Wo")]),
        np.stack([np_["L1_attn_" + n] for n in ("Wq", "Wk", "Wv", "Wo")]),
        np_["L1_ffn_Wg"], np_["L1_ffn_W1"], np_["L1_ffn_W2"], np_["L1_ffn_b2"])]


def kernel(**inputs):
    import numpy as np
    import concourse.bacc as bacc
    from concourse.bass_utils import run_bass_kernel_spmd

    nc = bacc.Bacc("TRN2", target_bir_lowering=False, num_devices=1)
    arrays, args = {}, []
    for name, a in zip(NAMES, layout(inputs)):
        arrays[f"in_{name}"] = a
        args.append(nc.dram_tensor(f"in_{name}", a.shape, mybir.dt.from_np(a.dtype), kind="ExternalInput").ap())
    args.append(nc.dram_tensor("out", (ROWS, D), F32, kind="ExternalOutput").ap())
    perceiver(nc, *args)
    r = run_bass_kernel_spmd(nc, [arrays], core_ids=[0])
    return r.results[0]["out"].reshape(B, T, D)
```

```python
from contextlib import ExitStack

import concourse.bass as bass
from concourse import mybir

F32 = mybir.dt.float32
F16 = mybir.dt.float16
ALU = mybir.AluOpType
ACT = mybir.ActivationFunctionType
AX = mybir.AxisListType

P = 128
B, T, D = 8, 64, 256
ROWS = B * T
RT = ROWS // P
DC = D // P
H, HD = 16, 16
PAIRS = H // 2
HPC = P // HD
S = 1601
KT_N = (S + P - 1) // P
S_LAST = S - (KT_N - 1) * P
HALF_A = 1024
BANK = 512
NE, FF = 8, 1024
FC = FF // P
CAP = 160
EPS = 1e-5
NEG = -1e30
K_UNITS = 8
V_UNITS = (KT_N + 1) // 2
UNITS = K_UNITS + V_UNITS
WS = 16.0
SPREAD = 16 * 16
KEY_BLOCKS = [(0, 512), (512, 512), (1024, 512), (1536, S - 1536)]

COLS = {"bq0": 0, "bk0": 8, "bv0": 10, "bq5": 12, "bk5": 14, "bv5": 16, "b1": 18}
N_COLS = 18 + NE * FC
ROWV = ["bo0", "ln1w", "ln1b", "ln2w", "ln2b", "bo3", "bo5"]


def perceiver(nc, x, ctxT, mask, cols, rowv, xw0, patt_k, patt_v, fk, fv, wqkv, wproj, wrt, m0w1, m0w2,
              xw1, aw, wg, m1w1, m1w2, b2, out):
    ctx = ExitStack()
    with ctx:
        def sb(name, shape, dt=F32):
            return ctx.enter_context(nc.sbuf_tensor(name, shape, dt))

        named = {}

        def sem(name):
            if name not in named:
                named[name] = ctx.enter_context(nc.semaphore(name))
            return named[name]

        PS = ctx.enter_context(nc.psum_tensor("PS", [P, 8, BANK], F32))
        psf = PS[:, :, :].rearrange("p a b -> p (a b)")

        X = sb("X", [P, RT, D])
        OT = sb("OT", [P, DC, ROWS])
        QS = sb("QS", [P, B, PAIRS, P], F16)
        rows_b = sb("rows_b", [P, len(ROWV), D])
        colv = sb("colv", [P, N_COLS])
        ident = sb("ident", [P, P])
        ones = sb("ones", [P, P])
        before = sb("before", [P, P])
        headmask = sb("headmask", [P, HPC])
        parity = sb("parity", [P, 2])
        causal = sb("causal", [P, T])
        causal2 = sb("causal2", [P, P])
        lower8 = sb("lower8", [P, NE, NE])
        eps_c = sb("eps_c", [P, 1])
        stats = sb("stats", [P, RT, 6])
        mv = sb("mv", [P, RT, 2])
        rstd = sb("rstd", [P, RT])
        mx = sb("mx", [P, PAIRS, 2])
        nmax = sb("nmax", [P, PAIRS])
        rsum = sb("rsum", [P, PAIRS])
        rinv = sb("rinv", [P, 4])
        rexp = sb("rexp", [P, 4, 32])
        rbc = sb("rbc", [P, P])
        osc = sb("osc", [P, P])
        otmp = sb("otmp", [P, T])
        W4 = sb("W4", [P, 4, DC, D])
        WH = sb("WH", [P, 2, DC, D], F16)
        WL = sb("WL", [P, 2, DC, D], F16)
        bkw = sb("bkw", [P, DC])

        ARENA = 39000
        arena = sb("arena", [P, ARENA])

        class Region:
            def __init__(self):
                self.at = 0

            def take(self, n):
                a = self.at
                self.at += (n + 7) // 8 * 8
                assert self.at <= ARENA, self.at
                return arena[:, a:a + n]

        r = Region()
        CR = r.take(DC * S).rearrange("p (c s) -> p c s", c=DC)
        CHL = [r.take(DC * S).bitcast(F16).rearrange("p (h c s) -> p h c s", h=2, c=DC) for _ in range(2)]
        KHL = r.take(DC * S).bitcast(F16).rearrange("p (h c s) -> p h c s", h=2, c=DC)
        KS = r.take(PAIRS * S // 2 + 4).bitcast(F16)[:, 0:PAIRS * S].rearrange("p (g s) -> p g s", g=PAIRS)
        VS = r.take(2 * KT_N * D).rearrange("p (b k d) -> p b k d", b=2, k=KT_N)
        SC = r.take(2 * S).rearrange("p (b s) -> p b s", b=2)
        MK = r.take(2 * S).rearrange("p (b s) -> p b s", b=2)
        PT_AT = r.at
        PT = r.take(KT_N * 4 * P).rearrange("p (k j q) -> p k j q", k=KT_N, j=4)
        r = Region()
        r.at = PT_AT
        Q32 = r.take(2 * ROWS).rearrange("p (u r) -> p u r", u=2)
        QH = r.take(ROWS).bitcast(F16).rearrange("p (u r) -> p u r", u=2)
        WQ4 = r.take(DC * PAIRS * P).rearrange("p (c g q n) -> p c g q n", c=DC, g=PAIRS, q=4)
        Q_END = r.at
        r = Region()
        r.at = ARENA - 2 * RT * D - 16
        assert r.at >= Q_END
        XN = r.take(RT * D).rearrange("p (t d) -> p t d", t=RT)
        XT = r.take(DC * ROWS).rearrange("p (c r) -> p c r", c=DC)
        STAGE_END = ARENA - 2 * RT * D - 16
        r = Region()
        PK = r.take(4 * DC * D).rearrange("p (i c d) -> p i c d", i=4, c=DC)
        PV = r.take(4 * DC * D).rearrange("p (i c d) -> p i c d", i=4, c=DC)
        PARAMS_END = r.at
        r = Region()
        r.at = PARAMS_END
        QT = r.take(DC * ROWS).rearrange("p (c r) -> p c r", c=DC)
        HN = r.take(RT * D).rearrange("p (t d) -> p t d", t=RT)
        X1 = r.take(RT * D).rearrange("p (t d) -> p t d", t=RT)
        PA = r.take(RT * FF).rearrange("p (t n) -> p t n", t=RT)
        PAT = r.take(FC * ROWS).rearrange("p (c r) -> p c r", c=FC)
        KT2 = r.take(DC * ROWS).rearrange("p (c r) -> p c r", c=DC)
        V2 = r.take(RT * D).rearrange("p (t d) -> p t d", t=RT)
        SP = r.take(2 * PAIRS * P).rearrange("p (u g k) -> p u g k", u=2, g=2 * PAIRS)
        SPT = r.take(2 * PAIRS * P).rearrange("p (u g q) -> p u g q", u=2, g=PAIRS)
        gmax = r.take(16)
        gsum = r.take(16)
        QB = r.take(2 * DC * HPC * T).rearrange("p (u c h q) -> p u c h q", u=2, c=DC, h=HPC)
        FF_AT = r.at
        FKs = r.take(DC * FF).rearrange("p (c n) -> p c n", c=DC)
        FVs = r.take(FC * D).rearrange("p (n d) -> p n d", n=FC)
        pmax = r.take(20)
        psm = r.take(20)
        otm = r.take(4 * T).rearrange("p (a q) -> p a q", a=4)
        WQKV = r.take(DC * 2 * D).rearrange("p (c n) -> p c n", c=DC)
        WPJ = r.take(DC * D).rearrange("p (c n) -> p c n", c=DC)
        r2 = Region()
        r2.at = PARAMS_END + 3 * RT * D
        QKV = r2.take(B * D).rearrange("p (b n) -> p b n", b=B)
        PRD = r2.take(2 * B * 64).rearrange("p (r n) -> p r n", r=2)
        PRV = r2.take(2 * 64 * B).rearrange("p (r n) -> p r n", r=2)
        SE = r2.take(B * 2 * 4 * B).rearrange("p (b r h k) -> p b r h k", b=B, r=2, h=4)
        AO = r2.take(B * P).rearrange("p (b n) -> p b n", b=B)
        gm2 = r2.take(64)
        gs2 = r2.take(64)
        r3 = Region()
        r3.at = FF_AT
        W1 = [None, r3.take(DC * FF).rearrange("p (c f) -> p c f", c=DC)]
        W2 = [None, r3.take(FC * D).rearrange("p (f d) -> p f d", f=FC)]
        r3.at = r.at
        W1[0] = r3.take(DC * FF).rearrange("p (c f) -> p c f", c=DC)
        W2[0] = r3.take(FC * D).rearrange("p (f d) -> p f d", f=FC)
        PROB, SEL, GW, GX = (r3.take(RT * NE).rearrange("p (t e) -> p t e", t=RT) for _ in range(4))
        GA, GB = (r3.take(RT * NE * NE).rearrange("p (t e j) -> p t e j", t=RT, e=NE) for _ in range(2))
        gmx, gsm = (r3.take(RT) for _ in range(2))
        wcur = r3.take(2 * 8).rearrange("p (b t) -> p b t", b=2)
        b1cur = r3.take(2 * FC).rearrange("p (b f) -> p b f", b=2)
        WRT = r3.take(DC * NE).rearrange("p (c e) -> p c e", c=DC)
        WGT = r3.take(DC * NE).rearrange("p (c e) -> p c e", c=DC)
        B2 = r3.take(D)
        wT = r3.take(ROWS)
        assert r3.at <= STAGE_END, r3.at
        r3 = Region()
        r3.at = PARAMS_END + 3 * RT * D
        HT = r3.take(FC * ROWS).rearrange("p (f r) -> p f r", f=FC)
        ACC = r3.take(RT * D).rearrange("p (t d) -> p t d", t=RT)
        r5 = Region()
        r5.at = PARAMS_END + DC * ROWS
        KT5 = r5.take(DC * ROWS).rearrange("p (c r) -> p c r", c=DC)
        V5 = r5.take(RT * D).rearrange("p (t d) -> p t d", t=RT)
        S5 = r5.take(RT * P).rearrange("p (t k) -> p t k", t=RT)
        S5T = r5.take(RT * P).rearrange("p (t q) -> p t q", t=RT)
        m5 = r5.take(RT)
        s5 = r5.take(RT)

        dve_n = [0]
        pool_n = [0]

        def lk(ins):
            dve_n[0] += 1
            ins.then_inc(sem("dve_step"), 1)
            nc.vector.wait_ge(sem("dve_step"), dve_n[0])

        def plk(ins):
            pool_n[0] += 1
            ins.then_inc(sem("pool_step"), 1)
            nc.gpsimd.wait_ge(sem("pool_step"), pool_n[0])

        def bc(ap, shape):
            return ap.broadcast_to(shape)

        def row(name):
            i = ROWV.index(name)
            return rows_b[:, i, :]

        def col(name, i=0, n=1):
            return colv[:, COLS[name] + i:COLS[name] + i + n]

        def ln_dve(v, k, src, dst, w=None, b=None, last=None):
            for t in range(RT):
                ins = v.bn_stats(stats[:, t, :], src[:, t, :])
            lk(ins)
            for t in range(RT):
                ins = v.bn_aggr(mv[:, t, :], stats[:, t, :])
            ins.then_inc(sem("ln_var"), 1)
            v.wait_ge(sem("ln_std"), k + 1)
            lk(v.reciprocal(rstd[:, :], rstd[:, :]))
            for t in range(RT):
                ins = v.tensor_scalar(dst[:, t, :], src[:, t, :], mv[:, t, 0:1], rstd[:, t:t + 1],
                                      ALU.subtract, ALU.mult)
            if w is not None:
                lk(ins)
                lk(v.tensor_tensor(dst[:, :, :], dst[:, :, :], bc(row(w).unsqueeze(1), [P, RT, D]), ALU.mult))
                ins = v.tensor_tensor(dst[:, :, :], dst[:, :, :], bc(row(b).unsqueeze(1), [P, RT, D]), ALU.add)
            dve_n[0] += 1
            ins.then_inc(sem("dve_step"), 1)
            v.wait_ge(sem("dve_step"), dve_n[0])
            v.engine_nop().then_inc(sem("ln_out"), 1)

        def ln_act(a, k):
            a.wait_ge(sem("ln_var"), k + 1)
            a.activation(rstd[:, :], mv[:, :, 1], ACT.Sqrt, bias=eps_c[:, 0:1]).then_inc(sem("ln_std"), 1)

        def tr_pe(pe, k, src, ready, value, bank=6):
            pe.wait_ge(ready, value)
            if k:
                pe.wait_ge(sem("tr_out_v"), k)
                pe.wait_ge(sem("tr_out_a"), k)
            for c in range(DC):
                for t in range(RT):
                    ins = pe.transpose(PS[:, bank + c, t * P:(t + 1) * P], src[:, t, c * P:(c + 1) * P], ident[:, :])
                ins.then_inc(sem("tr_ps"), 1)

        def tr_dve(v, k, dst, bank=6):
            v.wait_ge(sem("tr_ps"), 2 * k + 1)
            v.tensor_copy(dst[:, 0, :], PS[:, bank, :]).then_inc(sem("tr_out_v"), 1)

        def tr_act(a, k, dst, bank=6):
            a.wait_ge(sem("tr_ps"), 2 * k + 2)
            a.activation(dst[:, 1, :], PS[:, bank + 1, :], ACT.Copy).then_inc(sem("tr_out_a"), 1)

        def tr_done(eng, k):
            eng.wait_ge(sem("tr_out_v"), k + 1)
            eng.wait_ge(sem("tr_out_a"), k + 1)

        def rows_mm(pe, srcT, w, done, banks=(0, 1), n=D):
            for t in range(RT):
                for c in range(DC):
                    ins = pe.matmul(PS[:, banks[t // 2], (t % 2) * n:(t % 2 + 1) * n],
                                    srcT[:, c, t * P:(t + 1) * P], w[:, c, 0:n], start=(c == 0), stop=(c == DC - 1))
                ins.then_inc(done, 1)

        def cols_mm(pe, srcT, w, done, banks=(0, 1)):
            for m in range(DC):
                for c in range(DC):
                    ins = pe.matmul(PS[:, banks[m], :], w[:, c, m * P:(m + 1) * P], srcT[:, c, :],
                                    start=(c == 0), stop=(c == DC - 1))
                ins.then_inc(done, 1)

        def pst(banks, t):
            return PS[:, banks[t // 2], (t % 2) * D:(t % 2 + 1) * D]

        def hold(eng, s, v):
            eng.wait_ge(s, v)
            if not isinstance(v, int):
                eng.sem_inc(sem("held_pool" if eng is nc.gpsimd else "held_pe" if eng is nc.tensor else
                                 "held_sp" if eng is nc.sync else "held_dve"), 1)

        class Cross:
            def __init__(self, L, ln_k, tr_k):
                self.L, self.ln_k, self.tr_k = L, ln_k, tr_k
                x = f"x{L}_"
                self.q_ps, self.q_out = sem(x + "q_ps"), sem(x + "q_out")
                self.q_high, self.qs = sem(x + "q_high"), sem(x + "qs")
                self.wq = sem(x + "wq")
                self.w_split = sem(x + "w_split")
                self.ctx = sem(x + "ctx")
                self.high, self.split = sem(x + "high"), sem(x + "split")
                self.mask0, self.mask1 = sem(x + "mask0"), sem(x + "mask1")
                self.mk = sem(x + "mk")
                self.k_high = sem(x + "k_high")
                self.ks = [sem(x + "ks0"), sem(x + "ks1")]
                self.unit_ps = sem(x + "unit_ps")
                self.k_out, self.v_out = sem(x + "k_out"), sem(x + "v_out")
                self.score_ps = sem(x + "score_ps")
                self.score_out = sem(x + "score_out")
                self.nmax = sem(x + "nmax")
                self.exp = sem(x + "exp")
                self.turn_ps, self.turn_out = sem(x + "turn_ps"), sem(x + "turn_out")
                self.rexp = sem(x + "rexp")
                self.pv_ps, self.pv_out = sem(x + "pv_ps"), sem(x + "pv_out")
                self.gather_step = sem(x + "gather_step")
                self.o_ps = sem(x + "o_ps")
                self.done = sem(x + "done")

            def load_ctx(self, sp, b):
                if not isinstance(b, int) or b:
                    hold(sp, self.split, b)
                sp.dma_start(CR, ctxT[b].rearrange("(c p) s -> p c s", p=P)).then_inc(self.ctx, 16)

            def load_mask(self, sp, b, p):
                if self.L == 0:
                    sp.dma_start(MK[:, p, :], bc(mask[b:b + 1, :] if isinstance(b, int) else mask[bass.ds(b, 1), :],
                                                 [P, S])).then_inc(self.mask0 if p == 0 else self.mask1, 16)

            def spread_k(self, sp, b, c):
                hold(sp, self.k_out, K_UNITS * b + 4 * (c + 1))
                if not isinstance(b, int) or b:
                    hold(sp, self.score_ps, 16 * (b - 1) + 8 * (c + 1))
                for j in range(4):
                    for quad in range(4):
                        sp.dma_start(KS[32 * quad:32 * quad + 32, 4 * c + j, :],
                                     KHL[32 * j:32 * j + 32, quad // 2, c, :]).then_inc(self.ks[c], 16)

            def sp_first(self, sp):
                self.load_ctx(sp, 0)
                self.load_mask(sp, 0, 0)
                self.load_mask(sp, 1, 1)
                self.load_ctx(sp, 1)

            def sp_main(self, sp):
                self.load_ctx(sp, 2)
                for c in range(DC):
                    self.spread_k(sp, 0, c)
                with sp.Fori(0, 2) as i:
                    for p in range(2):
                        self.sp_batch(sp, 2 * i + p, p)
                self.sp_batch(sp, 4, 0)
                self.sp_batch(sp, 5, 1)
                for c in range(DC):
                    self.spread_k(sp, 7, c)
                for c in range(DC):
                    sp.wait_ge(self.ks[c], 8 * SPREAD)

            def sp_batch(self, sp, b, p):
                self.spread_k(sp, b + 1, 0)
                self.spread_k(sp, b + 1, 1)
                if not isinstance(b, int) or b + 3 < B:
                    self.load_ctx(sp, b + 3)
                if self.L == 0:
                    hold(sp, self.score_out, 16 * (b + 1))
                self.load_mask(sp, b + 2, p)

            def pool_split(self, g, b, p, free):
                hold(g, self.ctx, 16 * (b + 1))
                if free:
                    hold(g, self.unit_ps, UNITS * (b - 1))
                g.tensor_copy(CHL[p][:, 0], CR).then_inc(self.high, 1)
                hold(g, self.high, b + 1)
                g.tensor_tensor(CHL[p][:, 1], CR, CHL[p][:, 0], ALU.subtract).then_inc(self.split, 1)

            def pool_mask(self, g, b, p, j):
                if self.L == 0:
                    hold(g, self.mask0 if p == 0 else self.mask1, 16 * (j + 1))
                    g.tensor_scalar(MK[:, p, :], MK[:, p, :], -1e9 * WS, None, ALU.mult).then_inc(self.mk, 1)

            def pool_main(self, g):
                for p in range(2):
                    self.pool_split(g, p, p, False)
                    self.pool_mask(g, p, p, 0)
                with g.Fori(0, 3) as i:
                    for p in range(2):
                        self.pool_split(g, 2 * i + 2 + p, p, True)
                        self.pool_mask(g, 2 * i + 2 + p, p, i + 1)

            def pe_unit(self, pe, kind, b, p, n, bank):
                if kind == "k":
                    m, (k0, w) = n // 4, KEY_BLOCKS[n % 4]
                    mms = [(PS[:, bank, 0:w], W[:, 0, c, m * P:(m + 1) * P], CHL[p][:, h, c, k0:k0 + w], c == 0 and i == 0,
                            c == DC - 1 and i == 2)
                           for c in range(DC) for i, (W, h) in enumerate(((WH, 0), (WH, 1), (WL, 0)))]
                else:
                    mms = []
                    for s in range(2):
                        kt = 2 * n + s
                        if kt < KT_N:
                            w = P if kt < KT_N - 1 else S_LAST
                            mms += [(PS[0:w, bank, s * D:(s + 1) * D], CHL[p][:, h, c, kt * P:kt * P + w], W[:, 1, c, :],
                                     c == 0 and i == 0, c == DC - 1 and i == 2)
                                    for c in range(DC) for i, (W, h) in enumerate(((WH, 0), (WL, 0), (WH, 1)))]
                for o, lhs, rhs, first, last in mms:
                    ins = pe.matmul(o, lhs, rhs, start=first, stop=last)
                ins.then_inc(self.unit_ps, 1)

            def scores(self, pe, b, g):
                if g % 4 == 0:
                    hold(pe, self.ks[g // 4], SPREAD * (b + 1))
                lhs = QS[:, b, g, :] if isinstance(b, int) else QS[:, bass.ds(b, 1), g, :].rearrange("p o q -> p (o q)")
                for half in range(2):
                    if g or not isinstance(b, int) or b:
                        hold(pe, self.score_out, 16 * b + 2 * g - 1 + half)
                    for k0, n in KEY_BLOCKS[2 * half:2 * half + 2]:
                        ins = pe.matmul(psf[:, k0:k0 + n], lhs, KS[:, g, k0:k0 + n], start=True, stop=True)
                    ins.then_inc(self.score_ps, 1)

            def turn(self, pe, b, p, g):
                pe.wait_ge(self.exp, 8 * b + g + 1)
                for k in range(4):
                    if g or k >= 2 or not isinstance(b, int) or b:
                        pe.wait_ge(self.turn_out, 32 * b + 4 * g + k - 1)
                    for kt in range(4 * k, min(4 * k + 4, KT_N)):
                        n = P if kt < KT_N - 1 else S_LAST
                        ins = pe.transpose(PS[0:n, 4 + k % 2, (kt % 4) * P:(kt % 4 + 1) * P],
                                           SC[:, g % 2, kt * P:kt * P + n], ident[:, :])
                    ins.then_inc(self.turn_ps, 1)

            def pv(self, pe, b, p, q):
                if q == 0:
                    hold(pe, self.v_out, V_UNITS * (b + 1))
                pe.wait_ge(self.rexp, 2 * b + q + 1)
                if q:
                    pe.wait_ge(self.pv_out, 2 * b + 1)
                pe.matmul(PS[:, 7, P:2 * P], rexp[:, :, :].rearrange("p a b -> p (a b)"), ident[:, :],
                          start=True, stop=True)
                pe.wait_ge(self.turn_out, 32 * b + 16 * (q + 1))
                for kt in range(KT_N):
                    n = P if kt < KT_N - 1 else S_LAST
                    for j in range(4):
                        g = 4 * q + j
                        ins = pe.matmul(PS[32 * j:32 * j + 32, 7, 0:P], VS[0:n, p, kt, 32 * g:32 * g + 32],
                                        PT[0:n, kt, j, :], start=(kt == 0), stop=(kt == KT_N - 1))
                ins.then_inc(self.pv_ps, 1)

            def pe_batch(self, pe, b, p, project):
                nb, np_ = b + 1, 1 - p
                former = not isinstance(b, int) or b > 0
                for g in range(PAIRS):
                    self.scores(pe, b, g)
                    if project:
                        if g == 0:
                            hold(pe, self.split, nb + 1)
                            pe.wait_ge(self.v_out, V_UNITS * nb)
                        elif g == 1:
                            pe.wait_ge(self.k_out, K_UNITS * nb + 1)
                        else:
                            pe.wait_ge(self.v_out, V_UNITS * nb + g - 1)
                        self.pe_unit(pe, "k", nb, np_, g, 6)
                    if g == 1 and former:
                        self.pv(pe, b - 1, 1 - p, 1)
                    if g == 5:
                        self.pv(pe, b, p, 0)
                    if g:
                        self.turn(pe, b, p, g - 1)
                    elif former:
                        self.turn(pe, b - 1, 1 - p, PAIRS - 1)
                    if project and g:
                        pe.wait_ge(self.k_out, K_UNITS * nb + g + 1)
                        self.pe_unit(pe, "v", nb, np_, g - 1, 6)

            def pe_main(self, pe):
                tr_pe(pe, self.tr_k, XN, sem("ln_out"), self.ln_k + 1)
                tr_done(pe, self.tr_k)
                pe.wait_ge(self.wq, 2)
                for g in range(PAIRS):
                    if g >= 4:
                        pe.wait_ge(self.q_out, g - 3)
                    for c in range(DC):
                        ins = pe.matmul(PS[:, g % 4, :], WQ4[:, c, g, :, :].rearrange("p q n -> p (q n)"),
                                        XT[:, c, :], start=(c == 0), stop=(c == DC - 1))
                    ins.then_inc(self.q_ps, 1)
                pe.wait_ge(self.split, 1)
                pe.wait_ge(self.w_split, 1)
                for u in range(UNITS):
                    if u >= 3:
                        if u - 3 < K_UNITS:
                            pe.wait_ge(self.k_out, u - 2)
                        else:
                            pe.wait_ge(self.v_out, u - 2 - K_UNITS)
                    self.pe_unit(pe, "k" if u < K_UNITS else "v", 0, 0, u if u < K_UNITS else u - K_UNITS, 5 + u % 3)
                pe.wait_ge(self.qs, PAIRS)
                self.pe_batch(pe, 0, 0, True)
                with pe.Fori(0, 3) as i:
                    for p in range(2):
                        self.pe_batch(pe, 2 * i + 1 + p, 1 - p, True)
                self.pe_batch(pe, 7, 1, False)
                self.turn(pe, 7, 1, PAIRS - 1)
                self.pv(pe, 7, 1, 1)
                pe.wait_ge(self.done, 1)
                rows_mm(pe, OT, W4[:, 3], self.o_ps)

            def unit_no(self, b, kind, n):
                if isinstance(b, int) and b == 0:
                    return n + 1 + (K_UNITS if kind == "v" else 0)
                return UNITS * b + (n + 1 + max(0, n - 1) if kind == "k" else 2 * n + 3)

            def k_low(self, v, b, n, bank=6):
                v.wait_ge(self.k_high, K_UNITS * b + n + 1)
                m, (k0, w) = n // 4, KEY_BLOCKS[n % 4]
                if self.L == 0:
                    ins = v.scalar_tensor_tensor(KHL[:, 1, m, k0:k0 + w], PS[:, bank, 0:w], bkw[:, m:m + 1],
                                                 KHL[:, 0, m, k0:k0 + w], ALU.add, ALU.subtract)
                else:
                    ins = v.tensor_tensor(KHL[:, 1, m, k0:k0 + w], PS[:, bank, 0:w], KHL[:, 0, m, k0:k0 + w], ALU.subtract)
                ins.then_inc(self.k_out, 1)

            def v_evac(self, v, b, p, n, bank=6):
                v.wait_ge(self.unit_ps, self.unit_no(b, "v", n))
                kt = 2 * n
                if kt < KT_N - 1:
                    ins = v.tensor_scalar(VS[:, p, kt:kt + 2, :].rearrange("p k d -> p (k d)"), PS[:, bank, :], 1 / WS, None,
                                          ALU.mult)
                else:
                    ins = v.tensor_scalar(VS[0:S_LAST, p, kt, :], PS[0:S_LAST, bank, 0:D], 1 / WS, None, ALU.mult)
                ins.then_inc(self.v_out, 1)

            def row_max(self, v, b, p, g):
                if g == 0 and self.L == 0:
                    v.wait_ge(self.mk, b + 1)
                if g >= 2 or not isinstance(b, int) or b:
                    v.wait_ge(self.turn_ps, 32 * b + 4 * (g - 1))
                for half, (k0, k1) in enumerate(((0, HALF_A), (HALF_A, S))):
                    hold(v, self.score_ps, 16 * b + 2 * g + 1 + half)
                    if self.L == 0:
                        ins = v.tensor_tensor_reduce(SC[:, g % 2, k0:k1], psf[:, k0:k1], MK[:, p, k0:k1], 1.0, -3e38,
                                                     ALU.add, ALU.max, mx[:, g, half:half + 1])
                    else:
                        ins = v.tensor_scalar(SC[:, g % 2, k0:k1], psf[:, k0:k1], 1.0, -3e38, ALU.mult, ALU.max,
                                              accum_out=mx[:, g, half:half + 1])
                    ins.then_inc(self.score_out, 1)
                v.wait_ge(self.score_out, 16 * b + 2 * g + 2)
                v.tensor_scalar(nmax[:, g:g + 1], mx[:, g, 0:1], mx[:, g, 1:2], -1 / WS, ALU.max, ALU.mult)\
                    .then_inc(self.nmax, 1)

            def recip(self, v, b, q):
                v.wait_ge(self.exp, 8 * b + 4 * q + 4)
                v.reciprocal(rinv[:, :], rsum[:, 4 * q:4 * q + 4]).then_inc(self.gather_step, 1)
                v.wait_ge(self.gather_step, 5 * (2 * b + q) + 1)
                v.tensor_copy(rexp[:, :, :], bc(rinv[:, :].unsqueeze(2), [P, 4, 32])).then_inc(self.rexp, 1)

            def gather(self, v, b, q):
                n0 = 5 * (2 * b + q) + 1
                v.wait_ge(self.pv_ps, 2 * b + q + 1)
                v.tensor_copy(rbc[:, :], PS[:, 7, P:2 * P]).then_inc(self.gather_step, 1)
                v.wait_ge(self.gather_step, n0 + 1)
                v.tensor_tensor(osc[:, :], PS[:, 7, 0:P], rbc[:, :], ALU.mult).then_inc(self.pv_out, 1)
                v.wait_ge(self.pv_out, 2 * b + q + 1)
                if self.L == 0:
                    v.tensor_scalar(otmp[:, :], osc[:, 0:T], parity[:, 0:1], col("bv0", q), ALU.mult, ALU.add)\
                        .then_inc(self.gather_step, 1)
                else:
                    v.tensor_scalar(otmp[:, :], osc[:, 0:T], parity[:, 0:1], None, ALU.mult).then_inc(self.gather_step, 1)
                v.wait_ge(self.gather_step, n0 + 2)
                v.tensor_scalar(osc[:, T:P], osc[:, T:P], parity[:, 1:2], None, ALU.mult).then_inc(self.gather_step, 1)
                v.wait_ge(self.gather_step, n0 + 3)
                dst = OT[:, q, b * T:(b + 1) * T] if isinstance(b, int) else OT[:, q, bass.ds(b * T, T)]
                v.tensor_tensor(dst, osc[:, T:P], otmp[:, :], ALU.add).then_inc(self.gather_step, 1)

            def dve_batch(self, v, b, p, project):
                nb, np_ = b + 1, 1 - p
                former = not isinstance(b, int) or b > 0
                for g in range(PAIRS):
                    self.row_max(v, b, p, g)
                    if g == 2 and former:
                        self.gather(v, b - 1, 1)
                    if g == 6:
                        self.gather(v, b, 0)
                    if project:
                        self.k_low(v, nb, g)
                    if g == 0 and former:
                        self.recip(v, b - 1, 1)
                    if g == 4:
                        self.recip(v, b, 0)
                    if project and g:
                        self.v_evac(v, nb, np_, g - 1)

            def dve_main(self, v):
                ln_dve(v, self.ln_k, X, XN)
                v.wait_ge(sem(f"w_x{self.L}"), 64)
                for c in range(DC):
                    v.tensor_copy(WQ4[:, c, :, :, :], bc(W4[:, 0, c, :].rearrange("p (g n) -> p g n", g=PAIRS).unsqueeze(2),
                                                         [P, PAIRS, 4, 32])).then_inc(self.wq, 1)
                lk(v.tensor_scalar(W4[:, 1:3].rearrange("p i c d -> p (i c d)"), W4[:, 1:3].rearrange("p i c d -> p (i c d)"),
                                   WS, None, ALU.mult))
                lk(v.tensor_copy(WH[:, :, :, :].rearrange("p i c d -> p (i c d)"),
                                 W4[:, 1:3].rearrange("p i c d -> p (i c d)")))
                v.tensor_tensor(WL[:, :, :, :].rearrange("p i c d -> p (i c d)"), W4[:, 1:3].rearrange("p i c d -> p (i c d)"),
                                WH[:, :, :, :].rearrange("p i c d -> p (i c d)"), ALU.subtract).then_inc(self.w_split, 1)
                if self.L == 0:
                    v.tensor_scalar(bkw[:, :], col("bk0", 0, DC), WS, None, ALU.mult).then_inc(sem("bkw"), 1)
                    v.wait_ge(sem("bkw"), 1)
                tr_dve(v, self.tr_k, XT)

                def q_full(g):
                    v.wait_ge(self.q_ps, g + 1)
                    if self.L == 0:
                        ins = v.tensor_scalar(Q32[:, g % 2, :], PS[:, g % 4, :], col("bq0", g), HD ** -0.5, ALU.add, ALU.mult)
                    else:
                        ins = v.tensor_scalar(Q32[:, g % 2, :], PS[:, g % 4, :], HD ** -0.5, None, ALU.mult)
                    ins.then_inc(self.q_out, 1)

                def q_spread(g):
                    v.wait_ge(self.q_high, g + 1)
                    for quad in (1, 3):
                        part = QH[32 * quad:32 * quad + 32, g % 2, :]
                        ins = v.tensor_tensor(part, Q32[32 * quad:32 * quad + 32, g % 2, :], part, ALU.subtract)
                    lk(ins)
                    for s in range(2):
                        ins = v.tensor_scalar(QS[:, :, g, s * T:(s + 1) * T],
                                              QH[:, g % 2, :].rearrange("p (b q) -> p b q", b=B), parity[:, s:s + 1], None,
                                              ALU.mult)
                    ins.then_inc(self.qs, 1)

                for g in range(PAIRS):
                    q_full(g)
                    if g:
                        q_spread(g - 1)
                q_spread(PAIRS - 1)
                for u in range(K_UNITS):
                    self.k_low(v, 0, u, 5 + u % 3)
                for n in range(V_UNITS):
                    self.v_evac(v, 0, 0, n, 5 + (n + K_UNITS) % 3)
                self.dve_batch(v, 0, 0, True)
                with v.Fori(0, 3) as i:
                    for p in range(2):
                        self.dve_batch(v, 2 * i + 1 + p, 1 - p, True)
                self.dve_batch(v, 7, 1, False)
                self.recip(v, 7, 1)
                self.gather(v, 7, 1)
                v.wait_ge(self.gather_step, 80)
                v.engine_nop().then_inc(self.done, 1)
                lk(v.tensor_tensor(X[:, :, :], X[:, :, :], bc(row("bo0" if self.L == 0 else "bo3").unsqueeze(1),
                                                              [P, RT, D]), ALU.add))
                for t in range(RT):
                    v.wait_ge(self.o_ps, (t // 2 + 1) * 2)
                    ins = v.tensor_tensor(X[:, t, :], X[:, t, :], pst((0, 1), t), ALU.add)
                lk(ins)

            def k_high_half(self, a, b, n, bank=6):
                a.wait_ge(self.unit_ps, self.unit_no(b, "k", n))
                if n in (0, 4) and not (isinstance(b, int) and b == 0):
                    a.wait_ge(self.ks[n // 4], SPREAD * b)
                m, (k0, w) = n // 4, KEY_BLOCKS[n % 4]
                a.activation(KHL[:, 0, m, k0:k0 + w], PS[:, bank, 0:w], ACT.Identity,
                             bias=bkw[:, m:m + 1] if self.L == 0 else 0.0).then_inc(self.k_high, 1)

            def turn_evac(self, a, b, g):
                for k in range(4):
                    a.wait_ge(self.turn_ps, 32 * b + 4 * g + k + 1)
                    if k < 3:
                        ins = a.activation(PT[:, 4 * k:4 * k + 4, g % 4, :],
                                           PS[:, 4 + k % 2, :].rearrange("p (k q) -> p k q", k=4), ACT.Copy)
                    else:
                        ins = a.activation(PT[0:S_LAST, KT_N - 1, g % 4, :], PS[0:S_LAST, 4 + k % 2, 0:P], ACT.Copy)
                    ins.then_inc(self.turn_out, 1)

            def exp_row(self, a, b, g):
                a.wait_ge(self.nmax, 8 * b + g + 1)
                a.activation(SC[:, g % 2, :], SC[:, g % 2, :], ACT.Exp, bias=nmax[:, g:g + 1], scale=1 / WS,
                             accum_out=rsum[:, g:g + 1]).then_inc(self.exp, 1)

            def act_batch(self, a, b, p, project):
                for g in range(PAIRS):
                    if project:
                        self.k_high_half(a, b + 1, g)
                    if g:
                        self.turn_evac(a, b, g - 1)
                    elif not isinstance(b, int) or b:
                        self.turn_evac(a, b - 1, PAIRS - 1)
                    self.exp_row(a, b, g)

            def act_main(self, a):
                ln_act(a, self.ln_k)
                tr_act(a, self.tr_k, XT)
                for g in range(PAIRS):
                    a.wait_ge(self.q_out, g + 1)
                    if g >= 2:
                        a.wait_ge(self.qs, g - 1)
                    a.activation(QH[:, g % 2, :], Q32[:, g % 2, :], ACT.Copy).then_inc(self.q_high, 1)
                if self.L == 0:
                    a.wait_ge(sem("bkw"), 1)
                for u in range(K_UNITS):
                    self.k_high_half(a, 0, u, 5 + u % 3)
                self.act_batch(a, 0, 0, True)
                with a.Fori(0, 3) as i:
                    for p in range(2):
                        self.act_batch(a, 2 * i + 1 + p, 1 - p, True)
                self.act_batch(a, 7, 1, False)
                self.turn_evac(a, 7, PAIRS - 1)

        cross0 = Cross(0, 0, 0)
        cross1 = Cross(1, 7, 5)

        PATT = dict(
            q=dict(i=0, src=XT, k=PK[:, 0], v=PV[:, 0], nch=2, a=PA[:, :, 0:D], at=PAT[:, 0:2], C=0),
            k=dict(i=1, src=XT, k=PK[:, 1], v=PV[:, 1], nch=2, a=PA[:, :, D:2 * D], at=PAT[:, 2:4], C=2),
            v=dict(i=2, src=XT, k=PK[:, 2], v=PV[:, 2], nch=2, a=PA[:, :, 2 * D:3 * D], at=PAT[:, 4:6], C=4),
            p=dict(i=3, src=OT, k=PK[:, 3], v=PV[:, 3], nch=2, a=PA[:, :, 3 * D:4 * D], at=PAT[:, 6:8], C=6),
            f=dict(i=4, src=XT, k=FKs, v=FVs, nch=FC, a=PA, at=PAT, C=8))
        PSCALE = D ** -0.5

        def patt_scores(pe, p):
            for t in range(RT):
                n = RT * p["i"] + t
                if n >= 2:
                    pe.wait_ge(sem("p_exp"), n - 1)
                for blk in range(0, p["nch"] * P, BANK):
                    w = min(BANK, p["nch"] * P - blk)
                    for c in range(DC):
                        ins = pe.matmul(PS[:, 2 * (n % 2) + blk // BANK, 0:w], p["src"][:, c, t * P:(t + 1) * P],
                                        p["k"][:, c, blk:blk + w], start=(c == 0), stop=(c == DC - 1))
                ins.then_inc(sem("p_score"), 1)

        def patt_ps(p, n):
            return psf[:, 2 * BANK * (n % 2):2 * BANK * (n % 2) + p["nch"] * P]

        def patt_softmax_dve(v, p):
            def norm(n):
                v.wait_ge(sem("p_exp"), n + 1)
                lk(v.reciprocal(psm[:, n:n + 1], psm[:, n:n + 1]))
                a = p["a"][:, n % RT, :]
                v.tensor_scalar(a, a, psm[:, n:n + 1], None, ALU.mult).then_inc(sem("p_norm"), 1)

            for t in range(RT):
                n = RT * p["i"] + t
                v.wait_ge(sem("p_score"), n + 1)
                lk(v.tensor_reduce(pmax[:, n:n + 1], patt_ps(p, n), AX.X, ALU.max))
                v.tensor_scalar(pmax[:, n:n + 1], pmax[:, n:n + 1], -PSCALE, None, ALU.mult).then_inc(sem("p_nmax"), 1)
                if t:
                    norm(n - 1)
            norm(RT * p["i"] + RT - 1)

        def patt_exp(a, p):
            for t in range(RT):
                n = RT * p["i"] + t
                a.wait_ge(sem("p_nmax"), n + 1)
                a.activation(p["a"][:, t, :], patt_ps(p, n), ACT.Exp, bias=pmax[:, n:n + 1], scale=PSCALE,
                             accum_out=psm[:, n:n + 1]).then_inc(sem("p_exp"), 1)

        def patt_turn(pe, p):
            pe.wait_ge(sem("p_norm"), RT * (p["i"] + 1))
            for ch in range(p["nch"]):
                C = p["C"] + ch
                if C >= 2:
                    pe.wait_ge(sem("p_at_v" if C % 2 == 0 else "p_at_a"), C // 2)
                for t in range(RT):
                    ins = pe.transpose(PS[:, 4 + C % 2, t * P:(t + 1) * P], p["a"][:, t, ch * P:(ch + 1) * P],
                                       ident[:, :])
                ins.then_inc(sem("p_turn"), 1)

        def patt_turn_v(v, p):
            for ch in range(0, p["nch"], 2):
                v.wait_ge(sem("p_turn"), p["C"] + ch + 1)
                v.tensor_copy(p["at"][:, ch, :], PS[:, 4, :]).then_inc(sem("p_at_v"), 1)

        def patt_turn_a(a, p):
            for ch in range(1, p["nch"], 2):
                a.wait_ge(sem("p_turn"), p["C"] + ch + 1)
                a.activation(p["at"][:, ch, :], PS[:, 5, :], ACT.Copy).then_inc(sem("p_at_a"), 1)

        def patt_out(pe, p, cols):
            chunks = (p["C"] + p["nch"]) // 2
            pe.wait_ge(sem("p_at_v"), chunks)
            pe.wait_ge(sem("p_at_a"), chunks)
            for half in range(2):
                if 1 <= p["i"] <= 2:
                    pe.wait_ge(sem("p_out_v" if half == 0 else "p_out_a"), p["i"])
                if cols:
                    for ch in range(p["nch"]):
                        ins = pe.matmul(PS[:, 6 + half, :], p["v"][:, ch, half * P:(half + 1) * P], p["at"][:, ch, :],
                                        start=(ch == 0), stop=(ch == p["nch"] - 1))
                else:
                    for t in range(2 * half, 2 * half + 2):
                        for ch in range(p["nch"]):
                            ins = pe.matmul(pst((6, 7), t), p["at"][:, ch, t * P:(t + 1) * P], p["v"][:, ch, :],
                                            start=(ch == 0), stop=(ch == p["nch"] - 1))
                ins.then_inc(sem("p_out"), 1)

        def latent_dve(v):
            ln_dve(v, 1, X, XN)
            ln_dve(v, 2, XN, HN)
            tr_dve(v, 1, XT)
            patt_softmax_dve(v, PATT["q"])
            patt_softmax_dve(v, PATT["k"])
            patt_turn_v(v, PATT["q"])
            patt_softmax_dve(v, PATT["v"])
            patt_turn_v(v, PATT["k"])
            v.wait_ge(sem("p_out"), 1)
            v.tensor_scalar(QT[:, 0, :], PS[:, 6, :], HD ** -0.5, None, ALU.mult).then_inc(sem("p_out_v"), 1)
            patt_turn_v(v, PATT["v"])
            v.wait_ge(sem("p_out"), 3)
            v.tensor_copy(KT2[:, 0, :], PS[:, 6, :]).then_inc(sem("p_out_v"), 1)
            v.wait_ge(sem("p_out"), 5)
            v.tensor_copy(V2[:, 0:2, :].rearrange("p t d -> p (t d)"), PS[:, 6, :]).then_inc(sem("p_out_v"), 1)

            def soft(t):
                u = t % 2
                if t >= 2:
                    v.wait_ge(sem("s_turn"), 2 * (t - 1))
                v.wait_ge(sem("s_score"), t + 1)
                ins = v.tensor_tensor(SP[:, u], psf[:, 2 * BANK * u:2 * BANK * (u + 1)].rearrange("p (g k) -> p g k", k=T),
                                      bc(causal[:, :].unsqueeze(1), [P, 2 * PAIRS, T]), ALU.add)
                lk(ins)
                lk(v.tensor_reduce(gmax[:, :], SP[:, u], AX.X, ALU.max))
                v.tensor_tensor(SP[:, u], SP[:, u], bc(gmax[:, :].unsqueeze(2), [P, 2 * PAIRS, T]), ALU.subtract)\
                    .then_inc(sem("s_sub"), 1)

            def norm(t):
                u = t % 2
                v.wait_ge(sem("s_exp"), t + 1)
                lk(v.tensor_reduce(gsum[:, :], SP[:, u], AX.X, ALU.add))
                lk(v.reciprocal(gsum[:, :], gsum[:, :]))
                v.tensor_tensor(SP[:, u], SP[:, u], bc(gsum[:, :].unsqueeze(2), [P, 2 * PAIRS, T]), ALU.mult)\
                    .then_inc(sem("s_norm"), 1)

            def gather(t):
                v.wait_ge(sem("s_turn"), 2 * t + 1)
                v.tensor_copy(SPT[:, t % 2, 0:4].rearrange("p g q -> p (g q)"), PS[:, 4, :]).then_inc(sem("s_out_v"), 1)
                v.wait_ge(sem("s_pv"), t + 1)
                o = PS[:, 6:8, 0:D].rearrange("p b (c s q) -> p b c s q", c=DC, s=2)
                lk(v.tensor_scalar(otm[:, :, :].rearrange("p (b c) q -> p b c q", b=2), o[:, :, :, 0], parity[:, 0:1],
                                   None, ALU.mult))
                for bb in range(2):
                    b = 2 * t + bb
                    ins = v.scalar_tensor_tensor(OT[:, :, b * T:(b + 1) * T], o[:, bb, :, 1], parity[:, 1:2],
                                                 otm[:, 2 * bb:2 * bb + 2, :], ALU.mult, ALU.add)
                ins.then_inc(sem("s_o"), 1)

            for t in range(RT):
                soft(t)
                if t:
                    gather(t - 1)
                norm(t)
            gather(RT - 1)
            patt_softmax_dve(v, PATT["p"])
            patt_turn_v(v, PATT["p"])
            v.wait_ge(sem("p_out"), 8)
            for t in range(RT):
                ins = v.tensor_tensor(X1[:, t, :], pst((6, 7), t), XN[:, t, :], ALU.add)
            lk(ins)
            ln_dve(v, 3, X1, HN)
            tr_dve(v, 2, XT)
            patt_softmax_dve(v, PATT["f"])
            patt_turn_v(v, PATT["f"])
            lk(v.tensor_tensor(X[:, :, :], X[:, :, :], X1[:, :, :], ALU.add))
            for t in range(RT):
                v.wait_ge(sem("p_out"), 9 + t // 2)
                ins = v.tensor_tensor(X[:, t, :], X[:, t, :], pst((6, 7), t), ALU.add)
            lk(ins)

        def latent_act(a):
            ln_act(a, 1)
            ln_act(a, 2)
            tr_act(a, 1, XT)
            patt_exp(a, PATT["q"])
            patt_exp(a, PATT["k"])
            patt_turn_a(a, PATT["q"])
            patt_exp(a, PATT["v"])
            patt_turn_a(a, PATT["k"])
            a.wait_ge(sem("p_out"), 2)
            a.activation(QT[:, 1, :], PS[:, 7, :], ACT.Copy, scale=HD ** -0.5).then_inc(sem("p_out_a"), 1)
            patt_turn_a(a, PATT["v"])
            a.wait_ge(sem("p_out"), 4)
            a.activation(KT2[:, 1, :], PS[:, 7, :], ACT.Copy).then_inc(sem("p_out_a"), 1)
            a.wait_ge(sem("p_out"), 6)
            a.activation(V2[:, 2:4, :].rearrange("p t d -> p (t d)"), PS[:, 7, :], ACT.Copy).then_inc(sem("p_out_a"), 1)

            def turned(t):
                a.wait_ge(sem("s_turn"), 2 * t + 2)
                a.activation(SPT[:, t % 2, 4:8].rearrange("p g q -> p (g q)"), PS[:, 5, :], ACT.Copy)\
                    .then_inc(sem("s_out_a"), 1)

            for t in range(RT):
                a.wait_ge(sem("s_sub"), t + 1)
                a.activation(SP[:, t % 2], SP[:, t % 2], ACT.Exp).then_inc(sem("s_exp"), 1)
                if t:
                    turned(t - 1)
            turned(RT - 1)
            patt_exp(a, PATT["p"])
            patt_turn_a(a, PATT["p"])
            ln_act(a, 3)
            tr_act(a, 2, XT)
            patt_exp(a, PATT["f"])
            patt_turn_a(a, PATT["f"])

        def latent_pool(g):
            g.wait_ge(sem("p_out_v"), 1)
            g.wait_ge(sem("p_out_a"), 1)
            for b in range(B):
                if b >= 2:
                    g.wait_ge(sem("s_score"), b // 2)
                for c in range(DC):
                    g.tensor_tensor(QB[:, b % 2, c, :, :], bc(QT[:, c, b * T:(b + 1) * T].unsqueeze(1), [P, HPC, T]),
                                    bc(headmask[:, :].unsqueeze(2), [P, HPC, T]), ALU.mult).then_inc(sem("s_qb"), 1)

        def latent_pe(pe):
            tr_pe(pe, 1, HN, sem("ln_out"), 3)
            tr_done(pe, 1)
            pe.wait_ge(sem("w_patt"), 128)
            q, k, w, p, f = (PATT[n] for n in "qkvpf")
            patt_scores(pe, q)
            patt_scores(pe, k)
            patt_turn(pe, q)
            patt_scores(pe, w)
            patt_turn(pe, k)
            patt_out(pe, q, True)
            patt_turn(pe, w)
            patt_out(pe, k, True)
            patt_out(pe, w, False)

            def scores(t):
                if t == 0:
                    pe.wait_ge(sem("p_out_v"), 2)
                    pe.wait_ge(sem("p_out_a"), 2)
                    pe.wait_ge(sem("p_exp"), 12)
                if t >= 2:
                    pe.wait_ge(sem("s_sub"), t - 1)
                pe.wait_ge(sem("s_qb"), 4 * (t + 1))
                for g in range(PAIRS):
                    c, j = g // 4, g % 4
                    for bb in range(2):
                        b = 2 * t + bb
                        a0 = 2 * BANK * (t % 2) + g * P + bb * T
                        ins = pe.matmul(psf[:, a0:a0 + T], QB[:, bb, c, 2 * j:2 * j + 2, :].rearrange("p h q -> p (h q)"),
                                        KT2[:, c, b * T:(b + 1) * T], start=True, stop=True)
                ins.then_inc(sem("s_score"), 1)

            def turn(t):
                pe.wait_ge(sem("s_norm"), t + 1)
                for half in range(2):
                    if t:
                        pe.wait_ge(sem("s_out_v" if half == 0 else "s_out_a"), t)
                    for g in range(4 * half, 4 * half + 4):
                        ins = pe.transpose(PS[:, 4 + half, (g % 4) * P:(g % 4 + 1) * P],
                                           SP[:, t % 2, 2 * g:2 * g + 2, :].rearrange("p b k -> p (b k)"), ident[:, :])
                    ins.then_inc(sem("s_turn"), 1)

            def pv(t):
                if t == 0:
                    pe.wait_ge(sem("p_out_v"), 3)
                    pe.wait_ge(sem("p_out_a"), 3)
                pe.wait_ge(sem("s_out_v"), t + 1)
                pe.wait_ge(sem("s_out_a"), t + 1)
                if t:
                    pe.wait_ge(sem("s_o"), t)
                for bb in range(2):
                    for c in range(DC):
                        for j in range(4):
                            g = 4 * c + j
                            ins = pe.matmul(PS[32 * j:32 * j + 32, 6 + bb, c * P:(c + 1) * P],
                                            V2[T * bb:T * bb + T, t, 32 * g:32 * g + 32],
                                            SPT[T * bb:T * bb + T, t % 2, g, :], start=True, stop=True)
                ins.then_inc(sem("s_pv"), 1)

            scores(0)
            for t in range(RT):
                if t + 1 < RT:
                    scores(t + 1)
                turn(t)
                pv(t)
            pe.wait_ge(sem("s_o"), RT)
            patt_scores(pe, p)
            patt_turn(pe, p)
            patt_out(pe, p, False)
            tr_pe(pe, 2, HN, sem("ln_out"), 4)
            tr_done(pe, 2)
            pe.wait_ge(sem("w_ff"), 32)
            patt_scores(pe, f)
            patt_turn(pe, f)
            patt_out(pe, f, False)

        def top2(v):
            for t in range(RT):
                pj = bc(PROB[:, t, :].unsqueeze(1), [P, NE, NE])
                pe_ = bc(PROB[:, t, :].unsqueeze(2), [P, NE, NE])
                v.tensor_tensor(GA[:, t], pj, pe_, ALU.is_gt)
                ins = v.tensor_tensor(GB[:, t], pj, pe_, ALU.is_equal)
            lk(ins)
            lk(v.tensor_tensor(GB[:, :, :, :].rearrange("p t e j -> p t (e j)"),
                               GB[:, :, :, :].rearrange("p t e j -> p t (e j)"),
                               bc(lower8[:, :, :].rearrange("p e j -> p (e j)").unsqueeze(1), [P, RT, NE * NE]), ALU.mult))
            lk(v.tensor_tensor(GA[:, :, :, :].rearrange("p t e j -> p (t e j)"),
                               GA[:, :, :, :].rearrange("p t e j -> p (t e j)"),
                               GB[:, :, :, :].rearrange("p t e j -> p (t e j)"), ALU.add))
            lk(v.tensor_reduce(SEL[:, :, :], GA[:, :, :, :], AX.X, ALU.add))
            lk(v.tensor_scalar(SEL[:, :, :], SEL[:, :, :], 1.5, None, ALU.is_lt))

        def gate_pe(pe, L, tr_k, w):
            for t in range(RT):
                for c in range(DC):
                    ins = pe.matmul(PS[:, 0, t * NE:(t + 1) * NE], XT[:, c, t * P:(t + 1) * P], w[:, c, :],
                                    start=(c == 0), stop=(c == DC - 1))
            ins.then_inc(sem(f"g{L}_logit"), 1)

        class Experts:
            def __init__(self, L, w1, w2, act, bias):
                self.L, self.w1, self.w2, self.act, self.bias = L, w1, w2, act, bias
                e = f"e{L}_"
                self.s_w0, self.s_w1 = sem(e + "w0"), sem(e + "w1")
                self.s_h_ps, self.s_h_act = sem(e + "h_ps"), sem(e + "h_act")
                self.s_y_ps, self.s_y_out = sem(e + "y_ps"), sem(e + "y_out")
                self.s_b1 = sem(e + "b1")

            def load(self, sp, e, p):
                s = self.s_w1 if p else self.s_w0
                sp.dma_start(W1[p], self.w1[e].rearrange("(c p) f -> p c f", p=P)).then_inc(s, 16)
                sp.dma_start(W2[p], self.w2[e].rearrange("(f p) d -> p f d", p=P)).then_inc(s, 16)

            def sp_main(self, sp):
                with sp.Fori(0, 3) as i:
                    for p in range(2):
                        sp.wait_ge(self.s_y_ps, RT * (2 * i + p + 1))
                        self.load(sp, 2 * i + 2 + p, p)
                for s in (self.s_w0, self.s_w1):
                    sp.wait_ge(s, 128)

            def pe_main(self, pe):
                with pe.Fori(0, NE // 2) as i:
                    for p in range(2):
                        e = 2 * i + p
                        pe.wait_ge(self.s_w1 if p else self.s_w0, 32 * i + 32)
                        for f in range(FC):
                            if f >= 4:
                                pe.wait_ge(self.s_h_act, FC * e + f - 3)
                            for c in range(DC):
                                ins = pe.matmul(PS[:, f % 4, :], W1[p][:, c, f * P:(f + 1) * P], XT[:, c, :],
                                                start=(c == 0), stop=(c == DC - 1))
                            ins.then_inc(self.s_h_ps, 1)
                        pe.wait_ge(self.s_y_out, RT * e + RT)
                        for f in range(FC):
                            pe.wait_ge(self.s_h_act, FC * e + f + 1)
                            for t in range(RT):
                                ins = pe.matmul(PS[:, 4 + t, 0:D], HT[:, f, t * P:(t + 1) * P], W2[p][:, f, :],
                                                start=(f == 0), stop=(f == FC - 1))
                                if f == FC - 1:
                                    ins.then_inc(self.s_y_ps, 1)

            def act_main(self, a):
                with a.Fori(0, NE // 2) as i:
                    for p in range(2):
                        e = 2 * i + p
                        if self.bias:
                            a.wait_ge(self.s_b1, e + 1)
                        for f in range(FC):
                            a.wait_ge(self.s_h_ps, FC * e + f + 1)
                            a.activation(HT[:, f, :], PS[:, f % 4, :], self.act,
                                         bias=b1cur[:, p, f:f + 1] if self.bias else 0.0).then_inc(self.s_h_act, 1)

            def dve_main(self, v):
                v.engine_nop().then_inc(self.s_y_out, RT)
                with v.Fori(0, NE // 2) as i:
                    for p in range(2):
                        e = 2 * i + p
                        if self.bias:
                            v.tensor_copy(b1cur[:, p, :], colv[:, bass.ds(COLS["b1"] + FC * e, FC)]).then_inc(self.s_b1, 1)
                        v.tensor_copy(wcur[:, p, 0:RT], GW[:, :, bass.ds(e, 1)].rearrange("p t o -> p (t o)"))\
                            .then_inc(sem("wcur"), 1)
                        v.wait_ge(sem("wcur"), NE * self.L + e + 1)
                        for t in range(RT):
                            v.wait_ge(self.s_y_ps, RT * e + t + 1)
                            v.scalar_tensor_tensor(ACC[:, t, :], PS[:, 4 + t, 0:D], wcur[:, p, t:t + 1], ACC[:, t, :],
                                                   ALU.mult, ALU.add).then_inc(self.s_y_out, 1)
                v.wait_ge(self.s_y_out, RT * (NE + 1))
                lk(v.tensor_tensor(X[:, :, :], X[:, :, :], ACC[:, :, :], ALU.add))

        experts0 = Experts(0, m0w1, m0w2, ACT.Gelu, False)
        experts1 = Experts(1, m1w1, m1w2, ACT.Gelu_apprx_tanh, True)

        def across_pe(pe):
            tr_pe(pe, 3, HN, sem("ln_out"), 6)
            tr_done(pe, 3)
            pe.wait_ge(sem("w_moe"), 48)
            for b in range(B):
                for hh in range(2):
                    for c in range(DC):
                        ins = pe.matmul(PS[T * hh:T * hh + T, b // 2, (b % 2) * D:(b % 2 + 1) * D],
                                        XT[:, c, b * T:(b + 1) * T], WQKV[:, c, hh * D:(hh + 1) * D],
                                        start=(c == 0), stop=(c == DC - 1))
                if b % 2:
                    ins.then_inc(sem("c_qkv"), 1)
            pe.wait_ge(sem("c_ao"), 1)
            for half in range(2):
                for b in range(4 * half, 4 * half + 4):
                    ins = pe.transpose(PS[:, 4 + half, (b % 4) * P:(b % 4 + 1) * P], AO[:, b, :], ident[:, :])
                ins.then_inc(sem("c_turn"), 1)
            pe.wait_ge(sem("c_ot"), 2)
            rows_mm(pe, OT, WPJ, sem("c_proj"))
            tr_pe(pe, 4, XN, sem("ln_out"), 7)
            tr_done(pe, 4)
            gate_pe(pe, 0, 4, WRT)
            pe.wait_ge(sem("g0_sel"), 1)
            for t in range(RT):
                for s in range(t + 1):
                    ins = pe.matmul(PS[:, 1, t * NE:(t + 1) * NE], (before if s == t else ones)[:, :], SEL[:, s, :],
                                    start=(s == 0), stop=(s == t))
            ins.then_inc(sem("g0_rank"), 1)
            pe.wait_ge(sem("g0_w"), 1)
            experts0.pe_main(pe)

        def across_act(a):
            ln_act(a, 4)
            ln_act(a, 5)
            tr_act(a, 3, XT)
            for i in (1, 3):
                a.wait_ge(sem("c_qkv"), i + 1)
                a.activation(QKV[:, 2 * i:2 * i + 2, :].rearrange("p b n -> p (b n)"), PS[:, i, :], ACT.Copy)\
                    .then_inc(sem("c_in_a"), 1)
            a.wait_ge(sem("c_sub"), 1)
            a.activation(SE[:, :, :, :, :].rearrange("p b r h k -> p (b r h k)"),
                         SE[:, :, :, :, :].rearrange("p b r h k -> p (b r h k)"), ACT.Exp, scale=HD ** -0.5)\
                .then_inc(sem("c_exp"), 1)
            a.wait_ge(sem("c_turn"), 2)
            a.activation(OT[:, :, 4 * T:8 * T].rearrange("p h (b t) -> p b h t", b=4),
                         PS[:, 5, :].rearrange("p (b h t) -> p b h t", b=4, h=2), ACT.Copy).then_inc(sem("c_ot"), 1)
            ln_act(a, 6)
            tr_act(a, 4, XT)
            a.wait_ge(sem("g0_sub"), 1)
            a.activation(PROB[:, :, :], PROB[:, :, :], ACT.Exp).then_inc(sem("g0_exp"), 1)
            experts0.act_main(a)

        def across_dve(v):
            ln_dve(v, 4, X, XN)
            ln_dve(v, 5, XN, HN, "ln1w", "ln1b")
            tr_dve(v, 3, XT)
            lk(v.memset(SE[:, :, :, :, :].rearrange("p b r h k -> p (b r h k)"), NEG))
            for i in (0, 2):
                v.wait_ge(sem("c_qkv"), i + 1)
                ins = v.tensor_copy(QKV[:, 2 * i:2 * i + 2, :].rearrange("p b n -> p (b n)"), PS[:, i, :])
            lk(ins)
            v.wait_ge(sem("c_in_a"), 2)
            for b in range(B):
                n = b + 1
                for r in range(2):
                    ins = v.tensor_tensor(PRD[:, r, 0:n * 64].rearrange("p (k h d) -> p k h d", k=n, h=4),
                                          bc(QKV[:, b, 0:P].rearrange("p (h r d) -> p h r d", h=4, r=2)[:, :, r, :]
                                             .unsqueeze(1), [P, n, 4, HD]),
                                          QKV[:, 0:n, P:P + 64].rearrange("p k (h d) -> p k h d", h=4), ALU.mult)
                lk(ins)
                for r in range(2):
                    ins = v.tensor_reduce(SE[:, b, r, :, 0:n].rearrange("p h k -> p k h"),
                                          PRD[:, r, 0:n * 64].rearrange("p (k h d) -> p k h d", k=n, h=4), AX.X, ALU.add)
                lk(ins)
            se = SE[:, :, :, :, :].rearrange("p b r h k -> p (b r h) k")
            lk(v.tensor_reduce(gm2[:, :], se, AX.X, ALU.max))
            v.tensor_tensor(se, se, bc(gm2[:, :].unsqueeze(2), [P, 64, B]), ALU.subtract).then_inc(sem("c_sub"), 1)
            v.wait_ge(sem("c_exp"), 1)
            lk(v.tensor_reduce(gs2[:, :], se, AX.X, ALU.add))
            lk(v.reciprocal(gs2[:, :], gs2[:, :]))
            lk(v.tensor_tensor(se, se, bc(gs2[:, :].unsqueeze(2), [P, 64, B]), ALU.mult))
            for b in range(B):
                n = b + 1
                for r in range(2):
                    ins = v.tensor_tensor(PRV[:, r, 0:n * 64].rearrange("p (h d k) -> p h d k", h=4, d=HD),
                                          bc(SE[:, b, r, :, 0:n].unsqueeze(2), [P, 4, HD, n]),
                                          QKV[:, 0:n, P + 64:D].rearrange("p k (h d) -> p h d k", h=4), ALU.mult)
                lk(ins)
                for r in range(2):
                    ins = v.tensor_reduce(AO[:, b, :].rearrange("p (h r d) -> p h r d", h=4, r=2)[:, :, r, :],
                                          PRV[:, r, 0:n * 64].rearrange("p (h d k) -> p h d k", h=4, d=HD), AX.X, ALU.add)
                lk(ins)
            v.engine_nop().then_inc(sem("c_ao"), 1)
            v.wait_ge(sem("c_turn"), 1)
            v.tensor_copy(OT[:, :, 0:4 * T].rearrange("p h (b t) -> p b h t", b=4),
                          PS[:, 4, :].rearrange("p (b h t) -> p b h t", b=4, h=2)).then_inc(sem("c_ot"), 1)
            for t in range(RT):
                v.wait_ge(sem("c_proj"), (t // 2 + 1) * 2)
                ins = v.tensor_tensor(ACC[:, t, :], pst((0, 1), t), XN[:, t, :], ALU.add)
            lk(ins)
            ln_dve(v, 6, ACC, XN, "ln2w", "ln2b")
            tr_dve(v, 4, XT)
            v.wait_ge(sem("g0_logit"), 1)
            lg = PS[:, 0, 0:RT * NE].rearrange("p (t e) -> p t e", t=RT)
            lk(v.tensor_reduce(gmx[:, :], lg, AX.X, ALU.max))
            v.tensor_tensor(PROB[:, :, :], lg, bc(gmx[:, :].unsqueeze(2), [P, RT, NE]), ALU.subtract)\
                .then_inc(sem("g0_sub"), 1)
            v.wait_ge(sem("g0_exp"), 1)
            lk(v.tensor_reduce(gsm[:, :], PROB[:, :, :], AX.X, ALU.add))
            lk(v.reciprocal(gsm[:, :], gsm[:, :]))
            lk(v.tensor_tensor(PROB[:, :, :], PROB[:, :, :], bc(gsm[:, :].unsqueeze(2), [P, RT, NE]), ALU.mult))
            top2(v)
            v.engine_nop().then_inc(sem("g0_sel"), 1)
            lk(v.tensor_tensor(GW[:, :, :], PROB[:, :, :], SEL[:, :, :], ALU.mult))
            lk(v.tensor_reduce(gsm[:, :], GW[:, :, :], AX.X, ALU.add))
            lk(v.reciprocal(gsm[:, :], gsm[:, :]))
            lk(v.tensor_tensor(GW[:, :, :], GW[:, :, :], bc(gsm[:, :].unsqueeze(2), [P, RT, NE]), ALU.mult))
            v.wait_ge(sem("g0_rank"), 1)
            lk(v.tensor_scalar(GX[:, :, :], PS[:, 1, 0:RT * NE].rearrange("p (t e) -> p t e", t=RT), CAP - 0.5, None,
                               ALU.is_lt))
            lk(v.tensor_tensor(GW[:, :, :], GW[:, :, :], GX[:, :, :], ALU.mult))
            v.engine_nop().then_inc(sem("g0_w"), 1)
            experts0.dve_main(v)

        WA = PK

        def single_pe(pe):
            tr_pe(pe, 6, XN, sem("ln_out"), 9)
            tr_done(pe, 6)
            pe.wait_ge(sem("w_a"), 64)
            cols_mm(pe, XT, WA[:, 0], sem("d_q"), banks=(0, 1))
            cols_mm(pe, XT, WA[:, 1], sem("d_q"), banks=(2, 3))
            rows_mm(pe, XT, WA[:, 2], sem("d_q"), banks=(4, 5))
            pe.wait_ge(sem("d_in"), 4)
            for t in range(RT):
                for c in range(DC):
                    ins = pe.matmul(PS[:, 0, t * P:(t + 1) * P], QT[:, c, t * P:(t + 1) * P],
                                    KT5[:, c, t * P:(t + 1) * P], start=(c == 0), stop=(c == DC - 1))
            ins.then_inc(sem("d_score"), 1)
            pe.wait_ge(sem("d_norm"), 1)
            for t in range(RT):
                ins = pe.transpose(PS[:, 1, t * P:(t + 1) * P], S5[:, t, :], ident[:, :])
            ins.then_inc(sem("d_turn"), 1)
            pe.wait_ge(sem("d_p"), 1)
            pe.wait_ge(sem("d_v"), 2)
            for m in range(DC):
                for t in range(RT):
                    ins = pe.matmul(PS[:, 2 + m, t * P:(t + 1) * P], V5[:, t, m * P:(m + 1) * P], S5T[:, t, :],
                                    start=True, stop=True)
                ins.then_inc(sem("d_pv"), 1)
            pe.wait_ge(sem("d_o"), 2)
            rows_mm(pe, OT, WA[:, 3], sem("d_out"), banks=(4, 5))

        def single_dve(v):
            ln_dve(v, 8, X, XN)
            tr_dve(v, 6, XT)
            for m in range(DC):
                v.wait_ge(sem("d_q"), m + 1)
                v.tensor_scalar(QT[:, m, :], PS[:, m, :], col("bq5", m), D ** -0.5, ALU.add, ALU.mult)\
                    .then_inc(sem("d_in"), 1)
            for m in range(DC):
                v.wait_ge(sem("d_q"), 3 + m)
                v.tensor_scalar(KT5[:, m, :], PS[:, 2 + m, :], col("bk5", m), None, ALU.add).then_inc(sem("d_in"), 1)
            v.wait_ge(sem("d_score"), 1)
            lk(v.tensor_tensor(S5[:, :, :], PS[:, 0, :].rearrange("p (t k) -> p t k", t=RT),
                               bc(causal2[:, :].unsqueeze(1), [P, RT, P]), ALU.add))
            lk(v.tensor_reduce(m5[:, :], S5[:, :, :], AX.X, ALU.max))
            v.tensor_tensor(S5[:, :, :], S5[:, :, :], bc(m5[:, :].unsqueeze(2), [P, RT, P]), ALU.subtract)\
                .then_inc(sem("d_sub"), 1)
            v.wait_ge(sem("d_exp"), 1)
            lk(v.tensor_reduce(s5[:, :], S5[:, :, :], AX.X, ALU.add))
            lk(v.reciprocal(s5[:, :], s5[:, :]))
            v.tensor_tensor(S5[:, :, :], S5[:, :, :], bc(s5[:, :].unsqueeze(2), [P, RT, P]), ALU.mult)\
                .then_inc(sem("d_norm"), 1)
            v.wait_ge(sem("d_turn"), 1)
            v.tensor_copy(S5T[:, :, :].rearrange("p t q -> p (t q)"), PS[:, 1, :]).then_inc(sem("d_p"), 1)
            for m in range(DC):
                v.wait_ge(sem("d_pv"), m + 1)
                v.tensor_scalar(OT[:, m, :], PS[:, 2 + m, :], col("bv5", m), None, ALU.add).then_inc(sem("d_o"), 1)
            lk(v.tensor_tensor(X[:, :, :], X[:, :, :], bc(row("bo5").unsqueeze(1), [P, RT, D]), ALU.add))
            for t in range(RT):
                v.wait_ge(sem("d_out"), (t // 2 + 1) * 2)
                ins = v.tensor_tensor(X[:, t, :], X[:, t, :], pst((4, 5), t), ALU.add)
            lk(ins)

        def single_act(a):
            ln_act(a, 8)
            tr_act(a, 6, XT)
            for i in range(2):
                a.wait_ge(sem("d_q"), 4 + 2 * (i + 1))
                a.activation(V5[:, 2 * i:2 * i + 2, :].rearrange("p t d -> p (t d)"), PS[:, 4 + i, :], ACT.Copy)\
                    .then_inc(sem("d_v"), 1)
            a.wait_ge(sem("d_sub"), 1)
            a.activation(S5[:, :, :], S5[:, :, :], ACT.Exp).then_inc(sem("d_exp"), 1)

        def moe_pe(pe):
            tr_pe(pe, 7, XN, sem("ln_out"), 10)
            tr_done(pe, 7)
            pe.wait_ge(sem("w_gate1"), 32)
            gate_pe(pe, 1, 7, WGT)
            pe.wait_ge(sem("g1_w"), 1)
            for t in range(RT):
                ins = pe.transpose(PS[0:NE, 1, t * P:(t + 1) * P], GW[:, t, :], ident[:, :])
            ins.then_inc(sem("g1_turn"), 1)
            pe.wait_ge(sem("g1_wT"), 1)
            for t in range(RT):
                ins = pe.matmul(pst((2, 3), t), wT[0:NE, t * P:(t + 1) * P], B2[0:NE, :], start=True, stop=True)
            ins.then_inc(sem("g1_b2"), 1)
            pe.wait_ge(sem("g1_acc"), 1)
            experts1.pe_main(pe)

        def moe_dve(v):
            ln_dve(v, 9, X, XN)
            tr_dve(v, 7, XT)
            v.wait_ge(sem("g1_exp"), 1)
            lk(v.tensor_scalar(PROB[:, :, :], PROB[:, :, :], 1.0, None, ALU.add))
            lk(v.reciprocal(PROB[:, :, :], PROB[:, :, :]))
            top2(v)
            lk(v.tensor_tensor(GW[:, :, :], PROB[:, :, :], SEL[:, :, :], ALU.mult))
            v.engine_nop().then_inc(sem("g1_w"), 1)
            v.wait_ge(sem("g1_turn"), 1)
            v.tensor_copy(wT[0:NE, :], PS[0:NE, 1, :]).then_inc(sem("g1_wT"), 1)
            v.wait_ge(sem("g1_b2"), 1)
            for i in range(2):
                ins = v.tensor_copy(ACC[:, 2 * i:2 * i + 2, :].rearrange("p t d -> p (t d)"), PS[:, 2 + i, :])
            lk(ins)
            v.engine_nop().then_inc(sem("g1_acc"), 1)
            experts1.dve_main(v)

        def moe_act(a):
            ln_act(a, 9)
            tr_act(a, 7, XT)
            a.wait_ge(sem("g1_logit"), 1)
            a.activation(PROB[:, :, :], PS[:, 0, 0:RT * NE].rearrange("p (t e) -> p t e", t=RT), ACT.Exp, scale=-1.0)\
                .then_inc(sem("g1_exp"), 1)
            experts1.act_main(a)

        block = ctx.enter_context(nc.Block())

        def w_load(eng, dst, src, s):
            eng.dma_start(dst, src.rearrange("(c p) n -> p c n", p=P)).then_inc(s, 16)

        @block.sync
        def _(sp):
            sp.dma_start(X[:, :, :], x.rearrange("(t p) d -> p t d", p=P)).then_inc(sem("x_in"), 16)
            for i in range(4):
                w_load(sp, W4[:, i], xw0[i], sem("w_x0"))
            sp.dma_start(colv[:, :], cols).then_inc(sem("vec_in"), 16)
            sp.dma_start(rows_b[:, :, :], bc(rowv.unsqueeze(0), [P, len(ROWV), D])).then_inc(sem("vec_in"), 16)
            cross0.sp_first(sp)
            cross0.sp_main(sp)
            sp.wait_ge(cross0.split, B)
            sp.wait_ge(cross0.unit_ps, UNITS * 7)
            for i in range(4):
                w_load(sp, PK[:, i], patt_k[i], sem("w_patt"))
                w_load(sp, PV[:, i], patt_v[i], sem("w_patt"))
            sp.wait_ge(cross0.o_ps, RT)
            w_load(sp, FKs, fk, sem("w_ff"))
            w_load(sp, FVs, fv, sem("w_ff"))
            w_load(sp, WQKV, wqkv, sem("w_moe"))
            w_load(sp, WPJ, wproj, sem("w_moe"))
            w_load(sp, WRT, wrt, sem("w_moe"))
            experts0.load(sp, 0, 0)
            for i in range(4):
                w_load(sp, W4[:, i], xw1[i], sem("w_x1"))
            sp.wait_ge(sem("p_out"), 10)
            experts0.load(sp, 1, 1)
            experts0.sp_main(sp)
            sp.wait_ge(sem("experts0_done"), 1)
            cross1.sp_first(sp)
            cross1.sp_main(sp)
            sp.wait_ge(cross1.split, B)
            sp.wait_ge(cross1.unit_ps, UNITS * 7)
            for i in range(4):
                w_load(sp, WA[:, i], aw[i], sem("w_a"))
            sp.wait_ge(cross1.o_ps, RT)
            w_load(sp, WGT, wg, sem("w_gate1"))
            sp.dma_start(B2[0:NE, :], b2).then_inc(sem("w_gate1"), 16)
            for e in range(2):
                experts1.load(sp, e, e)
            experts1.sp_main(sp)
            sp.wait_ge(sem("x_final"), 1)
            sp.dma_start(out.rearrange("(t p) d -> p t d", p=P), X[:, :, :]).then_inc(sem("stored"), 16)
            sp.wait_ge(sem("stored"), 16)

        @block.gpsimd
        def _(g):
            plk(g.memset(ident[:, :], 0.0))
            plk(g.memset(ones[:, :], 1.0))
            plk(g.memset(before[:, :], 1.0))
            plk(g.memset(headmask[:, :], 1.0))
            plk(g.memset(causal[:, :], 0.0))
            plk(g.memset(causal2[:, :], 0.0))
            plk(g.memset(lower8[:, :, :], 1.0))
            plk(g.memset(eps_c[:, :], EPS))
            plk(g.affine_select(out=ident[:, :], in_=ident[:, :], compare_op=ALU.not_equal, fill=1.0, base=0,
                            pattern=[[-1, P]], channel_multiplier=1))
            plk(g.affine_select(out=before[:, :], in_=before[:, :], compare_op=ALU.is_gt, fill=0.0, base=0,
                            pattern=[[1, P]], channel_multiplier=-1))
            plk(g.affine_select(out=headmask[:, :], in_=headmask[:, :], compare_op=ALU.is_ge, fill=0.0, base=0,
                                pattern=[[-HD, HPC]], channel_multiplier=1))
            plk(g.affine_select(out=headmask[:, :], in_=headmask[:, :], compare_op=ALU.is_ge, fill=0.0, base=HD - 1,
                            pattern=[[HD, HPC]], channel_multiplier=-1))
            for i in range(2):
                plk(g.affine_select(out=causal[T * i:T * i + T, :], in_=causal[T * i:T * i + T, :], compare_op=ALU.is_ge,
                                fill=NEG, base=0, pattern=[[-1, T]], channel_multiplier=1))
            plk(g.affine_select(out=lower8[:, :, :], in_=lower8[:, :, :], compare_op=ALU.is_gt, fill=0.0, base=0,
                            pattern=[[1, NE], [-1, NE]], channel_multiplier=0))
            plk(g.affine_select(out=causal2[:, :], in_=causal2[:, :], compare_op=ALU.is_ge, fill=NEG, base=0,
                                pattern=[[-1, P]], channel_multiplier=1))
            plk(g.memset(causal2[T:P, 0:T], NEG))
            g.engine_nop().then_inc(sem("consts"), 1)
            cross0.pool_main(g)
            latent_pool(g)
            cross1.pool_main(g)

        @block.tensor
        def _(pe):
            pe.wait_ge(sem("consts"), 1)
            cross0.pe_main(pe)
            latent_pe(pe)
            across_pe(pe)
            cross1.pe_main(pe)
            single_pe(pe)
            moe_pe(pe)

        @block.vector
        def _(v):
            v.wait_ge(sem("consts"), 1)
            lk(v.tensor_reduce(parity[:, :], headmask[:, :].rearrange("p (a b) -> p b a", b=2), AX.X, ALU.add))
            v.wait_ge(sem("vec_in"), 32)
            v.wait_ge(sem("x_in"), 16)
            cross0.dve_main(v)
            latent_dve(v)
            across_dve(v)
            v.engine_nop().then_inc(sem("experts0_done"), 1)
            cross1.dve_main(v)
            single_dve(v)
            moe_dve(v)
            v.engine_nop().then_inc(sem("x_final"), 1)

        @block.scalar
        def _(a):
            a.wait_ge(sem("consts"), 1)
            cross0.act_main(a)
            latent_act(a)
            across_act(a)
            cross1.act_main(a)
            single_act(a)
            moe_act(a)


NAMES = ["x", "ctxT", "mask", "cols", "rowv", "xw0", "patt_k", "patt_v", "fk", "fv", "wqkv", "wproj", "wrt", "m0w1",
         "m0w2", "xw1", "aw", "wg", "m1w1", "m1w2", "b2"]


def layout(inputs):
    import numpy as np
    """What kernel() gives the program: every input in its own type, only laid out."""
    np_ = {k: np.asarray(v) for k, v in inputs.items()}
    t = lambda n: np_[n].T
    colm = lambda v: v.reshape(-1, 128).T
    bq = np.tile(np_["L0_xattn_bq"].reshape(8, 32).T, (4, 1))
    cols = np.concatenate([bq] + [colm(np_[n]) for n in ("L0_xattn_bk", "L0_xattn_bv", "L1_attn_bq", "L1_attn_bk", "L1_attn_bv", "L1_ffn_b1")], axis=1)
    rowv = np.stack([np_[n] for n in ("L0_xattn_bo", "L0_ffn_ln1_weight", "L0_ffn_ln1_bias", "L0_ffn_ln2_weight", "L0_ffn_ln2_bias", "L1_xattn_bo", "L1_attn_bo")])
    w = np_["L0_ffn_qkv_weight"].reshape(2, 4, 64, 256)
    wqkv = np.concatenate([w[:, :, 0:32].reshape(2, 128, 256), w[:, :, 32:48].reshape(2, 64, 256), w[:, :, 48:64].reshape(2, 64, 256)], axis=1).reshape(512, 256).T
    return [np.ascontiguousarray(a) for a in (
        np_["x"].reshape(512, 256), np_["ctx_1024"].transpose(0, 2, 1), np_["mask_Bx1x1xS2_ff0"].reshape(8, 1601), cols, rowv,
        np.stack([np_["L0_xattn_" + n] for n in ("wq", "wk", "wv", "wo")]),
        np.stack([t("L0_attn_" + n) for n in ("qK", "kK", "vK", "pK")]), np.stack([np_["L0_attn_" + n] for n in ("qV", "kV", "vV", "pV")]),
        t("L0_attn_fK"), np_["L0_attn_fV"], wqkv, t("L0_ffn_proj_weight"), np_["L0_ffn_router_weight"],
        np_["L0_ffn_moe_w1"], np_["L0_ffn_moe_w2"],
        np.stack([t("L1_xattn_" + n) for n in ("Wq", "Wk", "Wv", "Wo")]),
        np.stack([np_["L1_attn_" + n] for n in ("Wq", "Wk", "Wv", "Wo")]),
        np_["L1_ffn_Wg"], np_["L1_ffn_W1"], np_["L1_ffn_W2"], np_["L1_ffn_b2"])]


def kernel(**inputs):
    import numpy as np
    import concourse.bacc as bacc
    from concourse.bass_utils import run_bass_kernel_spmd

    nc = bacc.Bacc("TRN2", target_bir_lowering=False, num_devices=1)
    arrays, args = {}, []
    for name, a in zip(NAMES, layout(inputs)):
        arrays[f"in_{name}"] = a
        args.append(nc.dram_tensor(f"in_{name}", a.shape, mybir.dt.from_np(a.dtype), kind="ExternalInput").ap())
    args.append(nc.dram_tensor("out", (ROWS, D), F32, kind="ExternalOutput").ap())
    perceiver(nc, *args)
    r = run_bass_kernel_spmd(nc, [arrays], core_ids=[0])
    return r.results[0]["out"].reshape(B, T, D)
```

```python
from contextlib import ExitStack

import concourse.bass as bass
from concourse import mybir

F32 = mybir.dt.float32
F16 = mybir.dt.float16
ALU = mybir.AluOpType
ACT = mybir.ActivationFunctionType
AX = mybir.AxisListType

P = 128
B, T, D = 8, 64, 256
ROWS = B * T
RT = ROWS // P
DC = D // P
H, HD = 16, 16
PAIRS = H // 2
HPC = P // HD
S = 1601
KT_N = (S + P - 1) // P
S_LAST = S - (KT_N - 1) * P
HALF_A = 1024
BANK = 512
NE, FF = 8, 1024
FC = FF // P
CAP = 160
EPS = 1e-5
NEG = -1e30
K_UNITS = 8
V_UNITS = (KT_N + 1) // 2
UNITS = K_UNITS + V_UNITS
WS = 16.0
SPREAD = 16 * 16
KEY_BLOCKS = [(0, 512), (512, 512), (1024, 512), (1536, S - 1536)]

K_BLOCKS = [(k0, min(-(-S // 4), S - k0)) for k0 in range(0, S, -(-S // 4))]

COLS = {"bq0": 0, "bk0": 2, "bv0": 4, "bq5": 6, "bk5": 8, "bv5": 10, "b1": 12}
N_COLS = 12 + NE * FC
ROWV = ["bo0", "ln1w", "ln1b", "ln2w", "ln2b", "bo3", "bo5"]


def perceiver(nc, x, ctxT, mask, cols, rowv, xw0, patt_k, patt_v, fk, fv, wqkv, wproj, wrt, m0w1, m0w2,
              xw1, aw, wg, m1w1, m1w2, b2, out):
    ctx = ExitStack()
    with ctx:
        def sb(name, shape, dt=F32):
            return ctx.enter_context(nc.sbuf_tensor(name, shape, dt))

        named = {}

        def sem(name):
            if name not in named:
                named[name] = ctx.enter_context(nc.semaphore(name))
            return named[name]

        PS = ctx.enter_context(nc.psum_tensor("PS", [P, 8, BANK], F32))
        psf = PS[:, :, :].rearrange("p a b -> p (a b)")

        X = sb("X", [P, RT, D])
        OT = sb("OT", [P, DC, ROWS])
        QS = sb("QS", [P, PAIRS, B, P], F16)
        rows_b = sb("rows_b", [P, len(ROWV), D])
        colv = sb("colv", [P, N_COLS])
        ident = sb("ident", [P, P])
        ones = sb("ones", [P, P])
        pick = sb("pick", [P, NE, P], F16)
        before = sb("before", [P, P])
        headmask = sb("headmask", [P, HPC])
        parity = sb("parity", [P, 2])
        causal = sb("causal", [P, T])
        causal2 = sb("causal2", [P, P])
        lower8 = sb("lower8", [P, NE, NE])
        eps_c = sb("eps_c", [P, 1])
        stats = sb("stats", [P, RT, 6])
        mv = sb("mv", [P, RT, 2])
        rstd = sb("rstd", [P, RT])
        mx = sb("mx", [P, PAIRS, 2])
        nmax = sb("nmax", [P, PAIRS])
        rsum = sb("rsum", [P, PAIRS])
        rinv = sb("rinv", [P, 4])
        rexp = sb("rexp", [P, 4, 32])
        rbc = sb("rbc", [P, P])
        osc = sb("osc", [P, P])
        otmp = sb("otmp", [P, T])
        W4 = sb("W4", [P, 4, DC, D])
        WH = sb("WH", [P, 2, DC, D], F16)
        WL = sb("WL", [P, 2, DC, D], F16)
        bkw = sb("bkw", [P, DC])

        ARENA = 39000
        arena = sb("arena", [P, ARENA])

        class Region:
            def __init__(self):
                self.at = 0

            def take(self, n):
                a = self.at
                self.at += (n + 7) // 8 * 8
                assert self.at <= ARENA, self.at
                return arena[:, a:a + n]

        r = Region()
        CR = r.take(DC * S).rearrange("p (c s) -> p c s", c=DC)
        CHL = [r.take(DC * S).bitcast(F16).rearrange("p (h c s) -> p h c s", h=2, c=DC) for _ in range(2)]
        KHL = r.take(DC * S).bitcast(F16).rearrange("p (h c s) -> p h c s", h=2, c=DC)
        KS = r.take(PAIRS * S // 2 + 4).bitcast(F16)[:, 0:PAIRS * S].rearrange("p (g s) -> p g s", g=PAIRS)
        VS = r.take(2 * KT_N * D).rearrange("p (b k d) -> p b k d", b=2, k=KT_N)
        SC = r.take(2 * S).rearrange("p (b s) -> p b s", b=2)
        MK = r.take(2 * S).rearrange("p (b s) -> p b s", b=2)
        PT_AT = r.at
        PT = r.take(KT_N * 4 * P).rearrange("p (k j q) -> p k j q", k=KT_N, j=4)
        r = Region()
        r.at = PT_AT
        Q32 = r.take(DC * ROWS).rearrange("p (c r) -> p c r", c=DC)
        QHL = r.take(DC * ROWS).bitcast(F16).rearrange("p (h c r) -> p h c r", h=2, c=DC)
        QM = r.take(DC * B * P).bitcast(F16).rearrange("p (h c b q) -> p h c b q", h=2, c=DC, b=B)
        Q_END = r.at
        r = Region()
        r.at = ARENA - 2 * RT * D - 16
        assert r.at >= Q_END
        XN = r.take(RT * D).rearrange("p (t d) -> p t d", t=RT)
        XT = r.take(DC * ROWS).rearrange("p (c r) -> p c r", c=DC)
        STAGE_END = ARENA - 2 * RT * D - 16
        r = Region()
        PK = r.take(4 * DC * D).rearrange("p (i c d) -> p i c d", i=4, c=DC)
        PV = r.take(4 * DC * D).rearrange("p (i c d) -> p i c d", i=4, c=DC)
        PARAMS_END = r.at
        r = Region()
        r.at = PARAMS_END
        QT = r.take(DC * ROWS).rearrange("p (c r) -> p c r", c=DC)
        HN = r.take(RT * D).rearrange("p (t d) -> p t d", t=RT)
        X1 = r.take(RT * D).rearrange("p (t d) -> p t d", t=RT)
        PA = r.take(RT * FF).rearrange("p (t n) -> p t n", t=RT)
        PAT = r.take(FC * ROWS).rearrange("p (c r) -> p c r", c=FC)
        KT2 = r.take(DC * ROWS).rearrange("p (c r) -> p c r", c=DC)
        V2 = r.take(RT * D).rearrange("p (t d) -> p t d", t=RT)
        SP = r.take(2 * PAIRS * P).rearrange("p (u g k) -> p u g k", u=2, g=2 * PAIRS)
        SPT = r.take(2 * PAIRS * P).rearrange("p (u g q) -> p u g q", u=2, g=PAIRS)
        gmax = r.take(16)
        gsum = r.take(16)
        QB = r.take(2 * DC * HPC * T).rearrange("p (u c h q) -> p u c h q", u=2, c=DC, h=HPC)
        FF_AT = r.at
        FKs = r.take(DC * FF).rearrange("p (c n) -> p c n", c=DC)
        FVs = r.take(FC * D).rearrange("p (n d) -> p n d", n=FC)
        pmax = r.take(20)
        psm = r.take(20)
        otm = r.take(4 * T).rearrange("p (a q) -> p a q", a=4)
        WQKV = r.take(DC * 2 * D).rearrange("p (c n) -> p c n", c=DC)
        WPJ = r.take(DC * D).rearrange("p (c n) -> p c n", c=DC)
        r2 = Region()
        r2.at = PARAMS_END + 3 * RT * D
        QKV = r2.take(B * D).rearrange("p (b n) -> p b n", b=B)
        SE = r2.take(B * 2 * 4 * B).rearrange("p (b r h k) -> p b r h k", b=B, r=2, h=4)
        AO = r2.take(B * P).rearrange("p (b n) -> p b n", b=B)
        PAST = [b * (b + 1) // 2 for b in range(B)]
        PRD = arena[:, 0:PAST[B - 1] * P + B * P]
        assert PAST[B - 1] * P + B * P <= PARAMS_END + DC * ROWS
        gm2 = r2.take(64)
        gs2 = r2.take(64)
        r3 = Region()
        r3.at = FF_AT
        W1 = [None, r3.take(DC * FF).rearrange("p (c f) -> p c f", c=DC)]
        W2 = [None, r3.take(FC * D).rearrange("p (f d) -> p f d", f=FC)]
        r3.at = r.at
        W1[0] = r3.take(DC * FF).rearrange("p (c f) -> p c f", c=DC)
        W2[0] = r3.take(FC * D).rearrange("p (f d) -> p f d", f=FC)
        PROB, SEL, GW, GX = (r3.take(RT * NE).rearrange("p (t e) -> p t e", t=RT) for _ in range(4))
        GA, GB = (r3.take(RT * NE * NE).rearrange("p (t e j) -> p t e j", t=RT, e=NE) for _ in range(2))
        gmx, gsm = (r3.take(RT) for _ in range(2))
        wcur = r3.take(2 * 8).rearrange("p (b t) -> p b t", b=2)
        b1cur = r3.take(2 * FC).rearrange("p (b f) -> p b f", b=2)
        WRT = r3.take(DC * NE).rearrange("p (c e) -> p c e", c=DC)
        WGT = r3.take(DC * NE).rearrange("p (c e) -> p c e", c=DC)
        B2 = r3.take(D)
        wT = r3.take(ROWS)
        assert r3.at <= STAGE_END, r3.at
        r3 = Region()
        r3.at = PARAMS_END + 3 * RT * D
        HT = r3.take(FC * ROWS).bitcast(F16).rearrange("p (h f r) -> p h f r", h=2, f=FC)
        ACC = r3.take(RT * D).rearrange("p (t d) -> p t d", t=RT)
        r3.at = max(r3.at, r2.at)
        r4 = Region()
        WSP = [reg.take(2 * DC * FF).bitcast(F16).rearrange("p (h n) -> p h n", h=2) for reg in (r3, r4)]
        assert r4.at <= PARAMS_END
        W1S = [w[:, :, 0:DC * FF].rearrange("p h (c f) -> p h c f", c=DC) for w in WSP]
        W2S = [w[:, :, DC * FF:2 * DC * FF].rearrange("p h (f d) -> p h f d", f=FC) for w in WSP]
        HF = r3.take(2 * ROWS).rearrange("p (u r) -> p u r", u=2)
        XS = r3.take(DC * ROWS).bitcast(F16).rearrange("p (h c r) -> p h c r", h=2, c=DC)
        OH = r3.take(RT * CAP // 2).bitcast(F16).rearrange("p (t s) -> p t s", t=RT)
        SCT = r3.take(ROWS).bitcast(F16).rearrange("p (i r) -> p i r", i=2)
        XE = r3.take(DC * CAP).bitcast(F16).rearrange("p (h c s) -> p h c s", h=2, c=DC)
        YS = r3.take(2 * D).bitcast(F16).rearrange("p (h i d) -> p h i d", h=2, i=2)
        XNS = r3.take(RT * D).bitcast(F16).rearrange("p (h t d) -> p h t d", h=2, t=RT)
        slots = r3.take(CAP)
        slot = r3.take(2)
        RK = r3.take(RT * NE).rearrange("p (t e) -> p t e", t=RT)
        RKT = r3.take(ROWS // 2).bitcast(F16)
        rkcur = r3.take(8)
        assert r3.at <= FF_AT, r3.at
        r4 = Region()
        r4.at = PARAMS_END + 3 * RT * D
        HFE = r4.take(FC * CAP).rearrange("p (f s) -> p f s", f=FC)
        HTE = r4.take(FC * CAP).bitcast(F16).rearrange("p (h f s) -> p h f s", h=2, f=FC)
        r5 = Region()
        r5.at = PARAMS_END + DC * ROWS
        KT5 = r5.take(DC * ROWS).rearrange("p (c r) -> p c r", c=DC)
        V5 = r5.take(RT * D).rearrange("p (t d) -> p t d", t=RT)
        S5 = r5.take(RT * P).rearrange("p (t k) -> p t k", t=RT)
        S5T = r5.take(RT * P).rearrange("p (t q) -> p t q", t=RT)
        m5 = r5.take(RT)
        s5 = r5.take(RT)

        dve_n = [0]
        pool_n = [0]

        def lk(ins):
            dve_n[0] += 1
            ins.then_inc(sem("dve_step"), 1)
            nc.vector.wait_ge(sem("dve_step"), dve_n[0])

        def plk(ins):
            pool_n[0] += 1
            ins.then_inc(sem("pool_step"), 1)
            nc.gpsimd.wait_ge(sem("pool_step"), pool_n[0])

        def bc(ap, shape):
            return ap.broadcast_to(shape)

        def row(name):
            i = ROWV.index(name)
            return rows_b[:, i, :]

        def col(name, i=0, n=1):
            return colv[:, COLS[name] + i:COLS[name] + i + n]

        def ln_dve(v, k, src, dst, w=None, b=None, last=None):
            for t in range(RT):
                ins = v.bn_stats(stats[:, t, :], src[:, t, :])
            lk(ins)
            for t in range(RT):
                ins = v.bn_aggr(mv[:, t, :], stats[:, t, :])
            ins.then_inc(sem("ln_var"), 1)
            v.wait_ge(sem("ln_std"), k + 1)
            lk(v.reciprocal(rstd[:, :], rstd[:, :]))
            for t in range(RT):
                ins = v.tensor_scalar(dst[:, t, :], src[:, t, :], mv[:, t, 0:1], rstd[:, t:t + 1],
                                      ALU.subtract, ALU.mult)
            if w is not None:
                lk(ins)
                lk(v.tensor_tensor(dst[:, :, :], dst[:, :, :], bc(row(w).unsqueeze(1), [P, RT, D]), ALU.mult))
                ins = v.tensor_tensor(dst[:, :, :], dst[:, :, :], bc(row(b).unsqueeze(1), [P, RT, D]), ALU.add)
            dve_n[0] += 1
            ins.then_inc(sem("dve_step"), 1)
            v.wait_ge(sem("dve_step"), dve_n[0])
            v.engine_nop().then_inc(sem("ln_out"), 1)

        def ln_act(a, k):
            a.wait_ge(sem("ln_var"), k + 1)
            a.activation(rstd[:, :], mv[:, :, 1], ACT.Sqrt, bias=eps_c[:, 0:1]).then_inc(sem("ln_std"), 1)

        def tr_pe(pe, k, src, ready, value, bank=6):
            pe.wait_ge(ready, value)
            if k:
                pe.wait_ge(sem("tr_out_v"), k)
                pe.wait_ge(sem("tr_out_a"), k)
            for c in range(DC):
                for t in range(RT):
                    ins = pe.transpose(PS[:, bank + c, t * P:(t + 1) * P], src[:, t, c * P:(c + 1) * P], ident[:, :])
                ins.then_inc(sem("tr_ps"), 1)

        def tr_dve(v, k, dst, bank=6):
            v.wait_ge(sem("tr_ps"), 2 * k + 1)
            v.tensor_copy(dst[:, 0, :], PS[:, bank, :]).then_inc(sem("tr_out_v"), 1)

        def tr_act(a, k, dst, bank=6):
            a.wait_ge(sem("tr_ps"), 2 * k + 2)
            a.activation(dst[:, 1, :], PS[:, bank + 1, :], ACT.Copy).then_inc(sem("tr_out_a"), 1)

        def tr_done(eng, k):
            eng.wait_ge(sem("tr_out_v"), k + 1)
            eng.wait_ge(sem("tr_out_a"), k + 1)

        def rows_mm(pe, srcT, w, done, banks=(0, 1), n=D):
            for t in range(RT):
                for c in range(DC):
                    ins = pe.matmul(PS[:, banks[t // 2], (t % 2) * n:(t % 2 + 1) * n],
                                    srcT[:, c, t * P:(t + 1) * P], w[:, c, 0:n], start=(c == 0), stop=(c == DC - 1))
                ins.then_inc(done, 1)

        def cols_mm(pe, srcT, w, done, banks=(0, 1)):
            for m in range(DC):
                for c in range(DC):
                    ins = pe.matmul(PS[:, banks[m], :], w[:, c, m * P:(m + 1) * P], srcT[:, c, :],
                                    start=(c == 0), stop=(c == DC - 1))
                ins.then_inc(done, 1)

        def pst(banks, t):
            return PS[:, banks[t // 2], (t % 2) * D:(t % 2 + 1) * D]

        def hold(eng, s, v):
            eng.wait_ge(s, v)
            if not isinstance(v, int):
                eng.sem_inc(sem("held_pool" if eng is nc.gpsimd else "held_pe" if eng is nc.tensor else
                                 "held_sp" if eng is nc.sync else "held_dve"), 1)

        def v_unit(n):
            return (n + V_UNITS - 1) % V_UNITS

        class Cross:
            def __init__(self, L, ln_k, tr_k):
                self.L, self.ln_k, self.tr_k = L, ln_k, tr_k
                self.q0 = DC * L
                x = f"x{L}_"
                self.q_ps, self.q_out = sem("q_ps"), sem("q_out")
                self.q_high, self.qm = sem("q_high"), sem("qm")
                self.qs = sem("qs")
                self.w_split = sem("w_split")
                self.ctx = sem(x + "ctx")
                self.high, self.split = sem(x + "high"), sem(x + "split")
                if L == 0:
                    self.mask0, self.mask1 = sem(x + "mask0"), sem(x + "mask1")
                    self.mk = sem(x + "mk")
                self.k_high = sem(x + "k_high")
                self.ks = [sem(x + "ks0"), sem(x + "ks1")]
                self.unit_ps = sem(x + "unit_ps")
                self.k_out, self.v_out = sem(x + "k_out"), sem(x + "v_out")
                self.score_ps = sem(x + "score_ps")
                self.score_out = sem(x + "score_out")
                self.nmax = sem(x + "nmax")
                self.exp = sem(x + "exp")
                self.turn_ps = sem(x + "turn_ps")
                self.turn_out, self.turn_out_v = sem(x + "turn_out"), sem(x + "turn_out_v")
                self.rexp = sem(x + "rexp")
                self.pv_ps, self.pv_out = sem(x + "pv_ps"), sem(x + "pv_out")
                self.gather_step = sem(x + "gather_step")
                self.done, self.o_ps = sem("ot_done"), sem("o_ps")

            def load_ctx(self, sp, b):
                if not isinstance(b, int) or b:
                    hold(sp, self.split, b)
                sp.dma_start(CR, ctxT[b].rearrange("(c p) s -> p c s", p=P)).then_inc(self.ctx, 16)

            def load_mask(self, sp, b, p):
                if self.L == 0:
                    sp.dma_start(MK[:, p, :], bc(mask[b:b + 1, :] if isinstance(b, int) else mask[bass.ds(b, 1), :],
                                                 [P, S])).then_inc(self.mask0 if p == 0 else self.mask1, 16)

            def spread_k(self, sp, b, c):
                hold(sp, self.k_out, K_UNITS * b + 4 * (c + 1))
                if not isinstance(b, int) or b:
                    hold(sp, self.score_ps, 16 * (b - 1) + 8 * (c + 1))
                for j in range(4):
                    for quad in range(4):
                        sp.dma_start(KS[32 * quad:32 * quad + 32, 4 * c + j, :],
                                     KHL[32 * j:32 * j + 32, quad // 2, c, :]).then_inc(self.ks[c], 16)

            def spread_q(self, sp):
                sp.wait_ge(self.qm, self.L + 1)
                for quad in range(4):
                    for j in range(4):
                        sp.dma_start(QS[32 * quad:32 * quad + 32].rearrange("p (c j) b q -> p j c (b q)", j=4)[:, j],
                                     QM[32 * j:32 * j + 32, quad % 2].rearrange("p c b q -> p c (b q)"))\
                            .then_inc(self.qs, 16)

            def sp_first(self, sp):
                self.load_ctx(sp, 0)
                self.load_mask(sp, 0, 0)
                self.load_mask(sp, 1, 1)
                self.load_ctx(sp, 1)

            def sp_main(self, sp):
                self.spread_q(sp)
                for c in range(DC):
                    self.spread_k(sp, 0, c)
                self.load_ctx(sp, 2)
                with sp.Fori(0, 2) as i:
                    for p in range(2):
                        self.sp_batch(sp, 2 * i + p, p)
                self.sp_batch(sp, 4, 0)
                self.sp_batch(sp, 5, 1)
                for c in range(DC):
                    self.spread_k(sp, 7, c)
                for c in range(DC):
                    sp.wait_ge(self.ks[c], 8 * SPREAD)

            def sp_batch(self, sp, b, p):
                self.spread_k(sp, b + 1, 0)
                self.spread_k(sp, b + 1, 1)
                if not isinstance(b, int) or b + 3 < B:
                    self.load_ctx(sp, b + 3)
                if self.L == 0:
                    hold(sp, self.score_out, 16 * (b + 1))
                self.load_mask(sp, b + 2, p)

            def pool_split(self, g, b, p, free):
                hold(g, self.ctx, 16 * (b + 1))
                if free:
                    hold(g, self.unit_ps, UNITS * (b - 1))
                g.tensor_copy(CHL[p][:, 0], CR).then_inc(self.high, 1)
                hold(g, self.high, b + 1)
                g.tensor_tensor(CHL[p][:, 1], CR, CHL[p][:, 0], ALU.subtract).then_inc(self.split, 1)

            def pool_mask(self, g, b, p, j):
                if self.L == 0:
                    hold(g, self.mask0 if p == 0 else self.mask1, 16 * (j + 1))
                    g.tensor_scalar(MK[:, p, :], MK[:, p, :], -1e9 * WS, None, ALU.mult).then_inc(self.mk, 1)

            def pool_main(self, g):
                self.pool_mask(g, 0, 0, 0)
                self.pool_split(g, 1, 1, False)
                self.pool_mask(g, 1, 1, 0)
                with g.Fori(0, 3) as i:
                    for p in range(2):
                        self.pool_split(g, 2 * i + 2 + p, p, True)
                        self.pool_mask(g, 2 * i + 2 + p, p, i + 1)

            def pe_unit(self, pe, kind, b, p, n, bank):
                if kind == "k":
                    m, (k0, w) = n // 4, K_BLOCKS[n % 4]
                    mms = [(PS[:, bank, 0:w], W[:, 0, c, m * P:(m + 1) * P], CHL[p][:, h, c, k0:k0 + w], c == 0 and i == 0,
                            c == DC - 1 and i == 2)
                           for c in range(DC) for i, (W, h) in enumerate(((WH, 0), (WH, 1), (WL, 0)))]
                else:
                    mms = []
                    for s in range(2):
                        kt = 2 * v_unit(n) + s
                        if kt < KT_N:
                            w = P if kt < KT_N - 1 else S_LAST
                            mms += [(PS[0:w, bank, s * D:(s + 1) * D], CHL[p][:, h, c, kt * P:kt * P + w], W[:, 1, c, :],
                                     c == 0 and i == 0, c == DC - 1 and i == 2)
                                    for c in range(DC) for i, (W, h) in enumerate(((WH, 0), (WL, 0), (WH, 1)))]
                for o, lhs, rhs, first, last in mms:
                    ins = pe.matmul(o, lhs, rhs, start=first, stop=last)
                ins.then_inc(self.unit_ps, 1)

            def scores(self, pe, b, g):
                if g % 4 == 0:
                    hold(pe, self.ks[g // 4], SPREAD * (b + 1))
                lhs = QS[:, g, b, :] if isinstance(b, int) else QS[:, g, bass.ds(b, 1), :].rearrange("p o q -> p (o q)")
                for half in range(2):
                    if g or not isinstance(b, int) or b:
                        hold(pe, self.score_out, 16 * b + 2 * g - 1 + half)
                    for k0, n in KEY_BLOCKS[2 * half:2 * half + 2]:
                        ins = pe.matmul(psf[:, k0:k0 + n], lhs, KS[:, g, k0:k0 + n], start=True, stop=True)
                    ins.then_inc(self.score_ps, 1)

            def turn(self, pe, b, g, ks):
                if 0 in ks:
                    pe.wait_ge(self.exp, 8 * b + g + 1)
                pair = PAIRS * b + g
                for k in ks:
                    if k == 3:
                        pe.wait_ge(self.turn_out_v, pair + 1)
                    elif g or k >= 2 or not isinstance(b, int) or b:
                        pe.wait_ge(self.turn_out, 3 * pair + (k - 1 if k < 2 else 1))
                    for kt in range(4 * k, min(4 * k + 4, KT_N)):
                        n = P if kt < KT_N - 1 else S_LAST
                        ins = pe.transpose(PS[0:n, 4 + k % 2, (kt % 4) * P:(kt % 4 + 1) * P],
                                           SC[:, g % 2, kt * P:kt * P + n], ident[:, :])
                    ins.then_inc(self.turn_ps, 1)

            def pv(self, pe, b, p, q):
                if q == 0:
                    hold(pe, self.v_out, V_UNITS * (b + 1))
                pe.wait_ge(self.rexp, 2 * b + q + 1)
                if q:
                    pe.wait_ge(self.pv_out, 2 * b + 1)
                pe.matmul(PS[:, 7, P:2 * P], rexp[:, :, :].rearrange("p a b -> p (a b)"), ident[:, :],
                          start=True, stop=True)
                pe.wait_ge(self.turn_out, 24 * b + 12 * (q + 1))
                pe.wait_ge(self.turn_out_v, 8 * b + 4 * (q + 1))
                for kt in range(KT_N):
                    n = P if kt < KT_N - 1 else S_LAST
                    for j in range(4):
                        g = 4 * q + j
                        ins = pe.matmul(PS[32 * j:32 * j + 32, 7, 0:P], VS[0:n, p, kt, 32 * g:32 * g + 32],
                                        PT[0:n, kt, j, :], start=(kt == 0), stop=(kt == KT_N - 1))
                ins.then_inc(self.pv_ps, 1)

            def v_bank(self, g):
                return 6 if g in (1, 5) else 7

            def pe_batch(self, pe, b, p, project):
                nb, np_ = b + 1, 1 - p
                former = not isinstance(b, int) or b > 0
                for g in range(PAIRS):
                    self.scores(pe, b, g)
                    if project:
                        if g == 0:
                            hold(pe, self.split, nb + 1)
                            pe.wait_ge(self.v_out, V_UNITS * nb)
                        elif self.v_bank(g - 1) == 7:
                            pe.wait_ge(self.k_out, K_UNITS * nb + g)
                        else:
                            pe.wait_ge(self.v_out, V_UNITS * nb + g - 1)
                        self.pe_unit(pe, "k", nb, np_, g, 6)
                    if g == 1 and former:
                        hold(pe, self.v_out, V_UNITS * nb)
                        self.pv(pe, b - 1, 1 - p, 1)
                    if g == 5:
                        if project:
                            hold(pe, self.v_out, V_UNITS * nb + 4)
                        self.pv(pe, b, p, 0)
                    before_b, before_g = (b, g - 1) if g else (b - 1, PAIRS - 1)
                    if g or former:
                        self.turn(pe, before_b, before_g, (0, 1))
                    if project and g:
                        if self.v_bank(g) == 6:
                            pe.wait_ge(self.k_out, K_UNITS * nb + g + 1)
                        elif g > 2 and self.v_bank(g - 1) == 7:
                            pe.wait_ge(self.v_out, V_UNITS * nb + g - 1)
                        elif g > 4 or former:
                            pe.wait_ge(self.pv_out, 2 * b + (g > 4))
                        self.pe_unit(pe, "v", nb, np_, g - 1, self.v_bank(g))
                    if g or former:
                        self.turn(pe, before_b, before_g, (2, 3))

            def pe_main(self, pe):
                tr_pe(pe, self.tr_k, XN, sem("ln_out"), self.ln_k + 1)
                tr_done(pe, self.tr_k)
                pe.wait_ge(sem(f"w_x{self.L}"), 64)
                cols_mm(pe, XT, W4[:, 0], self.q_ps)
                pe.wait_ge(self.split, 1)
                pe.wait_ge(self.w_split, self.L + 1)
                for u in range(UNITS):
                    if u >= 3:
                        if u - 3 < K_UNITS:
                            pe.wait_ge(self.k_out, u - 2)
                        else:
                            pe.wait_ge(self.v_out, u - 2 - K_UNITS)
                    self.pe_unit(pe, "k" if u < K_UNITS else "v", 0, 0, u if u < K_UNITS else u - K_UNITS, 5 + u % 3)
                pe.wait_ge(self.qs, 256 * (self.L + 1))
                self.pe_batch(pe, 0, 0, True)
                with pe.Fori(0, 3) as i:
                    for p in range(2):
                        self.pe_batch(pe, 2 * i + 1 + p, 1 - p, True)
                self.pe_batch(pe, 7, 1, False)
                self.turn(pe, 7, PAIRS - 1, range(4))
                self.pv(pe, 7, 1, 1)
                pe.wait_ge(self.done, self.L + 1)
                rows_mm(pe, OT, W4[:, 3], self.o_ps)

            def unit_no(self, b, kind, n):
                if isinstance(b, int) and b == 0:
                    return n + 1 + (K_UNITS if kind == "v" else 0)
                return UNITS * b + (n + 1 + max(0, n - 1) if kind == "k" else 2 * n + 3)

            def k_low(self, v, b, n, bank=6):
                v.wait_ge(self.k_high, K_UNITS * b + n + 1)
                m, (k0, w) = n // 4, K_BLOCKS[n % 4]
                if self.L == 0:
                    ins = v.scalar_tensor_tensor(KHL[:, 1, m, k0:k0 + w], PS[:, bank, 0:w], bkw[:, m:m + 1],
                                                 KHL[:, 0, m, k0:k0 + w], ALU.add, ALU.subtract)
                else:
                    ins = v.tensor_tensor(KHL[:, 1, m, k0:k0 + w], PS[:, bank, 0:w], KHL[:, 0, m, k0:k0 + w], ALU.subtract)
                ins.then_inc(self.k_out, 1)

            def v_evac(self, v, b, p, n, bank=6):
                v.wait_ge(self.unit_ps, self.unit_no(b, "v", n))
                kt = 2 * v_unit(n)
                if kt < KT_N - 1:
                    ins = v.tensor_scalar(VS[:, p, kt:kt + 2, :].rearrange("p k d -> p (k d)"), PS[:, bank, :], 1 / WS, None,
                                          ALU.mult)
                else:
                    ins = v.tensor_scalar(VS[0:S_LAST, p, kt, :], PS[0:S_LAST, bank, 0:D], 1 / WS, None, ALU.mult)
                ins.then_inc(self.v_out, 1)

            def row_max(self, v, b, p, g):
                if g == 0 and self.L == 0:
                    v.wait_ge(self.mk, b + 1)
                if g >= 2 or not isinstance(b, int) or b:
                    v.wait_ge(self.turn_ps, 32 * b + 4 * (g - 1))
                for half, (k0, k1) in enumerate(((0, HALF_A), (HALF_A, S))):
                    hold(v, self.score_ps, 16 * b + 2 * g + 1 + half)
                    if self.L == 0:
                        ins = v.tensor_tensor_reduce(SC[:, g % 2, k0:k1], psf[:, k0:k1], MK[:, p, k0:k1], 1.0, -3e38,
                                                     ALU.add, ALU.max, mx[:, g, half:half + 1])
                    else:
                        ins = v.tensor_scalar(SC[:, g % 2, k0:k1], psf[:, k0:k1], 1.0, -3e38, ALU.mult, ALU.max,
                                              accum_out=mx[:, g, half:half + 1])
                    ins.then_inc(self.score_out, 1)
                v.wait_ge(self.score_out, 16 * b + 2 * g + 2)
                v.tensor_scalar(nmax[:, g:g + 1], mx[:, g, 0:1], mx[:, g, 1:2], -1 / WS, ALU.max, ALU.mult)\
                    .then_inc(self.nmax, 1)

            def turn_evac_v(self, v, b, g):
                v.wait_ge(self.turn_ps, 32 * b + 4 * g + 2)
                v.tensor_copy(PT[:, 4:8, g % 4, :], PS[:, 5, :].rearrange("p (k q) -> p k q", k=4))\
                    .then_inc(self.turn_out_v, 1)

            def recip(self, v, b, q):
                v.wait_ge(self.exp, 8 * b + 4 * q + 4)
                v.reciprocal(rinv[:, :], rsum[:, 4 * q:4 * q + 4]).then_inc(self.gather_step, 1)
                v.wait_ge(self.gather_step, 5 * (2 * b + q) + 1)
                v.tensor_copy(rexp[:, :, :], bc(rinv[:, :].unsqueeze(2), [P, 4, 32])).then_inc(self.rexp, 1)

            def gather(self, v, b, q):
                n0 = 5 * (2 * b + q) + 1
                v.wait_ge(self.pv_ps, 2 * b + q + 1)
                v.tensor_copy(rbc[:, :], PS[:, 7, P:2 * P]).then_inc(self.gather_step, 1)
                v.wait_ge(self.gather_step, n0 + 1)
                v.tensor_tensor(osc[:, :], PS[:, 7, 0:P], rbc[:, :], ALU.mult).then_inc(self.pv_out, 1)
                v.wait_ge(self.pv_out, 2 * b + q + 1)
                if self.L == 0:
                    v.tensor_scalar(otmp[:, :], osc[:, 0:T], parity[:, 0:1], col("bv0", q), ALU.mult, ALU.add)\
                        .then_inc(self.gather_step, 1)
                else:
                    v.tensor_scalar(otmp[:, :], osc[:, 0:T], parity[:, 0:1], None, ALU.mult).then_inc(self.gather_step, 1)
                v.wait_ge(self.gather_step, n0 + 2)
                v.tensor_scalar(osc[:, T:P], osc[:, T:P], parity[:, 1:2], None, ALU.mult).then_inc(self.gather_step, 1)
                v.wait_ge(self.gather_step, n0 + 3)
                dst = OT[:, q, b * T:(b + 1) * T] if isinstance(b, int) else OT[:, q, bass.ds(b * T, T)]
                v.tensor_tensor(dst, osc[:, T:P], otmp[:, :], ALU.add).then_inc(self.gather_step, 1)

            def dve_batch(self, v, b, p, project):
                nb, np_ = b + 1, 1 - p
                former = not isinstance(b, int) or b > 0
                for g in range(PAIRS):
                    before_b, before_g = (b, g - 1) if g else (b - 1, PAIRS - 1)
                    self.row_max(v, b, p, g)
                    if g == 0 and former:
                        self.turn_evac_v(v, before_b, before_g)
                    if project:
                        self.k_low(v, nb, g)
                    if g == 0 and former:
                        self.recip(v, b - 1, 1)
                    if g == 1 and former:
                        self.gather(v, b - 1, 1)
                    if g == 4:
                        self.recip(v, b, 0)
                    if g == 5:
                        self.gather(v, b, 0)
                    if g:
                        self.turn_evac_v(v, before_b, before_g)
                    if project and g:
                        self.v_evac(v, nb, np_, g - 1, self.v_bank(g))

            def dve_main(self, v):
                ln_dve(v, self.ln_k, X, XN)
                tr_dve(v, self.tr_k, XT)
                v.wait_ge(sem(f"w_x{self.L}"), 64)
                raw = W4[:, 1:3].rearrange("p i c d -> p (i c d)")
                high, low = (w[:, :, :, :].rearrange("p i c d -> p (i c d)") for w in (WH, WL))
                lk(v.tensor_scalar(high, raw, WS, None, ALU.mult))
                v.scalar_tensor_tensor(low, raw, WS, high, ALU.mult, ALU.subtract).then_inc(self.w_split, 1)
                if self.L == 0:
                    v.wait_ge(sem("consts"), 1)
                    lk(v.tensor_reduce(parity[:, :], headmask[:, :].rearrange("p (a b) -> p b a", b=2), AX.X, ALU.add))
                    v.wait_ge(sem("cols_in"), 16)
                    v.tensor_scalar(bkw[:, :], col("bk0", 0, DC), WS, None, ALU.mult).then_inc(sem("bkw"), 1)
                    v.wait_ge(sem("bkw"), 1)
                v.wait_ge(self.high, 1)
                v.tensor_tensor(CHL[0][:, 1], CR, CHL[0][:, 0], ALU.subtract).then_inc(self.split, 1)
                for c in range(DC):
                    v.wait_ge(self.q_ps, self.q0 + c + 1)
                    if self.L == 0:
                        ins = v.tensor_scalar(Q32[:, c, :], PS[:, c, :], col("bq0", c), HD ** -0.5, ALU.add, ALU.mult)
                    else:
                        ins = v.tensor_scalar(Q32[:, c, :], PS[:, c, :], HD ** -0.5, None, ALU.mult)
                    ins.then_inc(self.q_out, 1)
                v.wait_ge(self.q_high, self.L + 1)
                lk(v.tensor_tensor(QHL[:, 1], Q32, QHL[:, 0], ALU.subtract))
                for h in range(2):
                    for s in range(2):
                        ins = v.tensor_scalar(QM[:, h, :, :, s * T:(s + 1) * T].rearrange("p c b q -> p (c b) q"),
                                              QHL[:, h].rearrange("p c (b q) -> p (c b) q", b=B), parity[:, s:s + 1],
                                              None, ALU.mult)
                ins.then_inc(self.qm, 1)
                for u in range(K_UNITS):
                    self.k_low(v, 0, u, 5 + u % 3)
                for n in range(V_UNITS):
                    self.v_evac(v, 0, 0, n, 5 + (n + K_UNITS) % 3)
                self.dve_batch(v, 0, 0, True)
                with v.Fori(0, 3) as i:
                    for p in range(2):
                        self.dve_batch(v, 2 * i + 1 + p, 1 - p, True)
                self.dve_batch(v, 7, 1, False)
                self.turn_evac_v(v, 7, PAIRS - 1)
                self.recip(v, 7, 1)
                self.gather(v, 7, 1)
                v.wait_ge(self.gather_step, 80)
                v.engine_nop().then_inc(self.done, 1)
                if self.L == 0:
                    v.wait_ge(sem("rows_in"), 16)
                lk(v.tensor_tensor(X[:, :, :], X[:, :, :], bc(row("bo0" if self.L == 0 else "bo3").unsqueeze(1),
                                                              [P, RT, D]), ALU.add))
                for t in range(RT):
                    v.wait_ge(self.o_ps, RT * self.L + (t // 2 + 1) * 2)
                    ins = v.tensor_tensor(X[:, t, :], X[:, t, :], pst((0, 1), t), ALU.add)
                lk(ins)

            def k_high_half(self, a, b, n, bank=6):
                a.wait_ge(self.unit_ps, self.unit_no(b, "k", n))
                if n in (0, 4) and not (isinstance(b, int) and b == 0):
                    a.wait_ge(self.ks[n // 4], SPREAD * b)
                m, (k0, w) = n // 4, K_BLOCKS[n % 4]
                a.activation(KHL[:, 0, m, k0:k0 + w], PS[:, bank, 0:w], ACT.Identity,
                             bias=bkw[:, m:m + 1] if self.L == 0 else 0.0).then_inc(self.k_high, 1)

            def turn_evac(self, a, b, g, ks):
                for k in ks:
                    a.wait_ge(self.turn_ps, 32 * b + 4 * g + k + 1)
                    if k < 3:
                        ins = a.activation(PT[:, 4 * k:4 * k + 4, g % 4, :],
                                           PS[:, 4 + k % 2, :].rearrange("p (k q) -> p k q", k=4), ACT.Copy)
                    else:
                        ins = a.activation(PT[0:S_LAST, KT_N - 1, g % 4, :], PS[0:S_LAST, 4 + k % 2, 0:P], ACT.Copy)
                    ins.then_inc(self.turn_out, 1)

            def exp_row(self, a, b, g):
                a.wait_ge(self.nmax, 8 * b + g + 1)
                a.activation(SC[:, g % 2, :], SC[:, g % 2, :], ACT.Exp, bias=nmax[:, g:g + 1], scale=1 / WS,
                             accum_out=rsum[:, g:g + 1]).then_inc(self.exp, 1)

            def act_batch(self, a, b, p, project):
                for g in range(PAIRS):
                    before_b, before_g = (b, g - 1) if g else (b - 1, PAIRS - 1)
                    former = g or not isinstance(b, int) or b
                    if project:
                        self.k_high_half(a, b + 1, g)
                    if former:
                        self.turn_evac(a, before_b, before_g, (0,))
                    self.exp_row(a, b, g)
                    if former:
                        self.turn_evac(a, before_b, before_g, (2, 3))

            def act_main(self, a):
                ln_act(a, self.ln_k)
                tr_act(a, self.tr_k, XT)
                a.wait_ge(self.ctx, 16)
                a.activation(CHL[0][:, 0], CR, ACT.Copy).then_inc(self.high, 1)
                a.wait_ge(self.q_out, self.q0 + DC)
                a.activation(QHL[:, 0], Q32, ACT.Copy).then_inc(self.q_high, 1)
                if self.L == 0:
                    a.wait_ge(sem("bkw"), 1)
                for u in range(K_UNITS):
                    self.k_high_half(a, 0, u, 5 + u % 3)
                self.act_batch(a, 0, 0, True)
                with a.Fori(0, 3) as i:
                    for p in range(2):
                        self.act_batch(a, 2 * i + 1 + p, 1 - p, True)
                self.act_batch(a, 7, 1, False)
                self.turn_evac(a, 7, PAIRS - 1, (0, 2, 3))

        cross0 = Cross(0, 0, 0)
        cross1 = Cross(1, 7, 5)

        PATT = dict(
            q=dict(i=0, src=XT, k=PK[:, 0], v=PV[:, 0], nch=2, a=PA[:, :, 0:D], at=PAT[:, 0:2], C=0),
            k=dict(i=1, src=XT, k=PK[:, 1], v=PV[:, 1], nch=2, a=PA[:, :, D:2 * D], at=PAT[:, 2:4], C=2),
            v=dict(i=2, src=XT, k=PK[:, 2], v=PV[:, 2], nch=2, a=PA[:, :, 2 * D:3 * D], at=PAT[:, 4:6], C=4),
            p=dict(i=3, src=OT, k=PK[:, 3], v=PV[:, 3], nch=2, a=PA[:, :, 3 * D:4 * D], at=PAT[:, 6:8], C=6),
            f=dict(i=4, src=XT, k=FKs, v=FVs, nch=FC, a=PA, at=PAT, C=8))
        PSCALE = D ** -0.5

        def patt_scores(pe, p):
            for t in range(RT):
                n = RT * p["i"] + t
                if n >= 2:
                    pe.wait_ge(sem("p_exp"), n - 1)
                for blk in range(0, p["nch"] * P, BANK):
                    w = min(BANK, p["nch"] * P - blk)
                    for c in range(DC):
                        ins = pe.matmul(PS[:, 2 * (n % 2) + blk // BANK, 0:w], p["src"][:, c, t * P:(t + 1) * P],
                                        p["k"][:, c, blk:blk + w], start=(c == 0), stop=(c == DC - 1))
                ins.then_inc(sem("p_score"), 1)

        def patt_ps(p, n):
            return psf[:, 2 * BANK * (n % 2):2 * BANK * (n % 2) + p["nch"] * P]

        def patt_softmax_dve(v, p):
            def norm(n):
                v.wait_ge(sem("p_exp"), n + 1)
                lk(v.reciprocal(psm[:, n:n + 1], psm[:, n:n + 1]))
                a = p["a"][:, n % RT, :]
                v.tensor_scalar(a, a, psm[:, n:n + 1], None, ALU.mult).then_inc(sem("p_norm"), 1)

            for t in range(RT):
                n = RT * p["i"] + t
                v.wait_ge(sem("p_score"), n + 1)
                lk(v.tensor_reduce(pmax[:, n:n + 1], patt_ps(p, n), AX.X, ALU.max))
                v.tensor_scalar(pmax[:, n:n + 1], pmax[:, n:n + 1], -PSCALE, None, ALU.mult).then_inc(sem("p_nmax"), 1)
                if t:
                    norm(n - 1)
            norm(RT * p["i"] + RT - 1)

        def patt_exp(a, p):
            for t in range(RT):
                n = RT * p["i"] + t
                a.wait_ge(sem("p_nmax"), n + 1)
                a.activation(p["a"][:, t, :], patt_ps(p, n), ACT.Exp, bias=pmax[:, n:n + 1], scale=PSCALE,
                             accum_out=psm[:, n:n + 1]).then_inc(sem("p_exp"), 1)

        def patt_turn(pe, p):
            pe.wait_ge(sem("p_norm"), RT * (p["i"] + 1))
            for ch in range(p["nch"]):
                C = p["C"] + ch
                if C >= 2:
                    pe.wait_ge(sem("p_at_v" if C % 2 == 0 else "p_at_a"), C // 2)
                for t in range(RT):
                    ins = pe.transpose(PS[:, 4 + C % 2, t * P:(t + 1) * P], p["a"][:, t, ch * P:(ch + 1) * P],
                                       ident[:, :])
                ins.then_inc(sem("p_turn"), 1)

        def patt_turn_v(v, p):
            for ch in range(0, p["nch"], 2):
                v.wait_ge(sem("p_turn"), p["C"] + ch + 1)
                v.tensor_copy(p["at"][:, ch, :], PS[:, 4, :]).then_inc(sem("p_at_v"), 1)

        def patt_turn_a(a, p):
            for ch in range(1, p["nch"], 2):
                a.wait_ge(sem("p_turn"), p["C"] + ch + 1)
                a.activation(p["at"][:, ch, :], PS[:, 5, :], ACT.Copy).then_inc(sem("p_at_a"), 1)

        def patt_out(pe, p, cols):
            chunks = (p["C"] + p["nch"]) // 2
            pe.wait_ge(sem("p_at_v"), chunks)
            pe.wait_ge(sem("p_at_a"), chunks)
            for half in range(2):
                if 1 <= p["i"] <= 2:
                    pe.wait_ge(sem("p_out_v" if half == 0 else "p_out_a"), p["i"])
                if cols:
                    for ch in range(p["nch"]):
                        ins = pe.matmul(PS[:, 6 + half, :], p["v"][:, ch, half * P:(half + 1) * P], p["at"][:, ch, :],
                                        start=(ch == 0), stop=(ch == p["nch"] - 1))
                else:
                    for t in range(2 * half, 2 * half + 2):
                        for ch in range(p["nch"]):
                            ins = pe.matmul(pst((6, 7), t), p["at"][:, ch, t * P:(t + 1) * P], p["v"][:, ch, :],
                                            start=(ch == 0), stop=(ch == p["nch"] - 1))
                ins.then_inc(sem("p_out"), 1)

        def latent_dve(v):
            ln_dve(v, 1, X, XN)
            ln_dve(v, 2, XN, HN)
            tr_dve(v, 1, XT)
            patt_softmax_dve(v, PATT["q"])
            patt_softmax_dve(v, PATT["k"])
            patt_turn_v(v, PATT["q"])
            patt_softmax_dve(v, PATT["v"])
            patt_turn_v(v, PATT["k"])
            v.wait_ge(sem("p_out"), 1)
            v.tensor_scalar(QT[:, 0, :], PS[:, 6, :], HD ** -0.5, None, ALU.mult).then_inc(sem("p_out_v"), 1)
            patt_turn_v(v, PATT["v"])
            v.wait_ge(sem("p_out"), 3)
            v.tensor_copy(KT2[:, 0, :], PS[:, 6, :]).then_inc(sem("p_out_v"), 1)
            v.wait_ge(sem("p_out"), 5)
            v.tensor_copy(V2[:, 0:2, :].rearrange("p t d -> p (t d)"), PS[:, 6, :]).then_inc(sem("p_out_v"), 1)

            def soft(t):
                u = t % 2
                if t >= 2:
                    v.wait_ge(sem("s_turn"), 2 * (t - 1))
                v.wait_ge(sem("s_score"), t + 1)
                ins = v.tensor_tensor(SP[:, u], psf[:, 2 * BANK * u:2 * BANK * (u + 1)].rearrange("p (g k) -> p g k", k=T),
                                      bc(causal[:, :].unsqueeze(1), [P, 2 * PAIRS, T]), ALU.add)
                lk(ins)
                lk(v.tensor_reduce(gmax[:, :], SP[:, u], AX.X, ALU.max))
                v.tensor_tensor(SP[:, u], SP[:, u], bc(gmax[:, :].unsqueeze(2), [P, 2 * PAIRS, T]), ALU.subtract)\
                    .then_inc(sem("s_sub"), 1)

            def norm(t):
                u = t % 2
                v.wait_ge(sem("s_exp"), t + 1)
                lk(v.tensor_reduce(gsum[:, :], SP[:, u], AX.X, ALU.add))
                lk(v.reciprocal(gsum[:, :], gsum[:, :]))
                v.tensor_tensor(SP[:, u], SP[:, u], bc(gsum[:, :].unsqueeze(2), [P, 2 * PAIRS, T]), ALU.mult)\
                    .then_inc(sem("s_norm"), 1)

            def turned(t):
                v.wait_ge(sem("s_turn"), 2 * t + 1)
                v.tensor_copy(SPT[:, t % 2, 0:4].rearrange("p g q -> p (g q)"), PS[:, 4, :]).then_inc(sem("s_out_v"), 1)

            def gather(t):
                v.wait_ge(sem("s_pv"), t + 1)
                o = PS[:, 6:8, 0:D].rearrange("p b (c s q) -> p b c s q", c=DC, s=2)
                lk(v.tensor_scalar(otm[:, :, :].rearrange("p (b c) q -> p b c q", b=2), o[:, :, :, 0], parity[:, 0:1],
                                   None, ALU.mult))
                for bb in range(2):
                    b = 2 * t + bb
                    ins = v.scalar_tensor_tensor(OT[:, :, b * T:(b + 1) * T], o[:, bb, :, 1], parity[:, 1:2],
                                                 otm[:, 2 * bb:2 * bb + 2, :], ALU.mult, ALU.add)
                ins.then_inc(sem("s_o"), 1)

            soft(0)
            norm(0)
            soft(1)
            for t in range(RT):
                turned(t)
                if t + 1 < RT:
                    norm(t + 1)
                if t + 2 < RT:
                    soft(t + 2)
                gather(t)
            patt_softmax_dve(v, PATT["p"])
            patt_turn_v(v, PATT["p"])
            v.wait_ge(sem("p_out"), 8)
            for t in range(RT):
                ins = v.tensor_tensor(X1[:, t, :], pst((6, 7), t), XN[:, t, :], ALU.add)
            lk(ins)
            ln_dve(v, 3, X1, HN)
            tr_dve(v, 2, XT)
            patt_softmax_dve(v, PATT["f"])
            patt_turn_v(v, PATT["f"])
            lk(v.tensor_tensor(X[:, :, :], X[:, :, :], X1[:, :, :], ALU.add))
            for t in range(RT):
                v.wait_ge(sem("p_out"), 9 + t // 2)
                ins = v.tensor_tensor(X[:, t, :], X[:, t, :], pst((6, 7), t), ALU.add)
            lk(ins)

        def latent_act(a):
            ln_act(a, 1)
            ln_act(a, 2)
            tr_act(a, 1, XT)
            patt_exp(a, PATT["q"])
            patt_exp(a, PATT["k"])
            patt_turn_a(a, PATT["q"])
            patt_exp(a, PATT["v"])
            patt_turn_a(a, PATT["k"])
            a.wait_ge(sem("p_out"), 2)
            a.activation(QT[:, 1, :], PS[:, 7, :], ACT.Copy, scale=HD ** -0.5).then_inc(sem("p_out_a"), 1)
            patt_turn_a(a, PATT["v"])
            a.wait_ge(sem("p_out"), 4)
            a.activation(KT2[:, 1, :], PS[:, 7, :], ACT.Copy).then_inc(sem("p_out_a"), 1)
            a.wait_ge(sem("p_out"), 6)
            a.activation(V2[:, 2:4, :].rearrange("p t d -> p (t d)"), PS[:, 7, :], ACT.Copy).then_inc(sem("p_out_a"), 1)

            def turned(t):
                a.wait_ge(sem("s_turn"), 2 * t + 2)
                a.activation(SPT[:, t % 2, 4:8].rearrange("p g q -> p (g q)"), PS[:, 5, :], ACT.Copy)\
                    .then_inc(sem("s_out_a"), 1)

            for t in range(RT):
                a.wait_ge(sem("s_sub"), t + 1)
                a.activation(SP[:, t % 2], SP[:, t % 2], ACT.Exp).then_inc(sem("s_exp"), 1)
                if t:
                    turned(t - 1)
            turned(RT - 1)
            patt_exp(a, PATT["p"])
            patt_turn_a(a, PATT["p"])
            ln_act(a, 3)
            tr_act(a, 2, XT)
            patt_exp(a, PATT["f"])
            patt_turn_a(a, PATT["f"])

        def latent_pool(g):
            g.wait_ge(sem("p_out_v"), 1)
            g.wait_ge(sem("p_out_a"), 1)
            for b in range(B):
                if b >= 2:
                    g.wait_ge(sem("s_score"), b // 2)
                for c in range(DC):
                    g.tensor_tensor(QB[:, b % 2, c, :, :], bc(QT[:, c, b * T:(b + 1) * T].unsqueeze(1), [P, HPC, T]),
                                    bc(headmask[:, :].unsqueeze(2), [P, HPC, T]), ALU.mult).then_inc(sem("s_qb"), 1)

        def latent_pe(pe):
            tr_pe(pe, 1, HN, sem("ln_out"), 3)
            tr_done(pe, 1)
            pe.wait_ge(sem("w_patt"), 128)
            q, k, w, p, f = (PATT[n] for n in "qkvpf")
            patt_scores(pe, q)
            patt_scores(pe, k)
            patt_turn(pe, q)
            patt_scores(pe, w)
            patt_turn(pe, k)
            patt_out(pe, q, True)
            patt_turn(pe, w)
            patt_out(pe, k, True)
            patt_out(pe, w, False)

            def scores(t):
                if t == 0:
                    pe.wait_ge(sem("p_out_v"), 2)
                    pe.wait_ge(sem("p_out_a"), 2)
                    pe.wait_ge(sem("p_exp"), 12)
                if t >= 2:
                    pe.wait_ge(sem("s_sub"), t - 1)
                pe.wait_ge(sem("s_qb"), 4 * (t + 1))
                for g in range(PAIRS):
                    c, j = g // 4, g % 4
                    for bb in range(2):
                        b = 2 * t + bb
                        a0 = 2 * BANK * (t % 2) + g * P + bb * T
                        ins = pe.matmul(psf[:, a0:a0 + T], QB[:, bb, c, 2 * j:2 * j + 2, :].rearrange("p h q -> p (h q)"),
                                        KT2[:, c, b * T:(b + 1) * T], start=True, stop=True)
                ins.then_inc(sem("s_score"), 1)

            def turn(t):
                pe.wait_ge(sem("s_norm"), t + 1)
                for half in range(2):
                    if t:
                        pe.wait_ge(sem("s_out_v" if half == 0 else "s_out_a"), t)
                    for g in range(4 * half, 4 * half + 4):
                        ins = pe.transpose(PS[:, 4 + half, (g % 4) * P:(g % 4 + 1) * P],
                                           SP[:, t % 2, 2 * g:2 * g + 2, :].rearrange("p b k -> p (b k)"), ident[:, :])
                    ins.then_inc(sem("s_turn"), 1)

            def pv(t):
                if t == 0:
                    pe.wait_ge(sem("p_out_v"), 3)
                    pe.wait_ge(sem("p_out_a"), 3)
                pe.wait_ge(sem("s_out_v"), t + 1)
                pe.wait_ge(sem("s_out_a"), t + 1)
                if t:
                    pe.wait_ge(sem("s_o"), t)
                for bb in range(2):
                    for c in range(DC):
                        for j in range(4):
                            g = 4 * c + j
                            ins = pe.matmul(PS[32 * j:32 * j + 32, 6 + bb, c * P:(c + 1) * P],
                                            V2[T * bb:T * bb + T, t, 32 * g:32 * g + 32],
                                            SPT[T * bb:T * bb + T, t % 2, g, :], start=True, stop=True)
                ins.then_inc(sem("s_pv"), 1)

            scores(0)
            scores(1)
            for t in range(RT):
                turn(t)
                if t + 2 < RT:
                    scores(t + 2)
                pv(t)
            pe.wait_ge(sem("s_o"), RT)
            patt_scores(pe, p)
            patt_turn(pe, p)
            patt_out(pe, p, False)
            tr_pe(pe, 2, HN, sem("ln_out"), 4)
            tr_done(pe, 2)
            pe.wait_ge(sem("w_ff"), 32)
            patt_scores(pe, f)
            patt_turn(pe, f)
            patt_out(pe, f, False)

        def top2(v):
            for t in range(RT):
                pj = bc(PROB[:, t, :].unsqueeze(1), [P, NE, NE])
                pe_ = bc(PROB[:, t, :].unsqueeze(2), [P, NE, NE])
                v.tensor_tensor(GA[:, t], pj, pe_, ALU.is_gt)
                ins = v.tensor_tensor(GB[:, t], pj, pe_, ALU.is_equal)
            lk(ins)
            lk(v.tensor_tensor(GB[:, :, :, :].rearrange("p t e j -> p t (e j)"),
                               GB[:, :, :, :].rearrange("p t e j -> p t (e j)"),
                               bc(lower8[:, :, :].rearrange("p e j -> p (e j)").unsqueeze(1), [P, RT, NE * NE]), ALU.mult))
            lk(v.tensor_tensor(GA[:, :, :, :].rearrange("p t e j -> p (t e j)"),
                               GA[:, :, :, :].rearrange("p t e j -> p (t e j)"),
                               GB[:, :, :, :].rearrange("p t e j -> p (t e j)"), ALU.add))
            lk(v.tensor_reduce(SEL[:, :, :], GA[:, :, :, :], AX.X, ALU.add))
            lk(v.tensor_scalar(SEL[:, :, :], SEL[:, :, :], 1.5, None, ALU.is_lt))

        def gate_pe(pe, L, tr_k, w):
            for t in range(RT):
                for c in range(DC):
                    ins = pe.matmul(PS[:, 0, t * NE:(t + 1) * NE], XT[:, c, t * P:(t + 1) * P], w[:, c, :],
                                    start=(c == 0), stop=(c == DC - 1))
            ins.then_inc(sem("g_logit"), 1)

        class Experts:
            def __init__(self, L, w1, w2, act, bias):
                self.L, self.w1, self.w2, self.act, self.bias = L, w1, w2, act, bias
                e = f"e{L}_"
                self.s_w0, self.s_w1 = sem(e + "w0"), sem(e + "w1")
                self.s_h_ps, self.s_h_act = sem(e + "h_ps"), sem(e + "h_act")
                self.s_y_ps, self.s_y_out = sem(e + "y_ps"), sem(e + "y_out")
                if bias:
                    self.s_b1 = sem(e + "b1")
                self.s_high, self.s_low = sem(e + "high"), sem(e + "low")
                self.s_xs = sem("xs")
                self.s_h_low = sem(e + "h_low")

            def load(self, sp, e, p):
                s = self.s_w1 if p else self.s_w0
                sp.dma_start(W1[p], self.w1[e].rearrange("(c p) f -> p c f", p=P)).then_inc(s, 16)
                sp.dma_start(W2[p], self.w2[e].rearrange("(f p) d -> p f d", p=P)).then_inc(s, 16)

            def sp_main(self, sp):
                with sp.Fori(0, 3) as i:
                    for p in range(2):
                        hold(sp, self.s_low, 2 * (2 * i + p + 1))
                        self.load(sp, 2 * i + 2 + p, p)

            def pool_expert(self, g, e, p, j, free):
                hold(g, self.s_w1 if p else self.s_w0, 32 * (j + 1))
                if free:
                    hold(g, self.s_y_ps, RT * (e - 1))
                g.tensor_scalar(W1S[p][:, 0].rearrange("p c f -> p (c f)"), W1[p].rearrange("p c f -> p (c f)"), WS, None,
                                ALU.mult).then_inc(self.s_high, 1)
                g.tensor_scalar(W2S[p][:, 0].rearrange("p f d -> p (f d)"), W2[p].rearrange("p f d -> p (f d)"), WS, None,
                                ALU.mult).then_inc(self.s_high, 1)

            def pool_main(self, g):
                for p in range(2):
                    if p:
                        g.wait_ge(sem("c_ao") if self.L == 0 else sem("d_out"), 1 if self.L == 0 else RT)
                    self.pool_expert(g, p, p, 0, False)
                with g.Fori(0, 3) as i:
                    for p in range(2):
                        self.pool_expert(g, 2 * i + 2 + p, p, i + 1, True)

            def pe_main(self, pe):
                pe.wait_ge(self.s_xs, self.L + 1)
                with pe.Fori(0, NE // 2) as i:
                    for p in range(2):
                        e = 2 * i + p
                        hold(pe, self.s_low, 2 * e + 1)
                        for f in range(FC):
                            if f >= 4:
                                hold(pe, self.s_h_act, FC * e + f - 3)
                            for c in range(DC):
                                for n, (hw, hx) in enumerate(((0, 0), (0, 1), (1, 0))):
                                    ins = pe.matmul(PS[:, f % 4, :], W1S[p][:, hw, c, f * P:(f + 1) * P], XS[:, hx, c, :],
                                                    start=(c == 0 and n == 0), stop=(c == DC - 1 and n == 2))
                            ins.then_inc(self.s_h_ps, 1)
                        hold(pe, self.s_y_out, RT * e + RT)
                        hold(pe, self.s_low, 2 * e + 2)
                        for f in range(FC):
                            hold(pe, self.s_h_low, FC * e + f + 3)
                            for t in range(RT):
                                for n, (hh, hw) in enumerate(((0, 0), (0, 1), (1, 0))):
                                    ins = pe.matmul(PS[:, 4 + t, 0:D], HT[:, hh, f, t * P:(t + 1) * P],
                                                    W2S[p][:, hw, f, :], start=(f == 0 and n == 0),
                                                    stop=(f == FC - 1 and n == 2))
                                if f == FC - 1:
                                    ins.then_inc(self.s_y_ps, 1)

            def act_main(self, a):
                with a.Fori(0, NE // 2) as i:
                    for p in range(2):
                        e = 2 * i + p
                        if self.bias:
                            a.wait_ge(self.s_b1, e + 1)
                        for f in range(FC):
                            a.wait_ge(self.s_h_low, FC * e + f + 1)
                            a.wait_ge(self.s_h_ps, FC * e + f + 1)
                            bias = b1cur[:, p, f:f + 1] if self.bias else 0.0
                            a.activation(HF[:, f % 2, :], PS[:, f % 4, :], self.act, bias=bias, scale=1 / WS)
                            a.activation(HT[:, 0, f, :], PS[:, f % 4, :], self.act, bias=bias, scale=1 / WS)\
                                .then_inc(self.s_h_act, 1)

            def dve_rows(self, v):
                lk(v.tensor_copy(XS[:, 0, :, :], XT[:, :, :]))
                v.tensor_tensor(XS[:, 1, :, :], XT[:, :, :], XS[:, 0, :, :], ALU.subtract).then_inc(self.s_xs, 1)
                v.engine_nop().then_inc(self.s_h_low, 2)

            def dve_low(self, v, e, p, parts=(0, 1)):
                for n, (half, raw) in enumerate(((W1S[p].rearrange("p h c f -> p h (c f)"), W1[p].rearrange("p c f -> p (c f)")),
                                                 (W2S[p].rearrange("p h f d -> p h (f d)"), W2[p].rearrange("p f d -> p (f d)")))):
                    if n not in parts:
                        continue
                    v.wait_ge(self.s_high, 2 * e + n + 1)
                    v.scalar_tensor_tensor(half[:, 1], raw, WS, half[:, 0], ALU.mult, ALU.subtract).then_inc(self.s_low, 1)

            def dve_expert(self, v, e, p, last):
                if self.bias:
                    b1 = colv[:, COLS["b1"] + FC * e:COLS["b1"] + FC * e + FC] if last else \
                        colv[:, bass.ds(COLS["b1"] + FC * e, FC)]
                    v.tensor_copy(b1cur[:, p, :], b1).then_inc(self.s_b1, 1)
                w = GW[:, :, e] if last else GW[:, :, bass.ds(e, 1)].rearrange("p t o -> p (t o)")
                v.tensor_scalar(wcur[:, p, 0:RT], w, 1 / WS, None, ALU.mult).then_inc(sem("wcur"), 1)
                for f in range(FC):
                    v.wait_ge(self.s_h_act, FC * e + f + 1)
                    v.tensor_tensor(HT[:, 1, f, :], HF[:, f % 2, :], HT[:, 0, f, :], ALU.subtract)\
                        .then_inc(self.s_h_low, 1)
                if not last:
                    self.dve_low(v, e + 1, 1 - p)
                v.wait_ge(sem("wcur"), NE * self.L + e + 1)
                for t in range(RT):
                    v.wait_ge(self.s_y_ps, RT * e + t + 1)
                    v.scalar_tensor_tensor(ACC[:, t, :], PS[:, 4 + t, 0:D], wcur[:, p, t:t + 1], ACC[:, t, :],
                                           ALU.mult, ALU.add).then_inc(self.s_y_out, 1)

            def dve_main(self, v):
                v.engine_nop().then_inc(self.s_y_out, RT)
                with v.Fori(0, 3) as i:
                    for p in range(2):
                        self.dve_expert(v, 2 * i + p, p, False)
                self.dve_expert(v, 6, 0, False)
                self.dve_expert(v, 7, 1, True)
                v.wait_ge(self.s_y_out, RT * (NE + 1))
                lk(v.tensor_tensor(X[:, :, :], X[:, :, :], ACC[:, :, :], ALU.add))

        H_GROUPS = FC // 2
        H_BANKS = (2, 3, 0, 1)

        class Routed(Experts):
            def __init__(self, L, w1, w2, act):
                Experts.__init__(self, L, w1, w2, act, False)
                e = f"e{L}_"
                self.s_high2 = sem(e + "high2")
                self.s_oh = sem(e + "oh")
                self.s_ga, self.s_xe = sem(e + "ga"), sem(e + "xe")
                self.s_rk, self.s_sct = sem(e + "rk"), sem(e + "sct")
                self.s_y_high, self.s_y_low = sem(e + "y_high"), sem(e + "y_low")
                self.s_sc = sem(e + "sc")

            def pool_expert(self, g, e, p, j, free):
                hold(g, self.s_w1 if p else self.s_w0, 32 * (j + 1))
                if free:
                    hold(g, self.s_y_ps, e - 1)
                g.tensor_scalar(W1S[p][:, 0].rearrange("p c f -> p (c f)"), W1[p].rearrange("p c f -> p (c f)"), WS, None,
                                ALU.mult).then_inc(self.s_high, 1)

            def pe_gather(self, pe, e):
                pe.wait_ge(self.s_oh, e + 1)
                for c in range(DC):
                    for h in range(2):
                        for t in range(RT):
                            ins = pe.matmul(PS[:, c, h * CAP:(h + 1) * CAP], XNS[:, h, t, c * P:(c + 1) * P], OH[:, t, :],
                                            start=(t == 0), stop=(t == RT - 1))
                    ins.then_inc(self.s_ga, 1)
                if not isinstance(e, int) or e:
                    hold(pe, self.s_sct, e)
                lhs = pick[0:NE, e, :] if isinstance(e, int) else \
                    pick[0:NE, bass.ds(e, 1), :].rearrange("p o m -> p (o m)")
                pe.matmul(PS[:, 7, :], lhs, RKT[0:NE, :], start=True, stop=True).then_inc(self.s_rk, 1)

            def pe_expert(self, pe, e, p, last):
                hold(pe, self.s_low, 2 * e + 1)
                pe.wait_ge(self.s_xe, 2 * e + 2)
                for j in range(H_GROUPS):
                    for f in (2 * j, 2 * j + 1):
                        for c in range(DC):
                            for n, (hw, hx) in enumerate(((0, 0), (0, 1), (1, 0))):
                                ins = pe.matmul(PS[:, H_BANKS[j], (f % 2) * CAP:(f % 2 + 1) * CAP],
                                                W1S[p][:, hw, c, f * P:(f + 1) * P], XE[:, hx, c, :],
                                                start=(c == 0 and n == 0), stop=(c == DC - 1 and n == 2))
                    ins.then_inc(self.s_h_ps, 1)
                hold(pe, self.s_low, 2 * e + 2)
                for i, m in ((0, P), (1, CAP - P)):
                    for f in range(FC):
                        if i == 0 and f % 2 == 0:
                            pe.wait_ge(self.s_h_low, H_GROUPS * e + f // 2 + 1)
                        for n, (hh, hw) in enumerate(((0, 0), (0, 1), (1, 0))):
                            ins = pe.matmul(PS[0:m, 4, i * D:(i + 1) * D], HTE[:, hh, f, i * P:i * P + m],
                                            W2S[p][:, hw, f, :], start=(f == 0 and n == 0),
                                            stop=(f == FC - 1 and n == 2))
                ins.then_inc(self.s_y_ps, 1)
                if not last:
                    self.pe_gather(pe, e + 1)
                hold(pe, self.s_sct, e + 1)
                hold(pe, self.s_y_out, RT * e + RT)
                pe.wait_ge(self.s_y_low, e + 1)
                for t in range(RT):
                    for i, m in ((0, P), (1, CAP - P)):
                        for h in range(2):
                            ins = pe.matmul(pst((5, 6), t), SCT[0:m, i, t * P:(t + 1) * P], YS[0:m, h, i, :],
                                            start=(i == 0 and h == 0), stop=(i == 1 and h == 1))
                    if t % 2:
                        ins.then_inc(self.s_sc, 1)

            def pe_main(self, pe):
                pe.wait_ge(self.s_xs, 1)
                self.pe_gather(pe, 0)
                with pe.Fori(0, 3) as i:
                    for p in range(2):
                        self.pe_expert(pe, 2 * i + p, p, False)
                self.pe_expert(pe, 6, 0, False)
                self.pe_expert(pe, 7, 1, True)

            def act_high2(self, a, e, p, j):
                a.wait_ge(self.s_w1 if p else self.s_w0, 32 * (j + 1))
                a.activation(W2S[p][:, 0].rearrange("p f d -> p (f d)"), W2[p].rearrange("p f d -> p (f d)"), ACT.Copy,
                             scale=WS).then_inc(self.s_high2, 1)

            def act_rows(self, a, e):
                for c in range(DC):
                    a.wait_ge(self.s_ga, 2 * e + c + 1)
                    a.activation(XE[:, :, c, :], PS[:, c, 0:2 * CAP].rearrange("p (h s) -> p h s", h=2), ACT.Copy)\
                        .then_inc(self.s_xe, 1)

            def act_expert(self, a, e, p, j, last):
                for g in range(H_GROUPS):
                    a.wait_ge(self.s_h_ps, H_GROUPS * e + g + 1)
                    h = PS[:, H_BANKS[g], 0:2 * CAP]
                    a.activation(HFE[:, 2 * g:2 * g + 2, :].rearrange("p f s -> p (f s)"), h, self.act, scale=1 / WS)
                    a.activation(HTE[:, 0, 2 * g:2 * g + 2, :].rearrange("p f s -> p (f s)"), h, self.act, scale=1 / WS)\
                        .then_inc(self.s_h_act, 1)
                if not last:
                    self.act_high2(a, e + 1, 1 - p, j)
                a.wait_ge(self.s_y_ps, e + 1)
                a.activation(YS[:, 0, 0, :], PS[:, 4, 0:D], ACT.Copy)
                a.activation(YS[0:CAP - P, 0, 1, :], PS[0:CAP - P, 4, D:2 * D], ACT.Copy).then_inc(self.s_y_high, 1)
                if not last:
                    self.act_rows(a, e + 1)

            def act_main(self, a):
                self.act_rows(a, 0)
                with a.Fori(0, 3) as i:
                    for p in range(2):
                        self.act_expert(a, 2 * i + p, p, i + p, False)
                self.act_expert(a, 6, 0, 3, False)
                self.act_expert(a, 7, 1, 0, True)

            def dve_rows(self, v):
                lk(v.tensor_copy(XNS[:, 0], XN))
                v.tensor_tensor(XNS[:, 1], XN, XNS[:, 0], ALU.subtract).then_inc(self.s_xs, 1)

            def dve_one_hot(self, v, e):
                src = RK[:, :, e] if isinstance(e, int) else RK[:, :, bass.ds(e, 1)].rearrange("p t o -> p (t o)")
                v.tensor_copy(rkcur[:, 0:RT], src).then_inc(sem("rkcur"), 1)
                v.wait_ge(sem("rkcur"), e + 1)
                for t in range(RT):
                    ins = v.tensor_scalar(OH[:, t, :], slots[:, 0:CAP], rkcur[:, t:t + 1], None, ALU.is_equal)
                ins.then_inc(self.s_oh, 1)

            def dve_scatter(self, v, e):
                v.wait_ge(self.s_rk, e + 1)
                v.tensor_scalar(SCT[:, 0, :], PS[:, 7, :], slot[:, 0:1], None, ALU.is_equal)
                v.tensor_scalar(SCT[0:CAP - P, 1, :], PS[0:CAP - P, 7, :], slot[0:CAP - P, 1:2], None, ALU.is_equal)\
                    .then_inc(self.s_sct, 1)

            def dve_low(self, v, e, p):
                v.wait_ge(self.s_high, e + 1)
                v.scalar_tensor_tensor(W1S[p][:, 1].rearrange("p c f -> p (c f)"), W1[p].rearrange("p c f -> p (c f)"), WS,
                                       W1S[p][:, 0].rearrange("p c f -> p (c f)"), ALU.mult, ALU.subtract)\
                    .then_inc(self.s_low, 1)
                v.wait_ge(self.s_high2, e + 1)
                v.scalar_tensor_tensor(W2S[p][:, 1].rearrange("p f d -> p (f d)"), W2[p].rearrange("p f d -> p (f d)"), WS,
                                       W2S[p][:, 0].rearrange("p f d -> p (f d)"), ALU.mult, ALU.subtract)\
                    .then_inc(self.s_low, 1)

            def dve_expert(self, v, e, p, last):
                w = GW[:, :, e] if last else GW[:, :, bass.ds(e, 1)].rearrange("p t o -> p (t o)")
                v.tensor_scalar(wcur[:, p, 0:RT], w, 1 / WS, None, ALU.mult).then_inc(sem("wcur"), 1)
                for g in range(H_GROUPS):
                    v.wait_ge(self.s_h_act, H_GROUPS * e + g + 1)
                    v.tensor_tensor(HTE[:, 1, 2 * g:2 * g + 2, :], HFE[:, 2 * g:2 * g + 2, :], HTE[:, 0, 2 * g:2 * g + 2, :],
                                    ALU.subtract).then_inc(self.s_h_low, 1)
                if not last:
                    self.dve_one_hot(v, e + 1)
                    self.dve_low(v, e + 1, 1 - p)
                v.wait_ge(self.s_y_high, e + 1)
                v.tensor_tensor(YS[:, 1, 0, :], PS[:, 4, 0:D], YS[:, 0, 0, :], ALU.subtract)
                v.tensor_tensor(YS[0:CAP - P, 1, 1, :], PS[0:CAP - P, 4, D:2 * D], YS[0:CAP - P, 0, 1, :], ALU.subtract)\
                    .then_inc(self.s_y_low, 1)
                v.wait_ge(sem("wcur"), NE * self.L + e + 1)
                for t in range(RT):
                    hold(v, self.s_sc, 2 * e + t // 2 + 1)
                    v.scalar_tensor_tensor(ACC[:, t, :], pst((5, 6), t), wcur[:, p, t:t + 1], ACC[:, t, :],
                                           ALU.mult, ALU.add).then_inc(self.s_y_out, 1)
                if not last:
                    self.dve_scatter(v, e + 1)

            def dve_main(self, v):
                v.engine_nop().then_inc(self.s_y_out, RT)
                self.dve_one_hot(v, 0)
                self.dve_scatter(v, 0)
                with v.Fori(0, 3) as i:
                    for p in range(2):
                        self.dve_expert(v, 2 * i + p, p, False)
                self.dve_expert(v, 6, 0, False)
                self.dve_expert(v, 7, 1, True)
                v.wait_ge(self.s_y_out, RT * (NE + 1))
                lk(v.tensor_tensor(X[:, :, :], X[:, :, :], ACC[:, :, :], ALU.add))

        experts0 = Routed(0, m0w1, m0w2, ACT.Gelu)
        experts1 = Experts(1, m1w1, m1w2, ACT.Gelu_apprx_tanh, True)

        def across_pe(pe):
            tr_pe(pe, 3, HN, sem("ln_out"), 6)
            tr_done(pe, 3)
            pe.wait_ge(sem("w_moe"), 48)
            for b in range(B):
                for hh in range(2):
                    for c in range(DC):
                        ins = pe.matmul(PS[T * hh:T * hh + T, b // 2, (b % 2) * D:(b % 2 + 1) * D],
                                        XT[:, c, b * T:(b + 1) * T], WQKV[:, c, hh * D:(hh + 1) * D],
                                        start=(c == 0), stop=(c == DC - 1))
                if b % 2:
                    ins.then_inc(sem("c_qkv"), 1)
            pe.wait_ge(sem("c_ao"), 1)
            for half in range(2):
                for b in range(4 * half, 4 * half + 4):
                    ins = pe.transpose(PS[:, 4 + half, (b % 4) * P:(b % 4 + 1) * P], AO[:, b, :], ident[:, :])
                ins.then_inc(sem("c_turn"), 1)
            pe.wait_ge(sem("c_ot"), 2)
            rows_mm(pe, OT, WPJ, sem("c_proj"))
            tr_pe(pe, 4, XN, sem("ln_out"), 7)
            tr_done(pe, 4)
            gate_pe(pe, 0, 4, WRT)
            pe.wait_ge(sem("g0_sel"), 1)
            for t in range(RT):
                for s in range(t + 1):
                    ins = pe.matmul(PS[:, 1, t * NE:(t + 1) * NE], (before if s == t else ones)[:, :], SEL[:, s, :],
                                    start=(s == 0), stop=(s == t))
            pe.matmul(PS[:, 2, 0:P], ones[:, :], before[:, :], start=True, stop=True)
            pe.matmul(PS[:, 2, P:P + 1], before[:, :], ones[:, 0:1], start=True, stop=True).then_inc(sem("g0_rank"), 1)
            pe.wait_ge(sem("g_w"), 1)
            for t in range(RT):
                ins = pe.transpose(PS[0:NE, 3, t * P:(t + 1) * P], RK[:, t, :], ident[:, :])
            ins.then_inc(sem("g_turn"), 1)
            pe.wait_ge(sem("g0_rkt"), 1)
            experts0.pe_main(pe)

        def across_act(a):
            ln_act(a, 4)
            ln_act(a, 5)
            tr_act(a, 3, XT)
            for i in (1, 3):
                a.wait_ge(sem("c_qkv"), i + 1)
                a.activation(QKV[:, 2 * i:2 * i + 2, :].rearrange("p b n -> p (b n)"), PS[:, i, :], ACT.Copy)\
                    .then_inc(sem("c_in_a"), 1)
            a.wait_ge(sem("soft_sub"), 1)
            a.activation(SE[:, :, :, :, :].rearrange("p b r h k -> p (b r h k)"),
                         SE[:, :, :, :, :].rearrange("p b r h k -> p (b r h k)"), ACT.Exp, scale=HD ** -0.5)\
                .then_inc(sem("soft_exp"), 1)
            a.wait_ge(sem("c_turn"), 2)
            a.activation(OT[:, :, 4 * T:8 * T].rearrange("p h (b t) -> p b h t", b=4),
                         PS[:, 5, :].rearrange("p (b h t) -> p b h t", b=4, h=2), ACT.Copy).then_inc(sem("c_ot"), 1)
            ln_act(a, 6)
            tr_act(a, 4, XT)
            experts0.act_high2(a, 0, 0, 0)
            a.wait_ge(sem("soft_sub"), 2)
            a.activation(PROB[:, :, :], PROB[:, :, :], ACT.Exp).then_inc(sem("soft_exp"), 1)
            experts0.act_main(a)

        def across_dve(v):
            ln_dve(v, 4, X, XN)
            ln_dve(v, 5, XN, HN, "ln1w", "ln1b")
            tr_dve(v, 3, XT)
            lk(v.memset(SE[:, :, :, :, :].rearrange("p b r h k -> p (b r h k)"), NEG))
            for i in (0, 2):
                v.wait_ge(sem("c_qkv"), i + 1)
                ins = v.tensor_copy(QKV[:, 2 * i:2 * i + 2, :].rearrange("p b n -> p (b n)"), PS[:, i, :])
            lk(ins)
            v.wait_ge(sem("c_in_a"), 2)
            def products(b):
                return PRD[:, PAST[b] * P:(PAST[b] + b + 1) * P]

            for b in range(B):
                n = b + 1
                for r in range(2):
                    ins = v.tensor_tensor(products(b)[:, r * n * 64:(r + 1) * n * 64].rearrange("p (k h d) -> p k h d", k=n, h=4),
                                          bc(QKV[:, b, 0:P].rearrange("p (h r d) -> p h r d", h=4, r=2)[:, :, r, :]
                                             .unsqueeze(1), [P, n, 4, HD]),
                                          QKV[:, 0:n, P:P + 64].rearrange("p k (h d) -> p k h d", h=4), ALU.mult)
            lk(ins)
            for b in range(B):
                n = b + 1
                for r in range(2):
                    ins = v.tensor_reduce(SE[:, b, r, :, 0:n].rearrange("p h k -> p k h"),
                                          products(b)[:, r * n * 64:(r + 1) * n * 64]
                                          .rearrange("p (k h d) -> p k h d", k=n, h=4), AX.X, ALU.add)
            lk(ins)
            se = SE[:, :, :, :, :].rearrange("p b r h k -> p (b r h) k")
            lk(v.tensor_reduce(gm2[:, :], se, AX.X, ALU.max))
            v.tensor_tensor(se, se, bc(gm2[:, :].unsqueeze(2), [P, 64, B]), ALU.subtract).then_inc(sem("soft_sub"), 1)
            v.wait_ge(sem("soft_exp"), 1)
            lk(v.tensor_reduce(gs2[:, :], se, AX.X, ALU.add))
            lk(v.reciprocal(gs2[:, :], gs2[:, :]))
            lk(v.tensor_tensor(se, se, bc(gs2[:, :].unsqueeze(2), [P, 64, B]), ALU.mult))
            for b in range(B):
                n = b + 1
                for r in range(2):
                    ins = v.tensor_tensor(products(b).rearrange("p (h r d k) -> p h r d k", h=4, r=2, d=HD)[:, :, r],
                                          bc(SE[:, b, r, :, 0:n].unsqueeze(2), [P, 4, HD, n]),
                                          QKV[:, 0:n, P + 64:D].rearrange("p k (h d) -> p h d k", h=4), ALU.mult)
            lk(ins)
            for b in range(B):
                ins = v.tensor_reduce(AO[:, b, :], products(b).rearrange("p (x k) -> p x k", k=b + 1), AX.X, ALU.add)
            lk(ins)
            v.engine_nop().then_inc(sem("c_ao"), 1)
            v.wait_ge(sem("c_turn"), 1)
            v.tensor_copy(OT[:, :, 0:4 * T].rearrange("p h (b t) -> p b h t", b=4),
                          PS[:, 4, :].rearrange("p (b h t) -> p b h t", b=4, h=2)).then_inc(sem("c_ot"), 1)
            for t in range(RT):
                v.wait_ge(sem("c_proj"), (t // 2 + 1) * 2)
                ins = v.tensor_tensor(ACC[:, t, :], pst((0, 1), t), XN[:, t, :], ALU.add)
            lk(ins)
            ln_dve(v, 6, ACC, XN, "ln2w", "ln2b")
            tr_dve(v, 4, XT)
            experts0.dve_rows(v)
            experts0.dve_low(v, 0, 0)
            v.wait_ge(sem("g_logit"), 1)
            lg = PS[:, 0, 0:RT * NE].rearrange("p (t e) -> p t e", t=RT)
            lk(v.tensor_reduce(gmx[:, :], lg, AX.X, ALU.max))
            v.tensor_tensor(PROB[:, :, :], lg, bc(gmx[:, :].unsqueeze(2), [P, RT, NE]), ALU.subtract)\
                .then_inc(sem("soft_sub"), 1)
            v.wait_ge(sem("soft_exp"), 2)
            lk(v.tensor_reduce(gsm[:, :], PROB[:, :, :], AX.X, ALU.add))
            lk(v.reciprocal(gsm[:, :], gsm[:, :]))
            lk(v.tensor_tensor(PROB[:, :, :], PROB[:, :, :], bc(gsm[:, :].unsqueeze(2), [P, RT, NE]), ALU.mult))
            top2(v)
            v.engine_nop().then_inc(sem("g0_sel"), 1)
            lk(v.tensor_tensor(GW[:, :, :], PROB[:, :, :], SEL[:, :, :], ALU.mult))
            lk(v.tensor_reduce(gsm[:, :], GW[:, :, :], AX.X, ALU.add))
            lk(v.reciprocal(gsm[:, :], gsm[:, :]))
            lk(v.tensor_tensor(GW[:, :, :], GW[:, :, :], bc(gsm[:, :].unsqueeze(2), [P, RT, NE]), ALU.mult))
            v.wait_ge(sem("g0_rank"), 1)
            lk(v.tensor_scalar(GX[:, :, :], PS[:, 1, 0:RT * NE].rearrange("p (t e) -> p t e", t=RT), CAP - 0.5, None,
                               ALU.is_lt))
            lk(v.tensor_tensor(GW[:, :, :], GW[:, :, :], GX[:, :, :], ALU.mult))
            lk(v.tensor_scalar(RK[:, :, :], SEL[:, :, :], -1000.0, 1000.0, ALU.mult, ALU.add))
            lk(v.tensor_tensor(RK[:, :, :], RK[:, :, :], PS[:, 1, 0:RT * NE].rearrange("p (t e) -> p t e", t=RT), ALU.add))
            v.engine_nop().then_inc(sem("g_w"), 1)
            v.tensor_copy(slots[:, 0:P], PS[:, 2, 0:P])
            v.tensor_scalar(slots[:, P:CAP], PS[:, 2, 0:CAP - P], float(P), None, ALU.add)
            v.tensor_copy(slot[:, 0:1], PS[:, 2, P:P + 1])
            lk(v.tensor_scalar(slot[:, 1:2], PS[:, 2, P:P + 1], float(P), None, ALU.add))
            v.wait_ge(sem("g_turn"), 1)
            v.tensor_copy(RKT[0:NE, :], PS[0:NE, 3, :]).then_inc(sem("g0_rkt"), 1)
            experts0.dve_main(v)

        WA = PK

        def single_pe(pe):
            tr_pe(pe, 6, XN, sem("ln_out"), 9)
            tr_done(pe, 6)
            pe.wait_ge(sem("w_a"), 64)
            cols_mm(pe, XT, WA[:, 0], sem("d_q"), banks=(0, 1))
            cols_mm(pe, XT, WA[:, 1], sem("d_q"), banks=(2, 3))
            rows_mm(pe, XT, WA[:, 2], sem("d_q"), banks=(4, 5))
            pe.wait_ge(sem("d_in"), 4)
            for t in range(RT):
                for c in range(DC):
                    ins = pe.matmul(PS[:, 0, t * P:(t + 1) * P], QT[:, c, t * P:(t + 1) * P],
                                    KT5[:, c, t * P:(t + 1) * P], start=(c == 0), stop=(c == DC - 1))
            ins.then_inc(sem("d_score"), 1)
            pe.wait_ge(sem("d_norm"), 1)
            for t in range(RT):
                ins = pe.transpose(PS[:, 1, t * P:(t + 1) * P], S5[:, t, :], ident[:, :])
            ins.then_inc(sem("d_turn"), 1)
            pe.wait_ge(sem("d_p"), 1)
            pe.wait_ge(sem("d_v"), 2)
            for m in range(DC):
                for t in range(RT):
                    ins = pe.matmul(PS[:, 2 + m, t * P:(t + 1) * P], V5[:, t, m * P:(m + 1) * P], S5T[:, t, :],
                                    start=True, stop=True)
                ins.then_inc(sem("d_pv"), 1)
            pe.wait_ge(sem("d_o"), 2)
            rows_mm(pe, OT, WA[:, 3], sem("d_out"), banks=(4, 5))

        def single_dve(v):
            ln_dve(v, 8, X, XN)
            tr_dve(v, 6, XT)
            for m in range(DC):
                v.wait_ge(sem("d_q"), m + 1)
                v.tensor_scalar(QT[:, m, :], PS[:, m, :], col("bq5", m), D ** -0.5, ALU.add, ALU.mult)\
                    .then_inc(sem("d_in"), 1)
            for m in range(DC):
                v.wait_ge(sem("d_q"), 3 + m)
                v.tensor_scalar(KT5[:, m, :], PS[:, 2 + m, :], col("bk5", m), None, ALU.add).then_inc(sem("d_in"), 1)
            experts1.dve_low(v, 0, 0, (0,))
            v.wait_ge(sem("d_score"), 1)
            lk(v.tensor_tensor(S5[:, :, :], PS[:, 0, :].rearrange("p (t k) -> p t k", t=RT),
                               bc(causal2[:, :].unsqueeze(1), [P, RT, P]), ALU.add))
            lk(v.tensor_reduce(m5[:, :], S5[:, :, :], AX.X, ALU.max))
            v.tensor_tensor(S5[:, :, :], S5[:, :, :], bc(m5[:, :].unsqueeze(2), [P, RT, P]), ALU.subtract)\
                .then_inc(sem("soft_sub"), 1)
            v.wait_ge(sem("soft_exp"), 3)
            lk(v.tensor_reduce(s5[:, :], S5[:, :, :], AX.X, ALU.add))
            lk(v.reciprocal(s5[:, :], s5[:, :]))
            v.tensor_tensor(S5[:, :, :], S5[:, :, :], bc(s5[:, :].unsqueeze(2), [P, RT, P]), ALU.mult)\
                .then_inc(sem("d_norm"), 1)
            v.wait_ge(sem("d_turn"), 1)
            v.tensor_copy(S5T[:, :, :].rearrange("p t q -> p (t q)"), PS[:, 1, :]).then_inc(sem("d_p"), 1)
            for m in range(DC):
                v.wait_ge(sem("d_pv"), m + 1)
                v.tensor_scalar(OT[:, m, :], PS[:, 2 + m, :], col("bv5", m), None, ALU.add).then_inc(sem("d_o"), 1)
            lk(v.tensor_tensor(X[:, :, :], X[:, :, :], bc(row("bo5").unsqueeze(1), [P, RT, D]), ALU.add))
            for t in range(RT):
                v.wait_ge(sem("d_out"), (t // 2 + 1) * 2)
                ins = v.tensor_tensor(X[:, t, :], X[:, t, :], pst((4, 5), t), ALU.add)
            lk(ins)

        def single_act(a):
            ln_act(a, 8)
            tr_act(a, 6, XT)
            for i in range(2):
                a.wait_ge(sem("d_q"), 4 + 2 * (i + 1))
                a.activation(V5[:, 2 * i:2 * i + 2, :].rearrange("p t d -> p (t d)"), PS[:, 4 + i, :], ACT.Copy)\
                    .then_inc(sem("d_v"), 1)
            a.wait_ge(sem("soft_sub"), 3)
            a.activation(S5[:, :, :], S5[:, :, :], ACT.Exp).then_inc(sem("soft_exp"), 1)

        def moe_pe(pe):
            tr_pe(pe, 7, XN, sem("ln_out"), 10)
            tr_done(pe, 7)
            pe.wait_ge(sem("w_gate1"), 32)
            gate_pe(pe, 1, 7, WGT)
            pe.wait_ge(sem("g_w"), 2)
            for t in range(RT):
                ins = pe.transpose(PS[0:NE, 1, t * P:(t + 1) * P], GW[:, t, :], ident[:, :])
            ins.then_inc(sem("g_turn"), 1)
            pe.wait_ge(sem("g1_wT"), 1)
            for t in range(RT):
                ins = pe.matmul(pst((6, 7), t), wT[0:NE, t * P:(t + 1) * P], B2[0:NE, :], start=True, stop=True)
            ins.then_inc(sem("g1_b2"), 1)
            experts1.pe_main(pe)

        def moe_dve(v):
            ln_dve(v, 9, X, XN)
            tr_dve(v, 7, XT)
            tr_done(v, 7)
            experts1.dve_rows(v)
            experts1.dve_low(v, 0, 0, (1,))
            v.wait_ge(sem("soft_exp"), 4)
            lk(v.tensor_scalar(PROB[:, :, :], PROB[:, :, :], 1.0, None, ALU.add))
            lk(v.reciprocal(PROB[:, :, :], PROB[:, :, :]))
            top2(v)
            lk(v.tensor_tensor(GW[:, :, :], PROB[:, :, :], SEL[:, :, :], ALU.mult))
            v.engine_nop().then_inc(sem("g_w"), 1)
            v.wait_ge(sem("g_turn"), 2)
            v.tensor_copy(wT[0:NE, :], PS[0:NE, 1, :]).then_inc(sem("g1_wT"), 1)
            v.wait_ge(sem("g1_b2"), 1)
            for i in range(2):
                ins = v.tensor_copy(ACC[:, 2 * i:2 * i + 2, :].rearrange("p t d -> p (t d)"), PS[:, 6 + i, :])
            lk(ins)
            experts1.dve_main(v)

        def moe_act(a):
            ln_act(a, 9)
            tr_act(a, 7, XT)
            a.wait_ge(sem("g_logit"), 2)
            a.activation(PROB[:, :, :], PS[:, 0, 0:RT * NE].rearrange("p (t e) -> p t e", t=RT), ACT.Exp, scale=-1.0)\
                .then_inc(sem("soft_exp"), 1)
            experts1.act_main(a)

        block = ctx.enter_context(nc.Block())

        def w_load(eng, dst, src, s):
            eng.dma_start(dst, src.rearrange("(c p) n -> p c n", p=P)).then_inc(s, 16)

        @block.sync
        def _(sp):
            sp.dma_start(X[:, :, :], x.rearrange("(t p) d -> p t d", p=P)).then_inc(sem("x_in"), 16)
            for i in range(4):
                w_load(sp, W4[:, i], xw0[i], sem("w_x0"))
            sp.dma_start(colv[:, :], cols).then_inc(sem("cols_in"), 16)
            cross0.sp_first(sp)
            sp.dma_start(rows_b[:, :, :], bc(rowv.unsqueeze(0), [P, len(ROWV), D])).then_inc(sem("rows_in"), 16)
            cross0.sp_main(sp)
            sp.wait_ge(cross0.split, B)
            sp.wait_ge(cross0.unit_ps, UNITS * 7)
            for i in range(4):
                w_load(sp, PK[:, i], patt_k[i], sem("w_patt"))
                w_load(sp, PV[:, i], patt_v[i], sem("w_patt"))
            sp.wait_ge(cross0.o_ps, RT)
            w_load(sp, FKs, fk, sem("w_ff"))
            w_load(sp, FVs, fv, sem("w_ff"))
            w_load(sp, WQKV, wqkv, sem("w_moe"))
            w_load(sp, WPJ, wproj, sem("w_moe"))
            w_load(sp, WRT, wrt, sem("w_moe"))
            experts0.load(sp, 0, 0)
            for i in range(4):
                w_load(sp, W4[:, i], xw1[i], sem("w_x1"))
            sp.wait_ge(sem("p_out"), 10)
            experts0.load(sp, 1, 1)
            experts0.sp_main(sp)
            sp.wait_ge(experts0.s_y_ps, NE)
            cross1.sp_first(sp)
            cross1.sp_main(sp)
            sp.wait_ge(cross1.split, B)
            sp.wait_ge(cross1.unit_ps, UNITS * 7)
            for i in range(4):
                w_load(sp, WA[:, i], aw[i], sem("w_a"))
            sp.wait_ge(cross1.o_ps, 2 * RT)
            w_load(sp, WGT, wg, sem("w_gate1"))
            sp.dma_start(B2[0:NE, :], b2).then_inc(sem("w_gate1"), 16)
            for e in range(2):
                experts1.load(sp, e, e)
            experts1.sp_main(sp)
            sp.wait_ge(sem("x_final"), 1)
            sp.dma_start(out.rearrange("(t p) d -> p t d", p=P), X[:, :, :]).then_inc(sem("stored"), 16)
            sp.wait_ge(sem("stored"), 16)

        @block.gpsimd
        def _(g):
            plk(g.memset(ident[:, :], 0.0))
            plk(g.memset(ones[:, :], 1.0))
            plk(g.memset(pick[:, :, :], 0.0))
            plk(g.affine_select(out=pick[:, :, :], in_=pick[:, :, :], compare_op=ALU.not_equal, fill=1.0, base=0,
                                pattern=[[-1, NE], [0, P]], channel_multiplier=1))
            plk(g.memset(before[:, :], 1.0))
            plk(g.memset(headmask[:, :], 1.0))
            plk(g.memset(causal[:, :], 0.0))
            plk(g.memset(causal2[:, :], 0.0))
            plk(g.memset(lower8[:, :, :], 1.0))
            plk(g.affine_select(out=ident[:, :], in_=ident[:, :], compare_op=ALU.not_equal, fill=1.0, base=0,
                            pattern=[[-1, P]], channel_multiplier=1))
            plk(g.affine_select(out=before[:, :], in_=before[:, :], compare_op=ALU.is_gt, fill=0.0, base=0,
                            pattern=[[1, P]], channel_multiplier=-1))
            plk(g.affine_select(out=headmask[:, :], in_=headmask[:, :], compare_op=ALU.is_ge, fill=0.0, base=0,
                                pattern=[[-HD, HPC]], channel_multiplier=1))
            plk(g.affine_select(out=headmask[:, :], in_=headmask[:, :], compare_op=ALU.is_ge, fill=0.0, base=HD - 1,
                            pattern=[[HD, HPC]], channel_multiplier=-1))
            for i in range(2):
                plk(g.affine_select(out=causal[T * i:T * i + T, :], in_=causal[T * i:T * i + T, :], compare_op=ALU.is_ge,
                                fill=NEG, base=0, pattern=[[-1, T]], channel_multiplier=1))
            plk(g.affine_select(out=lower8[:, :, :], in_=lower8[:, :, :], compare_op=ALU.is_gt, fill=0.0, base=0,
                            pattern=[[1, NE], [-1, NE]], channel_multiplier=0))
            plk(g.affine_select(out=causal2[:, :], in_=causal2[:, :], compare_op=ALU.is_ge, fill=NEG, base=0,
                                pattern=[[-1, P]], channel_multiplier=1))
            plk(g.memset(causal2[T:P, 0:T], NEG))
            g.engine_nop().then_inc(sem("consts"), 1)
            cross0.pool_main(g)
            latent_pool(g)
            g.wait_ge(sem("p_out"), 10)
            experts0.pool_main(g)
            cross1.pool_main(g)
            experts1.pool_main(g)

        @block.tensor
        def _(pe):
            pe.wait_ge(sem("consts"), 1)
            cross0.pe_main(pe)
            latent_pe(pe)
            across_pe(pe)
            cross1.pe_main(pe)
            single_pe(pe)
            moe_pe(pe)

        @block.vector
        def _(v):
            lk(v.memset(eps_c[:, :], EPS))
            v.wait_ge(sem("x_in"), 16)
            cross0.dve_main(v)
            latent_dve(v)
            across_dve(v)
            cross1.dve_main(v)
            single_dve(v)
            moe_dve(v)
            v.engine_nop().then_inc(sem("x_final"), 1)

        @block.scalar
        def _(a):
            cross0.act_main(a)
            latent_act(a)
            across_act(a)
            cross1.act_main(a)
            single_act(a)
            moe_act(a)


NAMES = ["x", "ctxT", "mask", "cols", "rowv", "xw0", "patt_k", "patt_v", "fk", "fv", "wqkv", "wproj", "wrt", "m0w1",
         "m0w2", "xw1", "aw", "wg", "m1w1", "m1w2", "b2"]


def layout(inputs):
    import numpy as np
    """What kernel() gives the program: every input in its own type, only laid out."""
    np_ = {k: np.asarray(v) for k, v in inputs.items()}
    t = lambda n: np_[n].T
    colm = lambda v: v.reshape(-1, 128).T
    cols = np.concatenate([colm(np_[n]) for n in ("L0_xattn_bq", "L0_xattn_bk", "L0_xattn_bv", "L1_attn_bq", "L1_attn_bk", "L1_attn_bv", "L1_ffn_b1")], axis=1)
    rowv = np.stack([np_[n] for n in ("L0_xattn_bo", "L0_ffn_ln1_weight", "L0_ffn_ln1_bias", "L0_ffn_ln2_weight", "L0_ffn_ln2_bias", "L1_xattn_bo", "L1_attn_bo")])
    w = np_["L0_ffn_qkv_weight"].reshape(2, 4, 64, 256)
    wqkv = np.concatenate([w[:, :, 0:32].reshape(2, 128, 256), w[:, :, 32:48].reshape(2, 64, 256), w[:, :, 48:64].reshape(2, 64, 256)], axis=1).reshape(512, 256).T
    return [np.ascontiguousarray(a) for a in (
        np_["x"].reshape(512, 256), np_["ctx_1024"].transpose(0, 2, 1), np_["mask_Bx1x1xS2_ff0"].reshape(8, 1601), cols, rowv,
        np.stack([np_["L0_xattn_" + n] for n in ("wq", "wk", "wv", "wo")]),
        np.stack([t("L0_attn_" + n) for n in ("qK", "kK", "vK", "pK")]), np.stack([np_["L0_attn_" + n] for n in ("qV", "kV", "vV", "pV")]),
        t("L0_attn_fK"), np_["L0_attn_fV"], wqkv, t("L0_ffn_proj_weight"), np_["L0_ffn_router_weight"],
        np_["L0_ffn_moe_w1"], np_["L0_ffn_moe_w2"],
        np.stack([t("L1_xattn_" + n) for n in ("Wq", "Wk", "Wv", "Wo")]),
        np.stack([np_["L1_attn_" + n] for n in ("Wq", "Wk", "Wv", "Wo")]),
        np_["L1_ffn_Wg"], np_["L1_ffn_W1"], np_["L1_ffn_W2"], np_["L1_ffn_b2"])]


def kernel(**inputs):
    import numpy as np
    import concourse.bacc as bacc
    from concourse.bass_utils import run_bass_kernel_spmd

    nc = bacc.Bacc("TRN2", target_bir_lowering=False, num_devices=1)
    arrays, args = {}, []
    for name, a in zip(NAMES, layout(inputs)):
        arrays[f"in_{name}"] = a
        args.append(nc.dram_tensor(f"in_{name}", a.shape, mybir.dt.from_np(a.dtype), kind="ExternalInput").ap())
    args.append(nc.dram_tensor("out", (ROWS, D), F32, kind="ExternalOutput").ap())
    perceiver(nc, *args)
    r = run_bass_kernel_spmd(nc, [arrays], core_ids=[0])
    return r.results[0]["out"].reshape(B, T, D)
```
